# Optimizing a Trainium2 kernel written in Bass

```python
import numpy as np
import jax
import jax.numpy as jnp

def _softmax(x, axis=-1):
    return jax.nn.softmax(x, axis=axis)

def _gelu(x):
    return jax.nn.gelu(x, approximate=True)

def _silu(x):
    return jax.nn.silu(x)

def _sigmoid(x):
    return jax.nn.sigmoid(x)

def _layernorm(x, axis=-1, eps=1e-05):
    m = jnp.mean(x, axis=axis, keepdims=True)
    v = jnp.var(x, axis=axis, keepdims=True)
    return (x - m) / jnp.sqrt(v + eps)

def _scatter_add(tgt, idx, src, axis=0):
    return tgt.at[idx].add(src)

def _segment_sum(src, seg, n):
    return jax.ops.segment_sum(src, seg, n)
kernel_name = 'mk_gnn_preln_d4_gnn_r8_39b5a3'

def setup_inputs(seed: int=0):
    np.random.seed(seed)
    _w = jnp.asarray

    def _rec_inputs():
        import jax
        import jax.numpy as jnp
        _gk = jax.random.key(seed)
        x = -0.000202 + 1 * jax.random.normal(jax.random.fold_in(_gk, 1), (6250, 128), jnp.float32)
        _s = jax.random.randint(jax.random.fold_in(_gk, 2), (50000,), 0, 6250, jnp.int32)
        _d = jax.random.randint(jax.random.fold_in(_gk, 3), (50000,), 0, 6250, jnp.int32)
        _loop = jnp.arange(6250, dtype=jnp.int32)
        src = jnp.concatenate([_s, _d, _loop])
        dst = jnp.concatenate([_d, _s, _loop])
        _o = jnp.argsort(dst, stable=True)
        src = src[_o]
        dst = dst[_o]
        edge_attr_128 = 2.93046e-05 + 1.00006 * jax.random.normal(jax.random.fold_in(_gk, 12), (106250, 128), jnp.float32)
        edge_attr_128_n2 = 2.93046e-05 + 1.00006 * jax.random.normal(jax.random.fold_in(_gk, 13), (106250, 128), jnp.float32)
        edge_weight = jax.random.uniform(jax.random.fold_in(_gk, 15), (106250,), jnp.float32, 0.0, 0.999998)
        return (x, src, dst, edge_attr_128, edge_attr_128_n2, edge_weight)
    x, src, dst, edge_attr_128, edge_attr_128_n2, edge_weight = _rec_inputs()

    def _L0_gnn_setup():
        import jax, jax.numpy as jnp
        import numpy as np
        NEG_SLOPE = 0.2

        def _gatv2_layer(x, src, dst, Wl, bl, Wr, br, att, bias, heads, out_ch, concat):
            N = x.shape[0]
            xl = (x @ Wl + bl).reshape(N, heads, out_ch)
            xr = (x @ Wr + br).reshape(N, heads, out_ch)
            e = jax.nn.leaky_relu(xl[src] + xr[dst], NEG_SLOPE)
            logits = jnp.einsum('ehc,hc->eh', e, att)
            m = jax.ops.segment_max(logits, dst, num_segments=N)
            ex = jnp.exp(logits - m[dst])
            denom = jax.ops.segment_sum(ex, dst, num_segments=N)
            alpha = ex / denom[dst]
            msg = xl[src] * alpha[..., None]
            out = jax.ops.segment_sum(msg, dst, num_segments=N)
            if concat:
                out = out.reshape(N, heads * out_ch)
            else:
                out = out.mean(axis=1)
            return out + bias
        key = jax.random.key(seed)
        ks = jax.random.split(key, 16)
        N, F, E = (6250, 128, 100000)
        H1, C1 = (8, 16)
        C2 = 64
        OUT = 128
        s = lambda f: 1.0 / np.sqrt(f)
        inp = {'x': jax.random.normal(ks[0], (N, F), dtype=jnp.float32), 'edge_index': jax.random.randint(ks[1], (2, E), 0, N, dtype=jnp.int64), 'Wl1': jax.random.normal(ks[2], (F, H1 * C1), dtype=jnp.float32) * s(F), 'bl1': jnp.zeros((H1 * C1,), dtype=jnp.float32), 'Wr1': jax.random.normal(ks[3], (F, H1 * C1), dtype=jnp.float32) * s(F), 'br1': jnp.zeros((H1 * C1,), dtype=jnp.float32), 'att1': jax.random.normal(ks[4], (H1, C1), dtype=jnp.float32) * s(C1), 'bias1': jnp.zeros((H1 * C1,), dtype=jnp.float32), 'Wl2': jax.random.normal(ks[5], (H1 * C1, C2), dtype=jnp.float32) * s(H1 * C1), 'bl2': jnp.zeros((C2,), dtype=jnp.float32), 'Wr2': jax.random.normal(ks[6], (H1 * C1, C2), dtype=jnp.float32) * s(H1 * C1), 'br2': jnp.zeros((C2,), dtype=jnp.float32), 'att2': jax.random.normal(ks[7], (1, C2), dtype=jnp.float32) * s(C2), 'bias2': jnp.zeros((C2,), dtype=jnp.float32), 'Wlin': jax.random.normal(ks[8], (C2, OUT), dtype=jnp.float32) * s(C2), 'blin': jnp.zeros((OUT,), dtype=jnp.float32)}
        return inp
    _L0_gnn_all = _L0_gnn_setup()
    _L0_gnn_in = {k: v for k, v in _L0_gnn_all.items() if k in ('Wl1', 'bl1', 'Wr1', 'br1', 'att1', 'bias1', 'Wl2', 'bl2', 'Wr2', 'br2', 'att2', 'bias2', 'Wlin', 'blin')}
    del _L0_gnn_all

    def _L1_gnn_setup():
        import jax, jax.numpy as jnp
        import numpy as np
        N_NODES = 12500
        N_EDGES = 50000
        IN_DIM = 128
        OUT_DIM = 128
        LN_EPS = 1e-05
        key = jax.random.key(seed)
        ks = jax.random.split(key, 5)
        x = jax.random.normal(ks[0], (N_NODES, IN_DIM), dtype=jnp.float32)
        edge_index = jax.random.randint(ks[1], (2, N_EDGES), 0, N_NODES, dtype=jnp.int64)
        edge_weight = jax.random.uniform(ks[2], (N_EDGES,), dtype=jnp.float32)
        W = jax.random.normal(ks[3], (IN_DIM, OUT_DIM), dtype=jnp.float32) * (1.0 / np.sqrt(IN_DIM))
        b = jnp.zeros((OUT_DIM,), dtype=jnp.float32)
        ln_gamma = jnp.ones((OUT_DIM,), dtype=jnp.float32)
        ln_beta = jnp.zeros((OUT_DIM,), dtype=jnp.float32)
        return {'x': x, 'edge_index': edge_index, 'edge_weight': edge_weight, 'W': W, 'b': b, 'ln_gamma': ln_gamma, 'ln_beta': ln_beta}
    _L1_gnn_all = _L1_gnn_setup()
    _L1_gnn_in = {k: v for k, v in _L1_gnn_all.items() if k in ('W', 'b', 'ln_gamma', 'ln_beta')}
    del _L1_gnn_all

    def _L2_gnn_setup():
        import jax, jax.numpy as jnp
        import numpy as np
        N, E, H = (5000, 80000, 128)
        EPS = 1e-05

        def _bn(x, gamma, beta):
            mu = jnp.mean(x, axis=0)
            var = jnp.mean((x - mu) ** 2, axis=0)
            return (x - mu) * jax.lax.rsqrt(var + EPS) * gamma + beta
        key = jax.random.key(seed)
        ks = jax.random.split(key, 12)
        s = 1.0 / np.sqrt(H)
        return {'x_feat': jax.random.normal(ks[0], (N, H), jnp.float32), 'edge_attr': jax.random.normal(ks[1], (E, H), jnp.float32), 'bases': jax.random.normal(ks[2], (E, H), jnp.float32), 'src': jax.random.randint(ks[3], (E,), 0, N, jnp.int32), 'dst': jax.random.randint(ks[4], (E,), 0, N, jnp.int32), 'W1': jax.random.uniform(ks[5], (H, H), jnp.float32, -s, s), 'b1': jnp.zeros((H,), jnp.float32), 'W2': jax.random.uniform(ks[6], (H, H), jnp.float32, -s, s), 'b2': jnp.zeros((H,), jnp.float32), 'g1': jnp.ones((H,), jnp.float32), 'be1': jnp.zeros((H,), jnp.float32), 'W3': jax.random.uniform(ks[7], (H, H), jnp.float32, -s, s), 'b3': jnp.zeros((H,), jnp.float32), 'g2': jnp.ones((H,), jnp.float32), 'be2': jnpp_zeros if False else jnp.zeros((H,), jnp.float32)}
    _L2_gnn_all = _L2_gnn_setup()
    _L2_gnn_in = {k: v for k, v in _L2_gnn_all.items() if k in ('W1', 'b1', 'W2', 'b2', 'g1', 'be1', 'W3', 'b3', 'g2', 'be2')}
    del _L2_gnn_all

    def _L3_gnn_setup():
        import jax, jax.numpy as jnp
        import numpy as np
        from jax import lax
        N, E, D = (12500, 100000, 128)

        def _gcn_conv(x, W, b, src, dst, ew, n):
            xw = x @ W
            deg = jax.ops.segment_sum(ew, dst, num_segments=n)
            dinv = lax.rsqrt(deg)
            norm = dinv[src] * ew * dinv[dst]
            msg = xw[src] * norm[:, None]
            out = jax.ops.segment_sum(msg, dst, num_segments=n)
            return out + b
        key = jax.random.key(seed)
        ks = jax.random.split(key, 9)
        s = 1.0 / np.sqrt(D)
        return {'x': jax.random.normal(ks[0], (N, D), jnp.float32), 'edge_index': jax.random.randint(ks[1], (2, E), 0, N, jnp.int64), 'edge_weight': jax.random.uniform(ks[2], (E,), jnp.float32), 'W_init': jax.random.normal(ks[3], (D, D), jnp.float32) * s, 'W1': jax.random.normal(ks[4], (D, D), jnp.float32) * s, 'b1': jnp.zeros((D,), jnp.float32), 'W2': jax.random.normal(ks[5], (D, D), jnp.float32) * s, 'b2': jnp.zeros((D,), jnp.float32), 'W3': jax.random.normal(ks[6], (D, D), jnp.float32) * s, 'b3': jnp.zeros((D,), jnp.float32)}
    _L3_gnn_all = _L3_gnn_setup()
    _L3_gnn_in = {k: v for k, v in _L3_gnn_all.items() if k in ('W_init', 'W1', 'b1', 'W2', 'b2', 'W3', 'b3')}
    del _L3_gnn_all
    return {'x': x, 'src': src, 'dst': dst, 'edge_attr_128': edge_attr_128, 'edge_attr_128_n2': edge_attr_128_n2, 'edge_weight': edge_weight, 'L0_gnn_Wl1': _L0_gnn_in['Wl1'], 'L0_gnn_bl1': _L0_gnn_in['bl1'], 'L0_gnn_Wr1': _L0_gnn_in['Wr1'], 'L0_gnn_br1': _L0_gnn_in['br1'], 'L0_gnn_att1': _L0_gnn_in['att1'], 'L0_gnn_bias1': _L0_gnn_in['bias1'], 'L0_gnn_Wl2': _L0_gnn_in['Wl2'], 'L0_gnn_bl2': _L0_gnn_in['bl2'], 'L0_gnn_Wr2': _L0_gnn_in['Wr2'], 'L0_gnn_br2': _L0_gnn_in['br2'], 'L0_gnn_att2': _L0_gnn_in['att2'], 'L0_gnn_bias2': _L0_gnn_in['bias2'], 'L0_gnn_Wlin': _L0_gnn_in['Wlin'], 'L0_gnn_blin': _L0_gnn_in['blin'], 'L1_gnn_W': _L1_gnn_in['W'], 'L1_gnn_b': _L1_gnn_in['b'], 'L1_gnn_ln_gamma': _L1_gnn_in['ln_gamma'], 'L1_gnn_ln_beta': _L1_gnn_in['ln_beta'], 'L2_gnn_W1': _L2_gnn_in['W1'], 'L2_gnn_b1': _L2_gnn_in['b1'], 'L2_gnn_W2': _L2_gnn_in['W2'], 'L2_gnn_b2': _L2_gnn_in['b2'], 'L2_gnn_g1': _L2_gnn_in['g1'], 'L2_gnn_be1': _L2_gnn_in['be1'], 'L2_gnn_W3': _L2_gnn_in['W3'], 'L2_gnn_b3': _L2_gnn_in['b3'], 'L2_gnn_g2': _L2_gnn_in['g2'], 'L2_gnn_be2': _L2_gnn_in['be2'], 'L3_gnn_W_init': _L3_gnn_in['W_init'], 'L3_gnn_W1': _L3_gnn_in['W1'], 'L3_gnn_b1': _L3_gnn_in['b1'], 'L3_gnn_W2': _L3_gnn_in['W2'], 'L3_gnn_b2': _L3_gnn_in['b2'], 'L3_gnn_W3': _L3_gnn_in['W3'], 'L3_gnn_b3': _L3_gnn_in['b3']}

def reference(x, src, dst, edge_attr_128, edge_attr_128_n2, edge_weight, L0_gnn_Wl1, L0_gnn_bl1, L0_gnn_Wr1, L0_gnn_br1, L0_gnn_att1, L0_gnn_bias1, L0_gnn_Wl2, L0_gnn_bl2, L0_gnn_Wr2, L0_gnn_br2, L0_gnn_att2, L0_gnn_bias2, L0_gnn_Wlin, L0_gnn_blin, L1_gnn_W, L1_gnn_b, L1_gnn_ln_gamma, L1_gnn_ln_beta, L2_gnn_W1, L2_gnn_b1, L2_gnn_W2, L2_gnn_b2, L2_gnn_g1, L2_gnn_be1, L2_gnn_W3, L2_gnn_b3, L2_gnn_g2, L2_gnn_be2, L3_gnn_W_init, L3_gnn_W1, L3_gnn_b1, L3_gnn_W2, L3_gnn_b2, L3_gnn_W3, L3_gnn_b3):
    import jax
    import jax.numpy as jnp

    def _L0_gnn_ref(x, edge_index, Wl1, bl1, Wr1, br1, att1, bias1, Wl2, bl2, Wr2, br2, att2, bias2, Wlin, blin):
        import jax, jax.numpy as jnp
        import numpy as np
        NEG_SLOPE = 0.2

        def _gatv2_layer(x, src, dst, Wl, bl, Wr, br, att, bias, heads, out_ch, concat):
            N = x.shape[0]
            xl = (x @ Wl + bl).reshape(N, heads, out_ch)
            xr = (x @ Wr + br).reshape(N, heads, out_ch)
            e = jax.nn.leaky_relu(xl[src] + xr[dst], NEG_SLOPE)
            logits = jnp.einsum('ehc,hc->eh', e, att)
            m = jax.ops.segment_max(logits, dst, num_segments=N)
            ex = jnp.exp(logits - m[dst])
            denom = jax.ops.segment_sum(ex, dst, num_segments=N)
            alpha = ex / denom[dst]
            msg = xl[src] * alpha[..., None]
            out = jax.ops.segment_sum(msg, dst, num_segments=N)
            if concat:
                out = out.reshape(N, heads * out_ch)
            else:
                out = out.mean(axis=1)
            return out + bias
        N = x.shape[0]
        loops = jnp.arange(N, dtype=edge_index.dtype)
        src = jnp.concatenate([edge_index[0], loops])
        dst = jnp.concatenate([edge_index[1], loops])
        h = _gatv2_layer(x, src, dst, Wl1, bl1, Wr1, br1, att1, bias1, heads=8, out_ch=16, concat=True)
        h = jax.nn.elu(h)
        h = _gatv2_layer(h, src, dst, Wl2, bl2, Wr2, br2, att2, bias2, heads=1, out_ch=64, concat=False)
        h = jax.nn.elu(h)
        h = jax.nn.elu(h @ Wlin + blin)
        return h

    def _L1_gnn_ref(x, edge_index, edge_weight, W, b, ln_gamma, ln_beta):
        import jax, jax.numpy as jnp
        import numpy as np
        N_NODES = 12500
        N_EDGES = 50000
        IN_DIM = 128
        OUT_DIM = 128
        LN_EPS = 1e-05
        N = x.shape[0]
        xw = x @ W
        loop = jnp.arange(N, dtype=edge_index.dtype)
        row = jnp.concatenate([edge_index[0], loop])
        col = jnp.concatenate([edge_index[1], loop])
        w = jnp.concatenate([edge_weight, jnp.ones((N,), dtype=edge_weight.dtype)])
        deg = jax.ops.segment_sum(w, col, num_segments=N)
        deg_inv_sqrt = jnp.where(deg > 0, jax.lax.rsqrt(jnp.where(deg > 0, deg, 1.0)), 0.0)
        norm = deg_inv_sqrt[row] * w * deg_inv_sqrt[col]
        msgs = norm[:, None] * xw[row]
        out = jax.ops.segment_sum(msgs, col, num_segments=N)
        out = out + b
        mu = jnp.mean(out, axis=-1, keepdims=True)
        var = jnp.mean(jnp.square(out - mu), axis=-1, keepdims=True)
        out = (out - mu) * jax.lax.rsqrt(var + LN_EPS) * ln_gamma + ln_beta
        return out

    def _L2_gnn_ref(x_feat, edge_attr, bases, src, dst, W1, b1, W2, b2, g1, be1, W3, b3, g2, be2):
        import jax, jax.numpy as jnp
        import numpy as np
        N, E, H = (5000, 80000, 128)
        EPS = 1e-05

        def _bn(x, gamma, beta):
            mu = jnp.mean(x, axis=0)
            var = jnp.mean((x - mu) ** 2, axis=0)
            return (x - mu) * jax.lax.rsqrt(var + EPS) * gamma + beta
        n_nodes = x_feat.shape[0]
        pos_e = x_feat[src] + edge_attr
        v = jax.nn.gelu(pos_e @ W1.T + b1, approximate=False) * bases
        aggr = jax.ops.segment_sum(v, dst, num_segments=n_nodes)
        h = _bn(aggr @ W2.T + b2, g1, be1)
        h = jax.nn.gelu(h, approximate=False)
        h = _bn(h @ W3.T + b3, g2, be2)
        return jax.nn.gelu(h, approximate=False)

    def _L3_gnn_ref(x, edge_index, edge_weight, W_init, W1, b1, W2, b2, W3, b3):
        import jax, jax.numpy as jnp
        import numpy as np
        from jax import lax
        N, E, D = (12500, 100000, 128)

        def _gcn_conv(x, W, b, src, dst, ew, n):
            xw = x @ W
            deg = jax.ops.segment_sum(ew, dst, num_segments=n)
            dinv = lax.rsqrt(deg)
            norm = dinv[src] * ew * dinv[dst]
            msg = xw[src] * norm[:, None]
            out = jax.ops.segment_sum(msg, dst, num_segments=n)
            return out + b
        n = x.shape[0]
        loops = jnp.arange(n)
        src = jnp.concatenate([edge_index[0], loops])
        dst = jnp.concatenate([edge_index[1], loops])
        ew = jnp.concatenate([edge_weight, jnp.ones((n,), edge_weight.dtype)])
        h = x @ W_init
        x1 = _gcn_conv(h, W1, b1, src, dst, ew, n)
        x1 = jax.nn.relu(x1 + h)
        x2 = _gcn_conv(x1, W2, b2, src, dst, ew, n)
        x2 = jax.nn.relu(x2 + h)
        x3 = _gcn_conv(x2, W3, b3, src, dst, ew, n)
        return x3 + h
    edge_index = jnp.stack([src, dst])
    h = jnp.maximum(_layernorm(x, axis=-1), 0.0)
    x = x + _L0_gnn_ref(h, edge_index, L0_gnn_Wl1, L0_gnn_bl1, L0_gnn_Wr1, L0_gnn_br1, L0_gnn_att1, L0_gnn_bias1, L0_gnn_Wl2, L0_gnn_bl2, L0_gnn_Wr2, L0_gnn_br2, L0_gnn_att2, L0_gnn_bias2, L0_gnn_Wlin, L0_gnn_blin)
    h = jnp.maximum(_layernorm(x, axis=-1), 0.0)
    x = x + _L1_gnn_ref(h, edge_index, edge_weight, L1_gnn_W, L1_gnn_b, L1_gnn_ln_gamma, L1_gnn_ln_beta)
    h = jnp.maximum(_layernorm(x, axis=-1), 0.0)
    x = x + _L2_gnn_ref(h, edge_attr_128, edge_attr_128_n2, src, dst, L2_gnn_W1, L2_gnn_b1, L2_gnn_W2, L2_gnn_b2, L2_gnn_g1, L2_gnn_be1, L2_gnn_W3, L2_gnn_b3, L2_gnn_g2, L2_gnn_be2)
    h = jnp.maximum(_layernorm(x, axis=-1), 0.0)
    x = x + _L3_gnn_ref(h, edge_index, edge_weight, L3_gnn_W_init, L3_gnn_W1, L3_gnn_b1, L3_gnn_W2, L3_gnn_b2, L3_gnn_W3, L3_gnn_b3)
    return x

_drawn_inputs = setup_inputs


def setup_inputs(seed=0):
    import zlib

    import numpy as np

    out = dict(_drawn_inputs(seed))
    spreads = {'L0_gnn_bl1': (0.0, 0.1),
     'L0_gnn_br1': (0.0, 2.0),
     'L0_gnn_bias1': (0.0, 0.1),
     'L0_gnn_bl2': (0.0, 0.1),
     'L0_gnn_br2': (0.0, 2.0),
     'L0_gnn_bias2': (0.0, 0.1),
     'L0_gnn_blin': (0.0, 0.1),
     'L1_gnn_b': (0.0, 0.1),
     'L1_gnn_ln_gamma': (1.0, 0.2),
     'L1_gnn_ln_beta': (0.0, 0.1),
     'L2_gnn_b1': (0.0, 0.1),
     'L2_gnn_b2': (0.0, 2.0),
     'L2_gnn_g1': (1.0, 0.2),
     'L2_gnn_be1': (0.0, 0.268),
     'L2_gnn_b3': (0.0, 2.0),
     'L2_gnn_g2': (1.0, 0.2),
     'L2_gnn_be2': (0.0, 0.1),
     'L3_gnn_b1': (0.0, 0.325),
     'L3_gnn_b2': (0.0, 0.283),
     'L3_gnn_b3': (0.0, 0.1)}
    factors = {'L0_gnn_Wr1': 38.891, 'L0_gnn_Wr2': 43.41, 'L0_gnn_att2': 23.351}
    for name, (base, spread) in spreads.items():
        noise = np.random.default_rng([zlib.crc32(name.encode()), seed]).standard_normal(out[name].shape)
        drawn = base * np.exp(spread * noise) if base else spread * noise
        out[name] = jnp.asarray(drawn.astype(out[name].dtype))
    for name, factor in factors.items():
        out[name] = (out[name] * factor).astype(out[name].dtype)
    return out
```

```python
from contextlib import ExitStack

import numpy as np

import concourse.bass as bass
from concourse import mybir

ALU = mybir.AluOpType
ACT = mybir.ActivationFunctionType
F32 = mybir.dt.float32
I32 = mybir.dt.int32
AX_X = mybir.AxisListType.X
DVE = mybir.EngineType.DVE
PE = mybir.EngineType.PE
SP = mybir.EngineType.SP

P = 128
N, D, E = 6250, 128, 106250
NB = -(-N // P)
NPAD = NB * P
LAST = N - (NB - 1) * P
FRONT = P
TAIL = 2 * P
GT = 4
RING = 4
SORT_T = -(-E // P)
TILES = -(-((E + NB * (P - 1)) // P) // (GT * RING)) * GT * RING
GROUPS = TILES // GT
TCOL = -(-TILES // P)
TTAB = TCOL * P
BIG = 1e30
EPS = 1e-5
H1, C1, C2 = 8, 16, 64
SLOPE = 0.2
NCH = 7
WMAX = D + 2 * H1 + 2
EP, EC = 125, E // 125


class Sems:

    SOFT = ("gathered", "windows", "scattered")

    def __init__(self, nc, most=32):
        self.nc, self.names = nc, {}
        self.pool = [nc.alloc_semaphore(f"pool{i}") for i in range(most)]
        self.ids = range(self.pool[0].num, self.pool[0].num + most)
        assert [s.num for s in self.pool] == list(self.ids)
        self.free = list(self.pool)

    def __call__(self, name):
        if name not in self.names:
            soft = name.startswith(self.SOFT)
            self.names[name] = self.nc.alloc_semaphore(f"{name}_{self.nc.next_id()}") if soft else self.free.pop(0)
        return self.names[name]

    def end_stage(self):
        self.nc.all_engine_barrier(sems_to_clear=self.ids)
        self.names, self.free = {}, list(self.pool)


class Chain:

    def __init__(self, sem, base=0, settle=None):
        self.sem, self.n, self.settle = sem, base, settle

    def run(self, eng, ins_of, by=1):
        wait(eng, self.sem, self.n)
        if self.settle:
            self.settle(eng)
        ins_of().then_inc(self.sem, by)
        self.n = self.n + by


def wait(eng, sem, value):
    if not (isinstance(value, int) and value <= 0):
        eng.wait_ge(sem, value)


def pipeline(nc, pieces):
    most = max(late for _, late in pieces)
    first = -(-(most + RING) // RING) * RING

    def step(turn, u):
        for piece, late in pieces:
            slot = (u - late) % RING
            own = turn + (u - late - slot) // RING
            q = own * RING + slot
            if isinstance(q, int) and not 0 <= q < GROUPS:
                continue
            piece(q, slot, own)

    for t in range(first):
        step(t // RING, t % RING)
    with nc.Fori(first // RING, GROUPS // RING) as turn:
        for u in range(RING):
            step(turn, u)
    for t in range(GROUPS, GROUPS + most):
        step(t // RING, t % RING)


def gnn(nc, A, out):
    S = Sems(nc)
    ve, ac, pe, po, sp = nc.vector, nc.scalar, nc.tensor, nc.gpsimd, nc.sync
    with ExitStack() as ctx:
        def sb(name, shape, dt=F32):
            return ctx.enter_context(nc.sbuf_tensor(name, shape, dt))

        def dram(name, shape, dt=F32):
            return nc.dram_tensor(name, shape, dt).ap()

        ident = sb("ident", [P, P])
        iota_row = sb("iota_row", [P, P])
        iota_col = sb("iota_col", [P, 1])
        ones = sb("ones", [P, P])
        real = sb("real", [P, P])
        before = sb("before", [P, P])
        X = sb("X", [P, NB, D])
        BUF = [sb(f"BUF{i}", [P, NB, D]) for i in range(3)]
        ACC = sb("ACC", [P, NB * WMAX])
        LOCAL = sb("LOCAL", [P, TTAB])
        NEWSEG = sb("NEWSEG", [P, TTAB])
        WEIGHT = sb("WEIGHT", [P, TTAB])
        SRC = sb("SRC", [P, TTAB], I32)
        BLOCK = sb("BLOCK", [1, TTAB], I32)
        START = sb("START", [1, TTAB], I32)
        FLAG = sb("FLAG", [1, 4], I32)
        G = sb("G", [P, RING, GT, D + H1])
        IDX = sb("IDX", [P, RING, GT], I32)
        OH = sb("OH", [P, 2, GT, P])
        st = [sb(f"st{i}", [P, NB * H1]) for i in range(5)]
        dinv_guarded = sb("dinv_guarded", [P, NB])
        dinv = sb("dinv", [P, NB])
        bias = sb("bias", [P, D])
        gain = sb("gain", [P, D])
        att = sb("att", [P, D])
        wmat = sb("wmat", [P, D])

        src_s = dram("src_sorted", [E + TAIL], I32)
        dst_s = dram("dst_sorted", [FRONT + E + TAIL], I32)
        w_s = dram("w_sorted", [E + TAIL])
        attr_s = dram("attr_sorted", [E + P, D])
        base_s = dram("bases_sorted", [E + P, D])
        table = dram("table", [NPAD, D])
        table2 = dram("table2", [NPAD, C2])
        open_d = dram("open_pen", [TTAB * P])
        close_d = dram("close_pen", [TTAB * P])
        kept_d = dram("kept", [GROUPS, P, GT * (D + H1)])
        runmax_d = dram("runmax", [H1, GROUPS * GT * P])

        named = [0]

        def psum(stack, name, shape):
            named[0] += 1
            return stack.enter_context(nc.psum_tensor(f"{name}_{named[0]}", shape, F32))

        chain = [None]

        def begin():
            chain[0] = Chain(S("chain"))

        def go(eng, f, by=1):
            chain[0].run(eng, f, by=by)

        def load(dst, src):
            go(sp, lambda: sp.dma_start(dst, src), by=16)

        def end():
            sp.wait_ge(chain[0].sem, chain[0].n)
            S.end_stage()

        def spread(row, width):
            return row.rearrange("(a n) -> a n", a=1).broadcast_to([P, width])

        def settle(eng, name):
            eng.sem_inc(S(f"settled_{name}"), 1)

        def wide(a, n=NB):
            return a.unsqueeze(1).broadcast_to([P, n, a.shape[1]])

        def tall(a, width=D):
            return a.unsqueeze(2).broadcast_to([P, a.shape[1], width])

        def constants():
            begin()
            go(po, lambda: po.iota(SRC[:, 0:P], pattern=[[1, P]], base=0, channel_multiplier=0))
            go(ve, lambda: ve.tensor_copy(iota_row[:, :], SRC[:, 0:P]))
            go(po, lambda: po.iota(SRC[:, 0:1], pattern=[[1, 1]], base=0, channel_multiplier=1))
            go(ve, lambda: ve.tensor_copy(iota_col[:, :], SRC[:, 0:1]))
            go(ve, lambda: ve.memset(ones[:, :], 1.0))
            go(ve, lambda: ve.tensor_scalar(ident[:, :], iota_row[:, :], iota_col[:, 0:1], None, ALU.is_equal))
            go(ve, lambda: ve.tensor_scalar(before[:, :], iota_row[:, :], iota_col[:, 0:1], None, ALU.is_gt))
            go(ve, lambda: ve.tensor_scalar(real[:, :], ones[:, :], iota_col[:, 0:1], float(LAST),
                                            ALU.mult, ALU.is_lt))
            end()

        def sort_edges():
            begin()
            cnt = st[0][:, 0:NB + 1]
            starts = st[1][:, 0:NB + 2]
            thr = st[2][:, 0:NB]
            here = BUF[0][:, :, :].rearrange("p b d -> p (b d)")
            after = BUF[1][:, :, :].rearrange("p b d -> p (b d)")
            junk = BUF[2][:, :, :].rearrange("p b d -> p (b d)")
            here_i = here[0:EP, 2 * EC:3 * EC].bitcast(I32)
            after_i = after[0:EP, 2 * EC:3 * EC].bitcast(I32)
            load(src_s, A["src"])
            load(dst_s, A["dst"])
            load(w_s, A["edge_weight"])
            load(here_i, A["dst"][FRONT:FRONT + E].rearrange("(p c) -> p c", p=EP))
            load(after_i, A["dst"][FRONT + 1:FRONT + 1 + E].rearrange("(p c) -> p c", p=EP))
            go(ve, lambda: ve.tensor_copy(here[0:EP, 0:EC], here_i))
            go(ve, lambda: ve.tensor_copy(after[0:EP, 0:EC], after_i))
            go(ve, lambda: ve.memset(cnt, 0.0))
            go(ve, lambda: ve.tensor_scalar(thr, iota_row[:, 0:NB], float(P), None, ALU.mult))
            go(ve, lambda: ve.tensor_tensor(junk[0:EP, 0:EC], here[0:EP, 0:EC], after[0:EP, 0:EC], ALU.is_gt))
            go(ve, lambda: ve.tensor_reduce(cnt[0:EP, NB:NB + 1], junk[0:EP, 0:EC], AX_X, ALU.add))
            lap = S("count")
            ve.wait_ge(chain[0].sem, chain[0].n)
            ve.tensor_copy(junk[0:EP, 0:1], here[0:EP, 0:1]).then_inc(lap, 1)
            with ve.Fori(0, NB) as t:
                ve.wait_ge(lap, t + 1)
                ve.tensor_scalar(junk[0:EP, 0:EC], here[0:EP, 0:EC], thr[0:EP, bass.ds(t, 1)], 0.0,
                                 ALU.is_lt, ALU.add, accum_out=cnt[0:EP, bass.ds(t, 1)]).then_inc(lap, 1)
            pe.wait_ge(lap, NB + 1)
            with ExitStack() as ps:
                tot = psum(ps, "tot", [P, 64])
                go(pe, lambda: pe.matmul(tot[:, 0:NB + 1], ones[0:EP, :], cnt[0:EP, :], start=True, stop=True))
                go(ve, lambda: ve.tensor_copy(starts[:, 0:NB], tot[:, 0:NB]))
                go(ve, lambda: ve.tensor_scalar(junk[:, 0:1], tot[:, NB:NB + 1], 1.0, None, ALU.min))
            go(ve, lambda: ve.memset(starts[:, NB:NB + 1], float(E)))
            go(ve, lambda: ve.tensor_copy(FLAG[0:1, 0:1], junk[0:1, 0:1]))
            end()
            unsorted = nc.values_load(FLAG[0:1, 0:1], min_val=0, max_val=1,
                                      skip_runtime_bounds_check_because="it is a minimum with 1")
            with nc.If(unsorted == 1):
                counting_sort()
            nc.all_engine_barrier()

        def counting_sort():
            NA = NB + 1
            where = st[3][:, 0:NA]
            small = st[4]
            oh_b, oh_a = BUF[0][:, 0, :], BUF[0][:, 1, 0:NA]
            oh_bT, oh_aT, same = BUF[0][:, 2, :], BUF[0][:, 3, :], BUF[0][:, 4, :]
            attr_t, base_t = BUF[0][:, 5, :], BUF[0][:, 6, :]
            d_i, b_i, a_i, s_i, pos_i, pos_d = (BUF[0][:, 7, j:j + 1].bitcast(I32) for j in range(6))
            w_t, b_f, a_f, pos = (BUF[0][:, 7, j:j + 1] for j in range(8, 12))
            lap = S("lap")
            scattered = [S(f"scattered{j}") for j in range(5)]

            def digits(k, c):
                c.run(sp, lambda: sp.dma_start(d_i, A["dst"][bass.ds(k * P + FRONT, P)].rearrange("(p a) -> p a", a=1)),
                      by=16)
                c.run(ve, lambda: ve.tensor_scalar(b_i, d_i, P - 1, None, ALU.bitwise_and))
                c.run(ve, lambda: ve.tensor_scalar(a_i, d_i, 7, None, ALU.logical_shift_right))
                c.run(ve, lambda: ve.tensor_copy(b_f, b_i))
                c.run(ve, lambda: ve.tensor_copy(a_f, a_i))
                c.run(ve, lambda: ve.tensor_scalar(oh_b, iota_row[:, :], b_f, None, ALU.is_equal))
                c.run(ve, lambda: ve.tensor_scalar(oh_a, iota_row[:, 0:NA], a_f, None, ALU.is_equal))

            with ExitStack() as ps:
                pa, pb, pc = (psum(ps, f"ps{j}", [P, 512]) for j in range(3))

                def looped(body, steps, start):
                    with nc.Fori(0, SORT_T) as k:
                        c = Chain(lap, k * steps + start, lambda eng: settle(eng, "sync") if eng is sp else None)
                        body(k, c)
                    return start + SORT_T * steps

                c = Chain(lap)
                c.run(ve, lambda: ve.memset(where, 0.0))
                c.run(sp, lambda: sp.dma_start(attr_s[E:E + P, :], A["edge_attr_128"][E:E + P, :]), by=16)
                c.run(sp, lambda: sp.dma_start(base_s[E:E + P, :], A["edge_attr_128_n2"][E:E + P, :]), by=16)

                def count(k, c):
                    digits(k, c)
                    c.run(pe, lambda: pe.matmul(pa[:, 0:NA], oh_b, oh_a, start=True, stop=True))
                    c.run(ve, lambda: ve.tensor_tensor(where, where, pa[:, 0:NA], ALU.add))

                at = looped(count, 24, c.n)
                c = Chain(lap, at)
                c.run(pe, lambda: pe.matmul(pa[:, 0:NA], ones[:, :], where, start=True, stop=True))
                c.run(ve, lambda: ve.tensor_copy(small[:, 0:NA], pa[:, 0:NA]))
                c.run(ve, lambda: ve.tensor_tensor_scan(small[:, NA:2 * NA], small[:, 0:NA], small[:, 0:NA], 0.0,
                                                        ALU.add, ALU.bypass))
                c.run(pe, lambda: pe.matmul(pb[:, 0:NA], before[:, :], where, start=True, stop=True))
                c.run(ve, lambda: ve.tensor_tensor(small[:, NA:2 * NA], small[:, NA:2 * NA], small[:, 0:NA],
                                                   ALU.subtract))
                c.run(ve, lambda: ve.tensor_tensor(where, small[:, NA:2 * NA], pb[:, 0:NA], ALU.add))

                def place(k, c):
                    digits(k, c)
                    c.run(sp, lambda: sp.dma_start(s_i, A["src"][bass.ds(k * P, P)].rearrange("(p a) -> p a", a=1)),
                          by=16)
                    c.run(sp, lambda: sp.dma_start(w_t, A["edge_weight"][bass.ds(k * P, P)]
                                                   .rearrange("(p a) -> p a", a=1)), by=16)
                    c.run(sp, lambda: sp.dma_start(attr_t, A["edge_attr_128"][bass.ds(k * P, P), :]), by=16)
                    c.run(sp, lambda: sp.dma_start(base_t, A["edge_attr_128_n2"][bass.ds(k * P, P), :]), by=16)
                    c.run(pe, lambda: pe.transpose(pa[:, 0:P], oh_b, ident[:, :]))
                    c.run(ve, lambda: ve.tensor_copy(oh_bT, pa[:, 0:P]))
                    c.run(pe, lambda: pe.matmul(pa[0:NA, 0:P], oh_a, ident[:, :], start=True, stop=True))
                    c.run(ve, lambda: ve.tensor_copy(oh_aT[0:NA, :], pa[0:NA, 0:P]))
                    c.run(pe, lambda: pe.matmul(pa[:, 0:P], oh_bT, oh_bT, start=True, stop=True))
                    c.run(pe, lambda: pe.matmul(pb[:, 0:P], oh_aT[0:NA, :], oh_aT[0:NA, :], start=True, stop=True))
                    c.run(ve, lambda: ve.tensor_tensor(same, before[:, :], pa[:, 0:P], ALU.mult))
                    c.run(ve, lambda: ve.tensor_tensor(same, same, pb[:, 0:P], ALU.mult))
                    c.run(pe, lambda: pe.matmul(pc[:, 0:1], same, ones[:, 0:1], start=True, stop=True))
                    c.run(pe, lambda: pe.matmul(pa[:, 0:NA], oh_bT, where, start=True, stop=True))
                    c.run(ve, lambda: ve.tensor_tensor(same[:, 0:NA], oh_a, pa[:, 0:NA], ALU.mult))
                    c.run(ve, lambda: ve.tensor_reduce(pos, same[:, 0:NA], AX_X, ALU.add))
                    c.run(ve, lambda: ve.tensor_tensor(pos, pos, pc[:, 0:1], ALU.add))
                    c.run(ve, lambda: ve.tensor_copy(pos_i, pos))
                    c.run(ve, lambda: ve.tensor_scalar(pos_d, pos, float(FRONT), None, ALU.add))
                    for j, (rows, at, dst) in enumerate(((s_i, pos_i, src_s), (d_i, pos_d, dst_s),
                                                         (w_t, pos_i, w_s))):
                        po.wait_ge(lap, c.n)
                        settle(po, "pool")
                        po.indirect_dma_start(dst.rearrange("(n a) -> n a", a=1),
                                              bass.IndirectOffsetOnAxis(ap=at, axis=0), rows, None
                                              ).then_inc(scattered[j], 16)
                    for j, (rows, dst) in enumerate(((attr_t, attr_s), (base_t, base_s))):
                        po.indirect_dma_start(dst, bass.IndirectOffsetOnAxis(ap=pos_i, axis=0), rows, None
                                              ).then_inc(scattered[3 + j], 16)
                    for s in scattered:
                        po.wait_ge(s, 16 * k + 16)
                    po.wait_ge(lap, c.n)
                    c.n = c.n + 1
                    po.sem_inc(lap, 1)
                    c.run(pe, lambda: pe.matmul(pb[:, 0:NA], oh_b, oh_a, start=True, stop=True))
                    c.run(ve, lambda: ve.tensor_tensor(where, where, pb[:, 0:NA], ALU.add))

                at = looped(place, 22 + 64 + 15 + 1 + 2, c.n)
                sp.wait_ge(lap, at)

        def tile_tables():
            begin()
            starts = st[1][:, 0:NB + 1]
            starts_t = st[1][:, 0:NB]
            number = st[2][:, 0:NB + 1]
            number_i = st[3][:, 0:NB].bitcast(I32)
            first = st[4][:, 0:NB]
            shift = st[4][:, NB:2 * NB]
            step = st[4][:, 2 * NB:3 * NB]
            kk = st[0][:, 0:TCOL]
            blk = st[0][:, 8:8 + TCOL]
            edge = st[0][:, 16:16 + TCOL]
            edge_i = st[0][:, 24:24 + TCOL].bitcast(I32)
            prev_i = st[0][:, 32:32 + TCOL].bitcast(I32)
            scaled = st[0][:, 40:40 + TCOL]
            go(ve, lambda: ve.tensor_tensor(number[:, 0:NB], starts[:, 1:NB + 1], starts_t, ALU.subtract))
            go(ve, lambda: ve.tensor_scalar(number[:, 0:NB], number[:, 0:NB], float(P - 1), None, ALU.add))
            go(ve, lambda: ve.tensor_copy(number_i, number[:, 0:NB]))
            go(ve, lambda: ve.tensor_scalar(number_i, number_i, 7, None, ALU.logical_shift_right))
            go(ve, lambda: ve.tensor_copy(number[:, 0:NB], number_i))
            go(ve, lambda: ve.tensor_tensor_scan(first, number[:, 0:NB], number[:, 0:NB], 0.0, ALU.add, ALU.bypass))
            go(ve, lambda: ve.tensor_tensor(first, first, number[:, 0:NB], ALU.subtract))
            go(ve, lambda: ve.scalar_tensor_tensor(shift, first, float(-P), starts_t, ALU.mult, ALU.add))
            go(ve, lambda: ve.tensor_copy(step, shift))
            go(ve, lambda: ve.tensor_tensor(step[:, 1:NB], shift[:, 1:NB], shift[:, 0:NB - 1], ALU.subtract))
            for g in range(TCOL):
                go(ve, lambda: ve.tensor_scalar(kk[:, g:g + 1], iota_col[:, :], float(g * P), None, ALU.add))
            cube = BUF[0][:, 0:TCOL * NB * 2 // P + 1, :].rearrange("p b d -> p (b d)")
            le = cube[:, 0:TCOL * NB].rearrange("p (g t) -> p g t", g=TCOL)
            part = cube[:, TCOL * NB:2 * TCOL * NB].rearrange("p (g t) -> p g t", g=TCOL)
            go(ve, lambda: ve.tensor_tensor(le, first.unsqueeze(1).broadcast_to([P, TCOL, NB]),
                                            kk.unsqueeze(2).broadcast_to([P, TCOL, NB]), ALU.is_le))
            go(ve, lambda: ve.tensor_reduce(blk, le, AX_X, ALU.add))
            go(ve, lambda: ve.tensor_scalar(blk, blk, -1.0, None, ALU.add))
            go(ve, lambda: ve.tensor_tensor(part, le, step.unsqueeze(1).broadcast_to([P, TCOL, NB]), ALU.mult))
            go(ve, lambda: ve.tensor_reduce(edge, part, AX_X, ALU.add))
            go(ve, lambda: ve.scalar_tensor_tensor(edge, kk, float(P), edge, ALU.mult, ALU.add))
            go(ve, lambda: ve.tensor_scalar(edge, edge, float(E), None, ALU.min))
            go(ve, lambda: ve.tensor_copy(edge_i, edge))
            go(ve, lambda: ve.tensor_scalar(prev_i, edge, float(FRONT - 1), None, ALU.add))
            go(ve, lambda: ve.tensor_scalar(scaled, blk, float(P), None, ALU.mult))
            with ExitStack() as ps:
                rows = psum(ps, "rows", [1, 2, 1024])
                for n, (col, tab) in enumerate(((blk, BLOCK), (edge, START))):
                    for g in range(TCOL):
                        go(pe, lambda: pe.matmul(rows[0:1, n, g * P:(g + 1) * P], col[:, g:g + 1], ident[:, :],
                                                 start=True, stop=True))
                    go(ve, lambda: ve.tensor_copy(tab[0:1, :], rows[0:1, n, 0:TTAB]))
            W3 = P + 2
            raw = BUF[0][:, :, :].rearrange("p b d -> p (b d)")
            dst_i = raw[:, 0:TCOL * W3].bitcast(I32).rearrange("p (g e) -> p g e", g=TCOL)
            src_i = raw[:, 1024:1024 + TTAB].bitcast(I32).rearrange("p (g e) -> p g e", g=TCOL)
            wt = raw[:, 2048:2048 + TTAB].rearrange("p (g e) -> p g e", g=TCOL)
            two = BUF[1][:, :, :].rearrange("p b d -> p (b d)")
            dst_f = two[:, 0:TCOL * W3].rearrange("p (g e) -> p g e", g=TCOL)
            src_f = two[:, 1024:1024 + TTAB].rearrange("p (g e) -> p g e", g=TCOL)
            local, new, pen_open, pen_close = (
                two[:, 1024 * j:1024 * j + TTAB].rearrange("p (g e) -> p g e", g=TCOL) for j in (2, 3, 4, 5))
            for g in range(TCOL):
                for tile, tab, at, w in ((dst_i, dst_s, prev_i, W3), (src_i, src_s, edge_i, P), (wt, w_s, edge_i, P)):
                    total = tab.shape[0]
                    view = tab[0:total // w * w].rearrange("(n e) -> n e", e=w)
                    po.wait_ge(chain[0].sem, chain[0].n)
                    po.indirect_dma_start(tile[:, g, :], None, view,
                                          bass.IndirectOffsetOnAxis(ap=at[:, g:g + 1], axis=1)
                                          ).then_inc(S("windows"), 16)
            ve.wait_ge(S("windows"), 3 * TCOL * 16)
            go(ve, lambda: ve.tensor_copy(dst_f, dst_i))
            go(ve, lambda: ve.tensor_copy(src_f, src_i))
            mid = dst_f[:, :, 1:P + 1]
            go(ve, lambda: ve.tensor_tensor(local, mid, scaled.unsqueeze(2).broadcast_to([P, TCOL, P]), ALU.subtract))
            go(ve, lambda: ve.tensor_tensor(new, mid, dst_f[:, :, 0:P], ALU.not_equal))
            go(ve, lambda: ve.tensor_scalar(pen_open, new, -BIG, None, ALU.mult))
            go(ve, lambda: ve.tensor_tensor(pen_close, mid, dst_f[:, :, 2:P + 2], ALU.not_equal))
            go(ve, lambda: ve.tensor_scalar(pen_close, pen_close, -BIG, None, ALU.mult))
            load(open_d.rearrange("(g p e) -> p g e", g=TCOL, p=P), pen_open)
            load(close_d.rearrange("(g p e) -> p g e", g=TCOL, p=P), pen_close)
            with ExitStack() as ps:
                turned = psum(ps, "turned", [P, 1024])
                for rows, tab in ((local, LOCAL), (new, NEWSEG), (wt, WEIGHT), (src_f, SRC)):
                    for g in range(TCOL):
                        go(pe, lambda: pe.transpose(turned[:, g * P:(g + 1) * P], rows[:, g, :], ident[:, :]))
                    go(ve, lambda: ve.tensor_copy(tab[:, :], turned[:, 0:TTAB]))
            end()

        def norm(src, dst, eps=EPS):
            mean, var = st[0][:, 0:NB], st[1][:, 0:NB]
            sq = ACC[:, 0:NB * D].rearrange("p (b d) -> p b d", b=NB)
            go(ve, lambda: ve.tensor_reduce(mean, src, AX_X, ALU.add))
            go(ve, lambda: ve.tensor_scalar(mean, mean, 1.0 / D, None, ALU.mult))
            go(ve, lambda: ve.tensor_tensor(dst, src, tall(mean), ALU.subtract))
            go(ve, lambda: ve.tensor_tensor(sq, dst, dst, ALU.mult))
            go(ve, lambda: ve.tensor_reduce(var, sq, AX_X, ALU.add))
            go(ve, lambda: ve.tensor_scalar(var, var, 1.0 / D, eps, ALU.mult, ALU.add))
            inv_sqrt(var, var)
            go(ve, lambda: ve.tensor_tensor(dst, dst, tall(var), ALU.mult))

        def inv_sqrt(dst, src):
            w = src.shape[1]
            y, t = st[4][:, 0:w], st[4][:, w:2 * w]
            go(ve, lambda: ve.reciprocal(y, src))
            go(ac, lambda: ac.activation(y, y, ACT.Sqrt))
            go(ve, lambda: ve.tensor_tensor(t, y, y, ALU.mult))
            go(ve, lambda: ve.tensor_tensor(t, t, src, ALU.mult))
            go(ve, lambda: ve.tensor_scalar(t, t, -0.5, 1.5, ALU.mult, ALU.add))
            go(ve, lambda: ve.tensor_tensor(dst, y, t, ALU.mult))

        def relu(a):
            go(ve, lambda: ve.tensor_scalar(a, a, 0.0, None, ALU.max))

        def elu(a, tmp):
            go(ve, lambda: ve.tensor_scalar(tmp, a, 0.0, None, ALU.min))
            go(ac, lambda: ac.activation(tmp, tmp, ACT.Exp))
            go(ve, lambda: ve.tensor_scalar(a, a, 0.0, -1.0, ALU.max, ALU.add))
            go(ve, lambda: ve.tensor_tensor(a, a, tmp, ALU.add))

        def dense(src, weight, dst, K=D, M=D, bias_of=None):
            load(wmat[0:K, 0:M], weight)
            if bias_of is not None:
                load(bias[:, 0:M], spread(bias_of, M))
            end()
            turned, copied, product, moved = S("turned"), S("copied"), S("product"), S("moved")
            room = G[:, :, :, :].rearrange("p r t d -> p (r t d)")
            tT = room[:, 0:NCH * P]
            chunk = room[:, NCH * P:NCH * (P + K)].rearrange("p (b k) -> p b k", b=NCH)
            staged = S("staged")
            with ExitStack() as ps:
                tp = psum(ps, "tp", [P, 1024])
                yp = psum(ps, "yp", [P, 8, P])
                pe.sem_inc(turned, 1)
                pe.sem_inc(product, 1)
                ve.sem_inc(moved, 1)
                with nc.Fori(0, NB // NCH) as c:
                    po.wait_ge(turned, c + 1)
                    po.tensor_copy(chunk, src[:, bass.ds(c * NCH, NCH), :]).then_inc(staged, 1)
                    pe.wait_ge(staged, c + 1)
                    settle(pe, "tensor")
                    for j in range(NCH):
                        m = pe.transpose(tp[0:K, j * P:(j + 1) * P], chunk[:, j, :], ident[:, :])
                    m.then_inc(turned, 1)
                    ac.wait_ge(turned, c + 2)
                    ac.wait_ge(product, c + 1)
                    ac.activation(tT[0:K, 0:NCH * P], tp[0:K, 0:NCH * P], ACT.Copy).then_inc(copied, 1)
                    pe.wait_ge(copied, c + 1)
                    pe.wait_ge(moved, c + 1)
                    for j in range(NCH):
                        m = pe.matmul(yp[:, j, 0:M], tT[0:K, j * P:(j + 1) * P], wmat[0:K, 0:M],
                                      start=True, stop=True)
                    m.then_inc(product, 1)
                    ve.wait_ge(product, c + 2)
                    to = dst[:, bass.ds(c * NCH, NCH), :]
                    if bias_of is not None:
                        ve.tensor_tensor(to, yp[:, 0:NCH, 0:M], wide(bias[:, 0:M], NCH), ALU.add).then_inc(moved, 1)
                    else:
                        ve.tensor_copy(to, yp[:, 0:NCH, 0:M]).then_inc(moved, 1)
                ve.wait_ge(moved, NB // NCH + 1)
            S.end_stage()
            begin()

        def store_table(tab, src):
            load(tab.rearrange("(b p) d -> p b d", p=P), src)

        def blocks_of(engine, q):
            return nc.values_load_multi_w_load_instructions(
                BLOCK[0:1, bass.ds(q * GT, GT)], engines=(engine,), min_val=0, max_val=NB - 1,
                skip_runtime_bounds_check_because="a tile's block is a count of blocks, less one")[1]

        def gather_pieces(tab, width):
            def copy_index(q, slot, turn):
                wait(ac, S(f"gathered{slot}"), 16 * GT * turn)
                ac.activation(IDX[:, slot, :], SRC[:, bass.ds(q * GT, GT)], ACT.Copy).then_inc(S("indexed"), 1)

            def gather(q, slot, turn):
                po.wait_ge(S("indexed"), q + 1)
                wait(po, S("g_free"), q - RING + 1)
                settle(po, "pool")
                for j in range(GT):
                    po.indirect_dma_start(G[:, slot, j, 0:width], None, tab,
                                          bass.IndirectOffsetOnAxis(ap=IDX[:, slot, j:j + 1], axis=0)
                                          ).then_inc(S(f"gathered{slot}"), 16)
            return copy_index, gather

        def gathered(eng, slot, turn):
            eng.wait_ge(S(f"gathered{slot}"), 16 * GT * (turn + 1))

        def one_hots(tile, k, weighted, last):
            for j in range(GT):
                if weighted:
                    m = ve.tensor_scalar(tile[:, j, :], iota_row[:, :], LOCAL[:, bass.ds(k + j, 1)],
                                         WEIGHT[:, bass.ds(k + j, 1)], ALU.is_equal, ALU.mult)
                else:
                    m = ve.tensor_scalar(tile[:, j, :], iota_row[:, :], LOCAL[:, bass.ds(k + j, 1)], None,
                                         ALU.is_equal)
            m.then_inc(last, 1)

        def add_up(acc, sums, q, group, width, done):
            blocks = blocks_of(DVE, group)
            for j in range(GT):
                wait(ve, done, q * GT + j)
                at = acc[:, bass.ds(blocks[j], 1), :].rearrange("p a d -> p (a d)")
                ve.tensor_tensor(at, at, sums[:, j, 0:width], ALU.add).then_inc(done, 1)

        def gcn_pass(acc):
            with ExitStack() as ps:
                sums = [psum(ps, f"sums{i}", [P, GT, P]) for i in range(2)]
                copy_index, gather = gather_pieces(table, D)

                def hots(q, slot, turn):
                    wait(ve, S("g_free"), q - 1)
                    one_hots(OH[:, slot % 2], q * GT, True, S("hot"))

                def products(q, slot, turn):
                    pe.wait_ge(S("hot"), q + 1)
                    gathered(pe, slot, turn)
                    wait(pe, S("added"), (q - 1) * GT)
                    for j in range(GT):
                        m = pe.matmul(sums[slot % 2][:, j, :], OH[:, slot % 2, j, :], G[:, slot, j, 0:D],
                                      start=True, stop=True)
                    m.then_inc(S("g_free"), 1)

                def add(q, slot, turn):
                    ve.wait_ge(S("g_free"), q + 1)
                    add_up(acc, sums[slot % 2], q, q, D, S("added"))

                pipeline(nc, [(copy_index, 0), (gather, 0), (hots, 0), (products, 0), (add, 1)])
                ve.wait_ge(S("added"), GROUPS * GT)
            S.end_stage()

        def pair_pass(acc):
            EA = BUF[2][:, 0:2 * GT, :].rearrange("p (r t) d -> p r t d", r=2)
            BA = BUF[2][:, 2 * GT:4 * GT, :].rearrange("p (r t) d -> p r t d", r=2)
            EAT = BUF[2][:, 4 * GT:6 * GT, :].rearrange("p (r t) d -> p r t d", r=2)
            V = BUF[2][:, 6 * GT:8 * GT, :].rearrange("p (r t) d -> p r t d", r=2)
            unsorted = nc.values_load(FLAG[0:1, 0:1], engines=(SP,), min_val=0, max_val=1,
                                      skip_runtime_bounds_check_because="it is a minimum with 1")
            with ExitStack() as ps:
                turned = [psum(ps, f"turned{i}", [P, GT, P]) for i in range(2)]
                pre = [psum(ps, f"pre{i}", [P, GT, P]) for i in range(2)]
                sums = [psum(ps, f"sums{i}", [P, GT, P]) for i in range(2)]
                copy_index, gather = gather_pieces(table, D)

                def fetch(q, slot, turn):
                    at = nc.values_load_multi_w_load_instructions(
                        START[0:1, bass.ds(q * GT, GT)], engines=(SP,), min_val=0, max_val=E,
                        skip_runtime_bounds_check_because="a tile's first edge is a minimum with E")[1]
                    h = slot % 2
                    wait(sp, S("attr_free"), q - 1)
                    wait(sp, S("based"), q - 1)
                    settle(sp, "sync")

                    def rows(attr, base):
                        for j in range(GT):
                            sp.dma_start(EA[:, h, j, :], attr[bass.ds(at[j], P), :]).then_inc(S(f"attr{h}"), 16)
                            sp.dma_start(BA[:, h, j, :], base[bass.ds(at[j], P), :]).then_inc(S(f"base{h}"), 16)

                    with sp.If(unsorted == 1):
                        rows(attr_s, base_s)
                    with sp.Else():
                        rows(A["edge_attr_128"], A["edge_attr_128_n2"])

                def half_count(q, slot, turn):
                    return turn * (RING // 2) + slot // 2 + 1

                def turn_attr(q, slot, turn):
                    h = slot % 2
                    pe.wait_ge(S(f"attr{h}"), 16 * GT * half_count(q, slot, turn))
                    wait(pe, S("attr_copied"), q - 1)
                    for j in range(GT):
                        m = pe.transpose(turned[h][:, j, :], EA[:, h, j, :], ident[:, :])
                    m.then_inc(S("attr_free"), 1)

                def copy_attr(q, slot, turn):
                    h = slot % 2
                    ac.wait_ge(S("attr_free"), q + 1)
                    wait(ac, S("pre_done"), q - 1)
                    ac.activation(EAT[:, h], turned[h][:, :, :], ACT.Copy).then_inc(S("attr_copied"), 1)

                def times_w(q, slot, turn):
                    h = slot % 2
                    pe.wait_ge(S("attr_copied"), q + 1)
                    wait(pe, S("summed"), q - 1)
                    for j in range(GT):
                        m = pe.matmul(pre[h][:, j, :], EAT[:, h, j, :], wmat[:, :], start=True, stop=True)
                    m.then_inc(S("pre_done"), 1)

                def sum_up(q, slot, turn):
                    h = slot % 2
                    ve.wait_ge(S("pre_done"), q + 1)
                    gathered(ve, slot, turn)
                    wait(ve, S("v_free"), q - 1)
                    ve.tensor_tensor(V[:, h], pre[h][:, :, :], G[:, slot, :, 0:D], ALU.add).then_inc(S("summed"), 1)

                def gelu(q, slot, turn):
                    ac.wait_ge(S("summed"), q + 1)
                    ac.activation(V[:, slot % 2], V[:, slot % 2], ACT.Gelu).then_inc(S("gelu"), 1)

                def times_base(q, slot, turn):
                    h = slot % 2
                    ve.wait_ge(S("gelu"), q + 1)
                    ve.wait_ge(S(f"base{h}"), 16 * GT * half_count(q, slot, turn))
                    ve.tensor_tensor(V[:, h], V[:, h], BA[:, h], ALU.mult).then_inc(S("based"), 1)

                def hots(q, slot, turn):
                    wait(ve, S("v_free"), q - 1)
                    one_hots(OH[:, slot % 2], q * GT, False, S("hot"))

                def products(q, slot, turn):
                    h = slot % 2
                    pe.wait_ge(S("hot"), q + 1)
                    pe.wait_ge(S("based"), q + 1)
                    wait(pe, S("added"), (q - 1) * GT)
                    for j in range(GT):
                        m = pe.matmul(sums[h][:, j, :], OH[:, h, j, :], V[:, h, j, :], start=True, stop=True)
                    m.then_inc(S("v_free"), 1)

                def add(q, slot, turn):
                    ve.wait_ge(S("v_free"), q + 1)
                    add_up(acc, sums[slot % 2], q, q, D, S("added"))

                def gather_when_read(q, slot, turn):
                    po.wait_ge(S("indexed"), q + 1)
                    wait(po, S("summed"), q - RING + 1)
                    settle(po, "pool")
                    for j in range(GT):
                        po.indirect_dma_start(G[:, slot, j, 0:D], None, table,
                                              bass.IndirectOffsetOnAxis(ap=IDX[:, slot, j:j + 1], axis=0)
                                              ).then_inc(S(f"gathered{slot}"), 16)

                pipeline(nc, [(copy_index, 0), (gather_when_read, 0), (fetch, 0), (turn_attr, 0), (copy_attr, 0),
                              (times_w, 0), (hots, 0), (sum_up, 0), (gelu, 0), (times_base, 1), (products, 1),
                              (add, 2)])
                ve.wait_ge(S("added"), GROUPS * GT)
            S.end_stage()

        def gat_logits(tab, XR, H, C):
            W = H * C
            Z = BUF[2][:, 0:2 * GT, 0:W].rearrange("p (r t) d -> p r t d", r=2)
            OHT = BUF[2][:, 2 * GT:4 * GT, :].rearrange("p (r t) d -> p r t d", r=2)
            RM = BUF[2][0:H, 4 * GT:6 * GT, :].rearrange("p (r t) d -> p r (t d)", r=2)
            PEN = BUF[2][0:H, 6 * GT:8 * GT, :].rearrange("p (r t) d -> p r (t d)", r=2)
            att_g = att[:, 0:W].unsqueeze(1).broadcast_to([P, GT, W])
            ve.memset(RM[:, 1, GT * P - 1:GT * P], -BIG).then_inc(S("ready"), 1)
            with ExitStack() as ps:
                turned = [psum(ps, f"turned{i}", [P, GT, P]) for i in range(2)]
                picked = [psum(ps, f"picked{i}", [P, GT, P]) for i in range(2)]
                lrow = [psum(ps, f"lrow{i}", [H1, GT * P]) for i in range(2)]
                copy_index, _ = gather_pieces(tab, W)

                def gather(q, slot, turn):
                    po.wait_ge(S("indexed"), q + 1)
                    wait(po, S(f"kept{slot}"), 16 * turn)
                    settle(po, "pool")
                    for j in range(GT):
                        po.indirect_dma_start(G[:, slot, j, 0:W], None, tab,
                                              bass.IndirectOffsetOnAxis(ap=IDX[:, slot, j:j + 1], axis=0)
                                              ).then_inc(S(f"gathered{slot}"), 16)

                def hots(q, slot, turn):
                    wait(ve, S("turned"), q - 1)
                    one_hots(OH[:, slot % 2], q * GT, False, S("hot"))

                def turn_hots(q, slot, turn):
                    pe.wait_ge(S("hot"), q + 1)
                    wait(pe, S("oht"), q - 1)
                    for j in range(GT):
                        m = pe.transpose(turned[slot % 2][:, j, :], OH[:, slot % 2, j, :], ident[:, :])
                    m.then_inc(S("turned"), 1)

                def copy_hots(q, slot, turn):
                    ac.wait_ge(S("turned"), q + 1)
                    wait(ac, S("picked"), q - 1)
                    ac.activation(OHT[:, slot % 2], turned[slot % 2][:, :, :], ACT.Copy).then_inc(S("oht"), 1)

                def pick(q, slot, turn):
                    pe.wait_ge(S("oht"), q + 1)
                    wait(pe, S("z"), q - 1)
                    blocks = blocks_of(PE, q)
                    for j in range(GT):
                        m = pe.matmul(picked[slot % 2][:, j, 0:W], OHT[:, slot % 2, j, :],
                                      XR[:, bass.ds(blocks[j], 1), 0:W].rearrange("p a d -> p (a d)"),
                                      start=True, stop=True)
                    m.then_inc(S("picked"), 1)

                def logits(q, slot, turn):
                    z = Z[:, slot % 2]
                    ve.wait_ge(S("picked"), q + 1)
                    gathered(ve, slot, turn)
                    wait(ve, S("logit"), q - 1)
                    ve.tensor_tensor(z, picked[slot % 2][:, :, 0:W], G[:, slot, :, 0:W], ALU.add).then_inc(S("z"), 1)
                    ve.wait_ge(S("z"), q + 1)
                    ve.scalar_tensor_tensor(z, z, SLOPE, z, ALU.mult, ALU.max).then_inc(S("leaky"), 1)
                    ve.wait_ge(S("leaky"), q + 1)
                    ve.tensor_tensor(z, z, att_g, ALU.mult).then_inc(S("weighed"), 1)
                    ve.wait_ge(S("weighed"), q + 1)
                    ve.tensor_reduce(G[:, slot, :, W:W + H], z.rearrange("p t (h c) -> p t h c", h=H), AX_X,
                                     ALU.add).then_inc(S("logit"), 1)

                def turn_logits(q, slot, turn):
                    pe.wait_ge(S("logit"), q + 1)
                    wait(pe, S("ran"), q - 1)
                    for j in range(GT):
                        m = pe.transpose(lrow[slot % 2][0:H, j * P:(j + 1) * P], G[:, slot, j, W:W + H], ident[:, :])
                    m.then_inc(S("lrow"), 1)

                def fetch_pen(q, slot, turn):
                    wait(sp, S("ran"), q - 1)
                    settle(sp, "sync")
                    sp.dma_start(PEN[:, slot % 2], open_d[bass.ds(q * GT * P, GT * P)].rearrange("(a n) -> a n", a=1)
                                 .broadcast_to([H, GT * P])).then_inc(S(f"pen{slot % 2}"), 16)

                def run_max(q, slot, turn):
                    h = slot % 2
                    ve.wait_ge(S("lrow"), q + 1)
                    ve.wait_ge(S(f"pen{h}"), 16 * (turn * (RING // 2) + slot // 2 + 1))
                    wait(ve, S(f"stored{h}"), 16 * (turn * (RING // 2) + slot // 2))
                    wait(ve, S("ran"), q)
                    if isinstance(q, int) and q == 0:
                        ve.wait_ge(S("ready"), 1)
                    ve.tensor_tensor_scan(RM[:, h], PEN[:, h], lrow[h][0:H, :], RM[:, 1 - h, GT * P - 1:GT * P],
                                          ALU.add, ALU.max).then_inc(S("ran"), 1)

                def keep(q, slot, turn):
                    sp.wait_ge(S("lrow"), q + 1)
                    settle(sp, "sync")
                    sp.dma_start(kept_d[bass.ds(q, 1), :, 0:GT * (W + H)].rearrange("a p (t d) -> p (a t) d", t=GT),
                                 G[:, slot, :, 0:W + H]).then_inc(S(f"kept{slot}"), 16)
                    sp.wait_ge(S("ran"), q + 1)
                    settle(sp, "sync")
                    sp.dma_start(runmax_d[0:H, bass.ds(q * GT * P, GT * P)], RM[:, slot % 2]
                                 ).then_inc(S(f"stored{slot % 2}"), 16)

                pipeline(nc, [(copy_index, 0), (gather, 0), (fetch_pen, 0), (logits, 2), (hots, 0), (turn_logits, 2),
                              (turn_hots, 0), (copy_hots, 0), (pick, 0), (run_max, 2), (keep, 2)])
                for s in range(RING):
                    sp.wait_ge(S(f"kept{s}"), 16 * (GROUPS // RING))
                for s in range(2):
                    sp.wait_ge(S(f"stored{s}"), 16 * (GROUPS // 2))
            S.end_stage()

        def gat_sums(acc, H, C):
            W = H * C
            WA = W + 2 * H + 2
            RHS = BUF[2][:, :, :].rearrange("p b d -> p (b d)")[:, 0:2 * GT * WA].rearrange(
                "p (r t w) -> p r t w", r=2, t=GT)
            at = -(-2 * GT * WA // P)
            MX = BUF[2][0:H, at:at + 2 * GT, :].rearrange("p (r t) d -> p r (t d)", r=2)
            RM = BUF[2][0:H, at + 2 * GT:at + 4 * GT, :].rearrange("p (r t) d -> p r (t d)", r=2)
            PEN = BUF[2][0:H, at + 4 * GT:at + 6 * GT, :].rearrange("p (r t) d -> p r (t d)", r=2)
            DIF = BUF[2][:, at + 6 * GT:at + 6 * GT + 2, 0:GT * H].rearrange("p r (t h) -> p r t h", h=H)
            ve.memset(MX[:, 1, 0:1], -BIG).then_inc(S("ready"), 1)
            with ExitStack() as ps:
                mcol = [psum(ps, f"mcol{i}", [P, GT, P]) for i in range(2)]
                sums = [psum(ps, f"asum{i}", [P, GT, 2 * P]) for i in range(2)]

                def back(q):
                    return q * (-1) + (GROUPS - 1)

                def fetch(q, slot, turn):
                    g = back(q)
                    wait(sp, S("rows"), q - RING + 1)
                    settle(sp, "sync")
                    sp.dma_start(G[:, slot, :, 0:W + H], kept_d[bass.ds(g, 1), :, 0:GT * (W + H)]
                                 .rearrange("a p (t d) -> p (a t) d", t=GT)).then_inc(S(f"got{slot}"), 16)
                    h = slot % 2
                    wait(sp, S("max"), q - 1)
                    settle(sp, "sync")
                    sp.dma_start(RM[:, h], runmax_d[0:H, bass.ds(g * (GT * P), GT * P)]).then_inc(S(f"run{h}"), 16)
                    sp.dma_start(PEN[:, h], close_d[bass.ds(g * (GT * P), GT * P)].rearrange("(a n) -> a n", a=1)
                                 .broadcast_to([H, GT * P])).then_inc(S(f"run{h}"), 16)

                def back_max(q, slot, turn):
                    h = slot % 2
                    ve.wait_ge(S(f"run{h}"), 32 * (turn * (RING // 2) + slot // 2 + 1))
                    wait(ve, S("mcol"), q - 1)
                    wait(ve, S("max"), q)
                    if isinstance(q, int) and q == 0:
                        ve.wait_ge(S("ready"), 1)
                    ve.tensor_tensor_scan(MX[:, h, ::-1], PEN[:, h, ::-1], RM[:, h, ::-1], MX[:, 1 - h, 0:1],
                                          ALU.add, ALU.max).then_inc(S("max"), 1)

                def turn_max(q, slot, turn):
                    pe.wait_ge(S("max"), q + 1)
                    wait(pe, S("mfirst"), q - 1)
                    for j in range(GT):
                        m = pe.matmul(mcol[slot % 2][:, j, 0:H], MX[:, slot % 2, j * P:(j + 1) * P], ident[0:H, 0:H],
                                      start=True, stop=True)
                    m.then_inc(S("mcol"), 1)

                def hots(q, slot, turn):
                    wait(ve, S("summed"), q - 1)
                    one_hots(OH[:, slot % 2], back(q) * GT, False, S("hot"))

                def less_max(q, slot, turn):
                    h = slot % 2
                    k = back(q) * GT
                    ve.wait_ge(S("mcol"), q + 1)
                    ve.wait_ge(S(f"got{slot}"), 16 * (turn + 1))
                    wait(ve, S("exp"), q - 1)
                    wait(ve, S("summed"), q - 1)
                    ve.tensor_tensor(DIF[:, h], G[:, slot, :, W:W + H], mcol[h][:, :, 0:H], ALU.subtract
                                     ).then_inc(S("dif"), 1)
                    ve.tensor_tensor(RHS[:, h, :, W + H:W + 2 * H], mcol[h][:, :, 0:H],
                                     NEWSEG[:, bass.ds(k, GT)].unsqueeze(2).broadcast_to([P, GT, H]), ALU.mult
                                     ).then_inc(S("mfirst"), 1)

                def exps(q, slot, turn):
                    h = slot % 2
                    k = back(q) * GT
                    ac.wait_ge(S("dif"), q + 1)
                    ac.activation(RHS[:, h, :, W:W + H], DIF[:, h], ACT.Exp).then_inc(S("exp"), 1)
                    ac.activation(RHS[:, h, :, W + 2 * H], NEWSEG[:, bass.ds(k, GT)], ACT.Copy).then_inc(S("extra"), 1)
                    ac.activation(RHS[:, h, :, W + 2 * H + 1], WEIGHT[:, bass.ds(k, GT)], ACT.Copy
                                  ).then_inc(S("extra"), 1)

                def rows(q, slot, turn):
                    h = slot % 2
                    ve.wait_ge(S("exp"), q + 1)
                    for j in range(GT):
                        m = ve.tensor_tensor(
                            RHS[:, h, j, 0:W].rearrange("p (h c) -> p h c", h=H),
                            G[:, slot, j, 0:W].rearrange("p (h c) -> p h c", h=H),
                            RHS[:, h, j, W:W + H].unsqueeze(2).broadcast_to([P, H, C]), ALU.mult)
                    m.then_inc(S("rows"), 1)

                def products(q, slot, turn):
                    h = slot % 2
                    pe.wait_ge(S("hot"), q + 1)
                    pe.wait_ge(S("rows"), q + 1)
                    pe.wait_ge(S("mfirst"), q + 1)
                    pe.wait_ge(S("extra"), 2 * (q + 1))
                    wait(pe, S("added"), (q - 1) * GT)
                    for j in range(GT):
                        m = pe.matmul(sums[h][:, j, 0:WA], OH[:, h, j, :], RHS[:, h, j, :], start=True, stop=True)
                    m.then_inc(S("summed"), 1)

                def add(q, slot, turn):
                    ve.wait_ge(S("summed"), q + 1)
                    add_up(acc, sums[slot % 2], q, back(q), WA, S("added"))

                pipeline(nc, [(fetch, 0), (less_max, 1), (exps, 1), (back_max, 0), (turn_max, 0), (hots, 1), (rows, 1),
                              (products, 1), (add, 2)])
                ve.wait_ge(S("added"), GROUPS * GT)
            S.end_stage()

        def gat_layer(src, name, H, C, K, tab, XL, XR, dst):
            W = H * C
            WA = W + 2 * H + 2
            dense(src, A[f"L0_gnn_Wr{name}"], XR, K, W, A[f"L0_gnn_br{name}"])
            dense(src, A[f"L0_gnn_Wl{name}"], XL, K, W, A[f"L0_gnn_bl{name}"])
            store_table(tab, XL)
            load(att[:, 0:W], spread(A[f"L0_gnn_att{name}"].rearrange("h c -> (h c)"), W))
            acc = ACC[:, 0:NB * WA].rearrange("p (b w) -> p b w", b=NB)
            go(ve, lambda: ve.memset(ACC[:, :], 0.0))
            end()
            gat_logits(tab, XR, H, C)
            gat_sums(acc, H, C)
            begin()
            self_l, m_e, m_all, c_e, c_s = (st[i][:, 0:NB * H].rearrange("p (b h) -> p b h", h=H) for i in range(5))
            Zn = BUF[2][:, :, 0:W]
            go(ve, lambda: ve.tensor_tensor(Zn, XL, XR, ALU.add))
            go(ve, lambda: ve.scalar_tensor_tensor(Zn, Zn, SLOPE, Zn, ALU.mult, ALU.max))
            go(ve, lambda: ve.tensor_tensor(Zn, Zn, wide(att[:, 0:W]), ALU.mult))
            go(ve, lambda: ve.tensor_reduce(self_l, Zn.rearrange("p b (h c) -> p b h c", h=H), AX_X, ALU.add))
            has = acc[:, :, W + 2 * H].unsqueeze(2).broadcast_to([P, NB, H])
            go(ve, lambda: ve.tensor_scalar(m_all, has, -1.0, BIG, ALU.add, ALU.mult))
            go(ve, lambda: ve.tensor_tensor(m_e, acc[:, :, W + H:W + 2 * H], m_all, ALU.add))
            go(ve, lambda: ve.tensor_tensor(m_all, m_e, self_l, ALU.max))
            go(ve, lambda: ve.tensor_tensor(c_e, m_e, m_all, ALU.subtract))
            go(ve, lambda: ve.tensor_tensor(c_s, self_l, m_all, ALU.subtract))
            go(ac, lambda: ac.activation(c_e, c_e, ACT.Exp))
            go(ac, lambda: ac.activation(c_s, c_s, ACT.Exp))
            den = m_e
            go(ve, lambda: ve.tensor_tensor(den, acc[:, :, W:W + H], c_e, ALU.mult))
            go(ve, lambda: ve.tensor_tensor(den, den, c_s, ALU.add))
            go(ve, lambda: ve.reciprocal(den, den))
            go(ve, lambda: ve.tensor_tensor(c_e, c_e, den, ALU.mult))
            go(ve, lambda: ve.tensor_tensor(c_s, c_s, den, ALU.mult))

            def heads(a):
                return a.rearrange("p b (h c) -> p b h c", h=H)

            def each(c):
                return c.unsqueeze(3).broadcast_to([P, NB, H, C])

            go(ve, lambda: ve.tensor_tensor(heads(Zn), heads(acc[:, :, 0:W]), each(c_e), ALU.mult))
            go(ve, lambda: ve.tensor_tensor(heads(dst), heads(XL), each(c_s), ALU.mult))
            go(ve, lambda: ve.tensor_tensor(dst, dst, Zn, ALU.add))
            load(bias[:, 0:W], spread(A[f"L0_gnn_bias{name}"], W))
            go(ve, lambda: ve.tensor_tensor(dst, dst, wide(bias[:, 0:W]), ALU.add))
            elu(dst, Zn)
            return acc[:, :, W + 2 * H + 1]

        def batch_norm_gelu(a, tmp, gamma, beta):
            load(gain[:, :], spread(gamma, D))
            load(bias[:, :], spread(beta, D))
            mean = att[:, :]

            def column_means(src):
                with ExitStack() as ps:
                    tot = psum(ps, "tot", [P, P])
                    lap = S("lap")
                    pe.wait_ge(chain[0].sem, chain[0].n)
                    pe.matmul(tot[:, :], ones[:, :], src[:, 0, :], start=True, stop=False)
                    with pe.Fori(1, NB - 1) as b:
                        pe.matmul(tot[:, :], ones[:, :], src[:, b, :], start=False, stop=False)
                    go(pe, lambda: pe.matmul(tot[:, :], real[:, :], src[:, NB - 1, :], start=False, stop=True))
                    go(ve, lambda: ve.tensor_scalar(mean, tot[:, :], 1.0 / N, None, ALU.mult))

            column_means(a)
            go(ve, lambda: ve.tensor_tensor(a, a, wide(mean), ALU.subtract))
            go(ve, lambda: ve.tensor_tensor(tmp, a, a, ALU.mult))
            column_means(tmp)
            go(ve, lambda: ve.tensor_scalar(mean, mean, EPS, None, ALU.add))
            inv_sqrt(mean, mean)
            go(ve, lambda: ve.tensor_tensor(mean, mean, gain[:, :], ALU.mult))
            go(ve, lambda: ve.tensor_tensor(a, a, wide(mean), ALU.mult))
            go(ve, lambda: ve.tensor_tensor(a, a, wide(bias[:, :]), ALU.add))
            go(ac, lambda: ac.activation(a, a, ACT.Gelu))

        def node_view(t):
            return t[:, :, :]

        Xn, B0, B1, B2 = node_view(X), node_view(BUF[0]), node_view(BUF[1]), node_view(BUF[2])
        accn = ACC[:, 0:NB * D].rearrange("p (b d) -> p b d", b=NB)

        def gcn(src, weight, tmp, scale, bias_of):
            dense(src, weight, tmp)
            go(ve, lambda: ve.tensor_tensor(tmp, tmp, tall(scale), ALU.mult))
            store_table(table, tmp)
            go(ve, lambda: ve.tensor_copy(accn, tmp))
            end()
            gcn_pass(accn)
            begin()
            load(bias[:, :], spread(bias_of, D))
            go(ve, lambda: ve.tensor_tensor(accn, accn, tall(scale), ALU.mult))
            go(ve, lambda: ve.tensor_tensor(accn, accn, wide(bias[:, :]), ALU.add))

        constants()
        sort_edges()
        tile_tables()
        begin()
        load(Xn, A["x"].rearrange("(b p) d -> p b d", p=P))

        norm(Xn, B0)
        relu(B0)
        gat_layer(B0, "1", H1, C1, D, table, B0, B1, B0)
        deg, mask = st[0][:, 0:NB], st[1][:, 0:NB]
        WA = D + 2 * H1 + 2
        wsum = ACC[:, 0:NB * WA].rearrange("p (b w) -> p b w", b=NB)[:, :, WA - 1]
        go(ve, lambda: ve.tensor_scalar(deg, wsum, 1.0, None, ALU.add))
        inv_sqrt(dinv[:, :], deg)
        go(ve, lambda: ve.tensor_scalar(mask, deg, 0.0, None, ALU.is_gt))
        go(ve, lambda: ve.tensor_tensor(deg, deg, mask, ALU.mult))
        go(ve, lambda: ve.scalar_tensor_tensor(deg, mask, -1.0, deg, ALU.mult, ALU.add))
        go(ve, lambda: ve.tensor_scalar(deg, deg, 1.0, None, ALU.add))
        inv_sqrt(deg, deg)
        go(ve, lambda: ve.tensor_tensor(dinv_guarded[:, :], deg, mask, ALU.mult))
        gat_layer(B0, "2", 1, C2, D, table2, B0[:, :, 0:C2], B1[:, :, 0:C2], B0[:, :, 0:C2])
        dense(B0[:, :, 0:C2], A["L0_gnn_Wlin"], B1, C2, D, A["L0_gnn_blin"])
        elu(B1, B2)
        go(ve, lambda: ve.tensor_tensor(Xn, Xn, B1, ALU.add))

        norm(Xn, B0)
        relu(B0)
        gcn(B0, A["L1_gnn_W"], B1, dinv_guarded[:, :], A["L1_gnn_b"])
        go(ve, lambda: ve.tensor_copy(B0, accn))
        norm(B0, B1)
        load(gain[:, :], spread(A["L1_gnn_ln_gamma"], D))
        load(bias[:, :], spread(A["L1_gnn_ln_beta"], D))
        go(ve, lambda: ve.tensor_tensor(B1, B1, wide(gain[:, :]), ALU.mult))
        go(ve, lambda: ve.tensor_tensor(B1, B1, wide(bias[:, :]), ALU.add))
        go(ve, lambda: ve.tensor_tensor(Xn, Xn, B1, ALU.add))

        norm(Xn, B0)
        relu(B0)
        dense(B0, A["L2_gnn_W1"], B1, D, D, A["L2_gnn_b1"])
        store_table(table, B1)
        go(ve, lambda: ve.memset(ACC[:, :], 0.0))
        end()
        pair_pass(accn)
        begin()
        dense(accn, A["L2_gnn_W2"], B0, D, D, A["L2_gnn_b2"])
        batch_norm_gelu(B0, B1, A["L2_gnn_g1"], A["L2_gnn_be1"])
        dense(B0, A["L2_gnn_W3"], B1, D, D, A["L2_gnn_b3"])
        batch_norm_gelu(B1, B0, A["L2_gnn_g2"], A["L2_gnn_be2"])
        go(ve, lambda: ve.tensor_tensor(Xn, Xn, B1, ALU.add))

        norm(Xn, B0)
        relu(B0)
        dense(B0, A["L3_gnn_W_init"], B2)
        for n in "123":
            gcn(B2 if n == "1" else B0, A["L3_gnn_W" + n], B1, dinv[:, :], A["L3_gnn_b" + n])
            go(ve, lambda: ve.tensor_tensor(B0, accn, B2, ALU.add))
            if n != "3":
                relu(B0)
        go(ve, lambda: ve.tensor_tensor(Xn, Xn, B0, ALU.add))
        full = (NB - 1) * P
        load(out[0:full, :].rearrange("(b p) d -> p b d", p=P), X[:, 0:NB - 1, :])
        load(out[full:N, :], X[0:LAST, NB - 1, :])
        end()


NODES = ["x"]
EDGES = {"src": (0, TAIL, 0), "dst": (FRONT, TAIL, NPAD), "edge_weight": (0, TAIL, 0),
         "edge_attr_128": (0, P, 0), "edge_attr_128_n2": (0, P, 0)}
TURNED = ["L2_gnn_W1", "L2_gnn_W2", "L2_gnn_W3"]


def kernel(**inputs):
    import concourse.bacc as bacc
    from concourse.bass_utils import run_bass_kernel_spmd

    nc = bacc.Bacc("TRN2", target_bir_lowering=False, num_devices=1)
    arrays, args = {}, {}
    for name, value in inputs.items():
        a = np.asarray(value)
        if name in TURNED:
            a = a.T
        if name in NODES:
            a = np.pad(a, ((0, NPAD - N), (0, 0)))
        if name in EDGES:
            front, tail, fill = EDGES[name]
            a = np.pad(a, ((front, tail),) + ((0, 0),) * (a.ndim - 1), constant_values=fill)
        a = np.ascontiguousarray(a)
        arrays["in_" + name] = a
        args[name] = nc.dram_tensor("in_" + name, a.shape, mybir.dt.from_np(a.dtype), kind="ExternalInput").ap()
    out = nc.dram_tensor("out", (N, D), F32, kind="ExternalOutput").ap()
    gnn(nc, args, out)
    return run_bass_kernel_spmd(nc, [arrays], core_ids=[0]).results[0]["out"]
```

```python
from contextlib import ExitStack

import numpy as np

import concourse.bass as bass
from concourse import mybir

ALU = mybir.AluOpType
ACT = mybir.ActivationFunctionType
F32 = mybir.dt.float32
I32 = mybir.dt.int32
BF16 = mybir.dt.bfloat16
AX_X = mybir.AxisListType.X
DVE = mybir.EngineType.DVE
PE = mybir.EngineType.PE
SP = mybir.EngineType.SP

P = 128
N, D, E = 6250, 128, 106250
NB = -(-N // P)
NPAD = NB * P
LAST = N - (NB - 1) * P
FRONT = P
TAIL = 2 * P
GT = 4
RING = 4
SORT_T = -(-E // P)
TILES = -(-((E + NB * (P - 1)) // P) // (GT * RING)) * GT * RING
GROUPS = TILES // GT
TCOL = -(-TILES // P)
TTAB = TCOL * P
BIG = 1e30
EPS = 1e-5
H1, C1, C2 = 8, 16, 64
SLOPE = 0.2
NCH = 7
WMAX = D + 2 * H1 + 2
EP, EC = 125, E // 125


class Sems:

    SOFT = ("gathered", "windows", "scattered")

    def __init__(self, nc, most=32):
        self.nc, self.names = nc, {}
        self.pool = [nc.alloc_semaphore(f"pool{i}") for i in range(most)]
        self.ids = range(self.pool[0].num, self.pool[0].num + most)
        assert [s.num for s in self.pool] == list(self.ids)
        self.free = list(self.pool)

    def __call__(self, name):
        if name not in self.names:
            soft = name.startswith(self.SOFT)
            self.names[name] = self.nc.alloc_semaphore(f"{name}_{self.nc.next_id()}") if soft else self.free.pop(0)
        return self.names[name]

    def end_stage(self):
        self.nc.all_engine_barrier(sems_to_clear=self.ids)
        self.names, self.free = {}, list(self.pool)


class Chain:

    def __init__(self, sem, base=0, settle=None):
        self.sem, self.n, self.settle = sem, base, settle

    def run(self, eng, ins_of, by=1):
        wait(eng, self.sem, self.n)
        if self.settle:
            self.settle(eng)
        ins_of().then_inc(self.sem, by)
        self.n = self.n + by


def wait(eng, sem, value):
    if not (isinstance(value, int) and value <= 0):
        eng.wait_ge(sem, value)


def pipeline(nc, pieces):
    most = max(late for _, late in pieces)
    first = -(-(most + RING) // RING) * RING

    def step(turn, u):
        for piece, late in pieces:
            slot = (u - late) % RING
            own = turn + (u - late - slot) // RING
            q = own * RING + slot
            if isinstance(q, int) and not 0 <= q < GROUPS:
                continue
            piece(q, slot, own)

    for t in range(first):
        step(t // RING, t % RING)
    with nc.Fori(first // RING, GROUPS // RING) as turn:
        for u in range(RING):
            step(turn, u)
    for t in range(GROUPS, GROUPS + most):
        step(t // RING, t % RING)


def gnn(nc, A, out):
    S = Sems(nc)
    ve, ac, pe, po, sp = nc.vector, nc.scalar, nc.tensor, nc.gpsimd, nc.sync
    with ExitStack() as ctx:
        def sb(name, shape, dt=F32):
            return ctx.enter_context(nc.sbuf_tensor(name, shape, dt))

        def dram(name, shape, dt=F32):
            return nc.dram_tensor(name, shape, dt).ap()

        ident = sb("ident", [P, P])
        iota_row = sb("iota_row", [P, P])
        iota_col = sb("iota_col", [P, 1])
        ones = sb("ones", [P, P])
        real = sb("real", [P, P])
        before = sb("before", [P, P])
        X = sb("X", [P, NB, D])
        BUF = [sb(f"BUF{i}", [P, NB, D]) for i in range(3)]
        ACC = sb("ACC", [P, NB * WMAX])
        LOCAL = sb("LOCAL", [P, TTAB])
        NEWSEG = sb("NEWSEG", [P, TTAB])
        WEIGHT = sb("WEIGHT", [P, TTAB])
        SRC = sb("SRC", [P, TTAB], I32)
        BLOCK = sb("BLOCK", [1, TTAB], I32)
        START = sb("START", [1, TTAB], I32)
        FLAG = sb("FLAG", [1, 4], I32)
        G = sb("G", [P, RING, GT, D + H1])
        IDX = sb("IDX", [P, RING, GT], I32)
        OH = sb("OH", [P, 2, GT, P])
        st = [sb(f"st{i}", [P, NB * H1]) for i in range(5)]
        dinv_guarded = sb("dinv_guarded", [P, NB])
        dinv = sb("dinv", [P, NB])
        bias = sb("bias", [P, D])
        gain = sb("gain", [P, D])
        att = sb("att", [P, D])
        wmat = sb("wmat", [P, D])

        src_s = dram("src_sorted", [E + TAIL], I32)
        dst_s = dram("dst_sorted", [FRONT + E + TAIL], I32)
        w_s = dram("w_sorted", [E + TAIL])
        pair_s = dram("pair_sorted", [E + P, 2 * D])
        table = dram("table", [NPAD, D])
        table2 = dram("table2", [NPAD, C2])
        open_d = dram("open_pen", [TTAB * P], BF16)
        close_d = dram("close_pen", [TTAB * P], BF16)
        kept_d = dram("kept", [GROUPS, P, GT * (D + H1)])
        head_d = dram("heads", [H1 * TILES * P])

        named = [0]

        def psum(stack, name, shape):
            named[0] += 1
            return stack.enter_context(nc.psum_tensor(f"{name}_{named[0]}", shape, F32))

        chain = [None]

        def begin():
            chain[0] = Chain(S("chain"))

        def go(eng, f, by=1):
            chain[0].run(eng, f, by=by)

        def load(dst, src):
            go(sp, lambda: sp.dma_start(dst, src), by=16)

        def load_all(pairs):
            sp.wait_ge(chain[0].sem, chain[0].n)
            for dst, src in pairs:
                sp.dma_start(dst, src).then_inc(chain[0].sem, 16)
            chain[0].n += 16 * len(pairs)

        def end():
            sp.wait_ge(chain[0].sem, chain[0].n)
            S.end_stage()

        def spread(row, width):
            return row.rearrange("(a n) -> a n", a=1).broadcast_to([P, width])

        def settle(eng, name):
            eng.sem_inc(S(f"settled_{name}"), 1)

        def wide(a, n=NB):
            return a.unsqueeze(1).broadcast_to([P, n, a.shape[1]])

        def tall(a, width=D):
            return a.unsqueeze(2).broadcast_to([P, a.shape[1], width])

        def constants():
            begin()
            go(po, lambda: po.iota(SRC[:, 0:P], pattern=[[1, P]], base=0, channel_multiplier=0))
            go(ve, lambda: ve.tensor_copy(iota_row[:, :], SRC[:, 0:P]))
            go(po, lambda: po.iota(SRC[:, 0:1], pattern=[[1, 1]], base=0, channel_multiplier=1))
            go(ve, lambda: ve.tensor_copy(iota_col[:, :], SRC[:, 0:1]))
            go(ve, lambda: ve.memset(ones[:, :], 1.0))
            go(ve, lambda: ve.tensor_scalar(ident[:, :], iota_row[:, :], iota_col[:, 0:1], None, ALU.is_equal))
            go(ve, lambda: ve.tensor_scalar(before[:, :], iota_row[:, :], iota_col[:, 0:1], None, ALU.is_gt))
            go(ve, lambda: ve.tensor_scalar(real[:, :], ones[:, :], iota_col[:, 0:1], float(LAST),
                                            ALU.mult, ALU.is_lt))
            end()

        def sort_edges():
            begin()
            cnt = st[0][:, 0:NB + 1]
            starts = st[1][:, 0:NB + 2]
            thr = st[2][:, 0:NB]
            here = BUF[0][:, :, :].rearrange("p b d -> p (b d)")
            after = BUF[1][:, :, :].rearrange("p b d -> p (b d)")
            junk = BUF[2][:, :, :].rearrange("p b d -> p (b d)")
            here_i = here[0:EP, 2 * EC:3 * EC].bitcast(I32)
            after_i = after[0:EP, 2 * EC:3 * EC].bitcast(I32)
            load(src_s, A["src"])
            load(dst_s, A["dst"])
            load(w_s, A["edge_weight"])
            load(here_i, A["dst"][FRONT:FRONT + E].rearrange("(p c) -> p c", p=EP))
            load(after_i, A["dst"][FRONT + 1:FRONT + 1 + E].rearrange("(p c) -> p c", p=EP))
            go(ve, lambda: ve.tensor_copy(here[0:EP, 0:EC], here_i))
            go(ve, lambda: ve.tensor_copy(after[0:EP, 0:EC], after_i))
            go(ve, lambda: ve.memset(cnt, 0.0))
            go(ve, lambda: ve.tensor_scalar(thr, iota_row[:, 0:NB], float(P), None, ALU.mult))
            go(ve, lambda: ve.tensor_tensor(junk[0:EP, 0:EC], here[0:EP, 0:EC], after[0:EP, 0:EC], ALU.is_gt))
            go(ve, lambda: ve.tensor_reduce(cnt[0:EP, NB:NB + 1], junk[0:EP, 0:EC], AX_X, ALU.add))
            lap = S("count")
            ve.wait_ge(chain[0].sem, chain[0].n)
            ve.tensor_copy(junk[0:EP, 0:1], here[0:EP, 0:1]).then_inc(lap, 1)
            with ve.Fori(0, NB) as t:
                ve.wait_ge(lap, t + 1)
                ve.tensor_scalar(junk[0:EP, 0:EC], here[0:EP, 0:EC], thr[0:EP, bass.ds(t, 1)], 0.0,
                                 ALU.is_lt, ALU.add, accum_out=cnt[0:EP, bass.ds(t, 1)]).then_inc(lap, 1)
            pe.wait_ge(lap, NB + 1)
            with ExitStack() as ps:
                tot = psum(ps, "tot", [P, 64])
                go(pe, lambda: pe.matmul(tot[:, 0:NB + 1], ones[0:EP, :], cnt[0:EP, :], start=True, stop=True))
                go(ve, lambda: ve.tensor_copy(starts[:, 0:NB], tot[:, 0:NB]))
                go(ve, lambda: ve.tensor_scalar(junk[:, 0:1], tot[:, NB:NB + 1], 1.0, None, ALU.min))
            go(ve, lambda: ve.memset(starts[:, NB:NB + 1], float(E)))
            go(ve, lambda: ve.tensor_copy(FLAG[0:1, 0:1], junk[0:1, 0:1]))
            end()
            unsorted = nc.values_load(FLAG[0:1, 0:1], min_val=0, max_val=1,
                                      skip_runtime_bounds_check_because="it is a minimum with 1")
            with nc.If(unsorted == 1):
                counting_sort()
            nc.all_engine_barrier()

        def counting_sort():
            NA = NB + 1
            where = st[3][:, 0:NA]
            small = st[4]
            oh_b, oh_a = BUF[0][:, 0, :], BUF[0][:, 1, 0:NA]
            oh_bT, oh_aT, same = BUF[0][:, 2, :], BUF[0][:, 3, :], BUF[0][:, 4, :]
            pair_t = BUF[0][:, 5:7, :].rearrange("p a d -> p (a d)")
            d_i, b_i, a_i, s_i, pos_i, pos_d = (BUF[0][:, 7, j:j + 1].bitcast(I32) for j in range(6))
            w_t, b_f, a_f, pos = (BUF[0][:, 7, j:j + 1] for j in range(8, 12))
            lap = S("lap")
            scattered = [S(f"scattered{j}") for j in range(4)]

            def digits(k, c):
                c.run(sp, lambda: sp.dma_start(d_i, A["dst"][bass.ds(k * P + FRONT, P)].rearrange("(p a) -> p a", a=1)),
                      by=16)
                c.run(ve, lambda: ve.tensor_scalar(b_i, d_i, P - 1, None, ALU.bitwise_and))
                c.run(ve, lambda: ve.tensor_scalar(a_i, d_i, 7, None, ALU.logical_shift_right))
                c.run(ve, lambda: ve.tensor_copy(b_f, b_i))
                c.run(ve, lambda: ve.tensor_copy(a_f, a_i))
                c.run(ve, lambda: ve.tensor_scalar(oh_b, iota_row[:, :], b_f, None, ALU.is_equal))
                c.run(ve, lambda: ve.tensor_scalar(oh_a, iota_row[:, 0:NA], a_f, None, ALU.is_equal))

            with ExitStack() as ps:
                pa, pb, pc = (psum(ps, f"ps{j}", [P, 512]) for j in range(3))

                def looped(body, steps, start):
                    with nc.Fori(0, SORT_T) as k:
                        c = Chain(lap, k * steps + start, lambda eng: settle(eng, "sync") if eng is sp else None)
                        body(k, c)
                    return start + SORT_T * steps

                c = Chain(lap)
                c.run(ve, lambda: ve.memset(where, 0.0))
                c.run(sp, lambda: sp.dma_start(pair_s[E:E + P, :], A["edge_pair"][E:E + P, :]), by=16)

                def count(k, c):
                    digits(k, c)
                    c.run(pe, lambda: pe.matmul(pa[:, 0:NA], oh_b, oh_a, start=True, stop=True))
                    c.run(ve, lambda: ve.tensor_tensor(where, where, pa[:, 0:NA], ALU.add))

                at = looped(count, 24, c.n)
                c = Chain(lap, at)
                c.run(pe, lambda: pe.matmul(pa[:, 0:NA], ones[:, :], where, start=True, stop=True))
                c.run(ve, lambda: ve.tensor_copy(small[:, 0:NA], pa[:, 0:NA]))
                c.run(ve, lambda: ve.tensor_tensor_scan(small[:, NA:2 * NA], small[:, 0:NA], small[:, 0:NA], 0.0,
                                                        ALU.add, ALU.bypass))
                c.run(pe, lambda: pe.matmul(pb[:, 0:NA], before[:, :], where, start=True, stop=True))
                c.run(ve, lambda: ve.tensor_tensor(small[:, NA:2 * NA], small[:, NA:2 * NA], small[:, 0:NA],
                                                   ALU.subtract))
                c.run(ve, lambda: ve.tensor_tensor(where, small[:, NA:2 * NA], pb[:, 0:NA], ALU.add))

                def place(k, c):
                    digits(k, c)
                    c.run(sp, lambda: sp.dma_start(s_i, A["src"][bass.ds(k * P, P)].rearrange("(p a) -> p a", a=1)),
                          by=16)
                    c.run(sp, lambda: sp.dma_start(w_t, A["edge_weight"][bass.ds(k * P, P)]
                                                   .rearrange("(p a) -> p a", a=1)), by=16)
                    c.run(sp, lambda: sp.dma_start(pair_t, A["edge_pair"][bass.ds(k * P, P), :]), by=16)
                    c.run(pe, lambda: pe.transpose(pa[:, 0:P], oh_b, ident[:, :]))
                    c.run(ve, lambda: ve.tensor_copy(oh_bT, pa[:, 0:P]))
                    c.run(pe, lambda: pe.matmul(pa[0:NA, 0:P], oh_a, ident[:, :], start=True, stop=True))
                    c.run(ve, lambda: ve.tensor_copy(oh_aT[0:NA, :], pa[0:NA, 0:P]))
                    c.run(pe, lambda: pe.matmul(pa[:, 0:P], oh_bT, oh_bT, start=True, stop=True))
                    c.run(pe, lambda: pe.matmul(pb[:, 0:P], oh_aT[0:NA, :], oh_aT[0:NA, :], start=True, stop=True))
                    c.run(ve, lambda: ve.tensor_tensor(same, before[:, :], pa[:, 0:P], ALU.mult))
                    c.run(ve, lambda: ve.tensor_tensor(same, same, pb[:, 0:P], ALU.mult))
                    c.run(pe, lambda: pe.matmul(pc[:, 0:1], same, ones[:, 0:1], start=True, stop=True))
                    c.run(pe, lambda: pe.matmul(pa[:, 0:NA], oh_bT, where, start=True, stop=True))
                    c.run(ve, lambda: ve.tensor_tensor(same[:, 0:NA], oh_a, pa[:, 0:NA], ALU.mult))
                    c.run(ve, lambda: ve.tensor_reduce(pos, same[:, 0:NA], AX_X, ALU.add))
                    c.run(ve, lambda: ve.tensor_tensor(pos, pos, pc[:, 0:1], ALU.add))
                    c.run(ve, lambda: ve.tensor_copy(pos_i, pos))
                    c.run(ve, lambda: ve.tensor_scalar(pos_d, pos, float(FRONT), None, ALU.add))
                    for j, (rows, at, dst) in enumerate(((s_i, pos_i, src_s), (d_i, pos_d, dst_s),
                                                         (w_t, pos_i, w_s))):
                        po.wait_ge(lap, c.n)
                        settle(po, "pool")
                        po.indirect_dma_start(dst.rearrange("(n a) -> n a", a=1),
                                              bass.IndirectOffsetOnAxis(ap=at, axis=0), rows, None
                                              ).then_inc(scattered[j], 16)
                    po.indirect_dma_start(pair_s, bass.IndirectOffsetOnAxis(ap=pos_i, axis=0), pair_t, None
                                          ).then_inc(scattered[3], 16)
                    for s in scattered:
                        po.wait_ge(s, 16 * k + 16)
                    po.wait_ge(lap, c.n)
                    c.n = c.n + 1
                    po.sem_inc(lap, 1)
                    c.run(pe, lambda: pe.matmul(pb[:, 0:NA], oh_b, oh_a, start=True, stop=True))
                    c.run(ve, lambda: ve.tensor_tensor(where, where, pb[:, 0:NA], ALU.add))

                at = looped(place, 22 + 48 + 15 + 1 + 2, c.n)
                sp.wait_ge(lap, at)

        def tile_tables():
            begin()
            starts = st[1][:, 0:NB + 1]
            starts_t = st[1][:, 0:NB]
            number = st[2][:, 0:NB + 1]
            number_i = st[3][:, 0:NB].bitcast(I32)
            first = st[4][:, 0:NB]
            shift = st[4][:, NB:2 * NB]
            step = st[4][:, 2 * NB:3 * NB]
            kk = st[0][:, 0:TCOL]
            blk = st[0][:, 8:8 + TCOL]
            edge = st[0][:, 16:16 + TCOL]
            edge_i = st[0][:, 24:24 + TCOL].bitcast(I32)
            prev_i = st[0][:, 32:32 + TCOL].bitcast(I32)
            scaled = st[0][:, 40:40 + TCOL]
            go(ve, lambda: ve.tensor_tensor(number[:, 0:NB], starts[:, 1:NB + 1], starts_t, ALU.subtract))
            go(ve, lambda: ve.tensor_scalar(number[:, 0:NB], number[:, 0:NB], float(P - 1), None, ALU.add))
            go(ve, lambda: ve.tensor_copy(number_i, number[:, 0:NB]))
            go(ve, lambda: ve.tensor_scalar(number_i, number_i, 7, None, ALU.logical_shift_right))
            go(ve, lambda: ve.tensor_copy(number[:, 0:NB], number_i))
            go(ve, lambda: ve.tensor_tensor_scan(first, number[:, 0:NB], number[:, 0:NB], 0.0, ALU.add, ALU.bypass))
            go(ve, lambda: ve.tensor_tensor(first, first, number[:, 0:NB], ALU.subtract))
            go(ve, lambda: ve.scalar_tensor_tensor(shift, first, float(-P), starts_t, ALU.mult, ALU.add))
            go(ve, lambda: ve.tensor_copy(step, shift))
            go(ve, lambda: ve.tensor_tensor(step[:, 1:NB], shift[:, 1:NB], shift[:, 0:NB - 1], ALU.subtract))
            for g in range(TCOL):
                go(ve, lambda: ve.tensor_scalar(kk[:, g:g + 1], iota_col[:, :], float(g * P), None, ALU.add))
            cube = BUF[0][:, 0:TCOL * NB * 2 // P + 1, :].rearrange("p b d -> p (b d)")
            le = cube[:, 0:TCOL * NB].rearrange("p (g t) -> p g t", g=TCOL)
            part = cube[:, TCOL * NB:2 * TCOL * NB].rearrange("p (g t) -> p g t", g=TCOL)
            go(ve, lambda: ve.tensor_tensor(le, first.unsqueeze(1).broadcast_to([P, TCOL, NB]),
                                            kk.unsqueeze(2).broadcast_to([P, TCOL, NB]), ALU.is_le))
            go(ve, lambda: ve.tensor_reduce(blk, le, AX_X, ALU.add))
            go(ve, lambda: ve.tensor_scalar(blk, blk, -1.0, None, ALU.add))
            go(ve, lambda: ve.tensor_tensor(part, le, step.unsqueeze(1).broadcast_to([P, TCOL, NB]), ALU.mult))
            go(ve, lambda: ve.tensor_reduce(edge, part, AX_X, ALU.add))
            go(ve, lambda: ve.scalar_tensor_tensor(edge, kk, float(P), edge, ALU.mult, ALU.add))
            go(ve, lambda: ve.tensor_scalar(edge, edge, float(E), None, ALU.min))
            go(ve, lambda: ve.tensor_copy(edge_i, edge))
            go(ve, lambda: ve.tensor_scalar(prev_i, edge, float(FRONT - 1), None, ALU.add))
            go(ve, lambda: ve.tensor_scalar(scaled, blk, float(P), None, ALU.mult))
            with ExitStack() as ps:
                rows = psum(ps, "rows", [1, 2, 1024])
                for n, (col, tab) in enumerate(((blk, BLOCK), (edge, START))):
                    for g in range(TCOL):
                        go(pe, lambda: pe.matmul(rows[0:1, n, g * P:(g + 1) * P], col[:, g:g + 1], ident[:, :],
                                                 start=True, stop=True))
                    go(ve, lambda: ve.tensor_copy(tab[0:1, :], rows[0:1, n, 0:TTAB]))
            W3 = P + 2
            raw = BUF[0][:, :, :].rearrange("p b d -> p (b d)")
            dst_i = raw[:, 0:TCOL * W3].bitcast(I32).rearrange("p (g e) -> p g e", g=TCOL)
            src_i = raw[:, 1024:1024 + TTAB].bitcast(I32).rearrange("p (g e) -> p g e", g=TCOL)
            wt = raw[:, 2048:2048 + TTAB].rearrange("p (g e) -> p g e", g=TCOL)
            two = BUF[1][:, :, :].rearrange("p b d -> p (b d)")
            dst_f = two[:, 0:TCOL * W3].rearrange("p (g e) -> p g e", g=TCOL)
            src_f = two[:, 1024:1024 + TTAB].rearrange("p (g e) -> p g e", g=TCOL)
            local, new = (two[:, 1024 * j:1024 * j + TTAB].rearrange("p (g e) -> p g e", g=TCOL) for j in (2, 3))
            pen_open, pen_close = (two[:, 1024 * j:1024 * j + TTAB // 2].bitcast(BF16).rearrange(
                "p (g e) -> p g e", g=TCOL) for j in (4, 5))
            for g in range(TCOL):
                for tile, tab, at, w in ((dst_i, dst_s, prev_i, W3), (src_i, src_s, edge_i, P), (wt, w_s, edge_i, P)):
                    total = tab.shape[0]
                    view = tab[0:total // w * w].rearrange("(n e) -> n e", e=w)
                    po.wait_ge(chain[0].sem, chain[0].n)
                    po.indirect_dma_start(tile[:, g, :], None, view,
                                          bass.IndirectOffsetOnAxis(ap=at[:, g:g + 1], axis=1)
                                          ).then_inc(S("windows"), 16)
            ve.wait_ge(S("windows"), 3 * TCOL * 16)
            go(ve, lambda: ve.tensor_copy(dst_f, dst_i))
            go(ve, lambda: ve.tensor_copy(src_f, src_i))
            mid = dst_f[:, :, 1:P + 1]
            go(ve, lambda: ve.tensor_tensor(local, mid, scaled.unsqueeze(2).broadcast_to([P, TCOL, P]), ALU.subtract))
            go(ve, lambda: ve.tensor_tensor(new, mid, dst_f[:, :, 0:P], ALU.not_equal))
            go(ve, lambda: ve.tensor_scalar(pen_open, new, -BIG, None, ALU.mult))
            src_spare = raw[:, 3072:3072 + TTAB].rearrange("p (g e) -> p g e", g=TCOL)
            go(ve, lambda: ve.tensor_tensor(src_spare, mid, dst_f[:, :, 2:P + 2], ALU.not_equal))
            go(ve, lambda: ve.tensor_scalar(pen_close, src_spare, -BIG, None, ALU.mult))
            load(open_d.rearrange("(g p e) -> p g e", g=TCOL, p=P), pen_open)
            load(close_d.rearrange("(g p e) -> p g e", g=TCOL, p=P), pen_close)
            with ExitStack() as ps:
                turned = psum(ps, "turned", [P, 1024])
                for rows, tab in ((local, LOCAL), (new, NEWSEG), (wt, WEIGHT), (src_f, SRC)):
                    for g in range(TCOL):
                        go(pe, lambda: pe.transpose(turned[:, g * P:(g + 1) * P], rows[:, g, :], ident[:, :]))
                    go(ve, lambda: ve.tensor_copy(tab[:, :], turned[:, 0:TTAB]))
            end()

        def norm(src, dst, eps=EPS):
            mean, var = st[0][:, 0:NB], st[1][:, 0:NB]
            sq = ACC[:, 0:NB * D].rearrange("p (b d) -> p b d", b=NB)
            go(ve, lambda: ve.tensor_reduce(mean, src, AX_X, ALU.add))
            go(ve, lambda: ve.tensor_scalar(mean, mean, 1.0 / D, None, ALU.mult))
            go(ve, lambda: ve.tensor_tensor(dst, src, tall(mean), ALU.subtract))
            go(ve, lambda: ve.tensor_tensor(sq, dst, dst, ALU.mult))
            go(ve, lambda: ve.tensor_reduce(var, sq, AX_X, ALU.add))
            go(ve, lambda: ve.tensor_scalar(var, var, 1.0 / D, eps, ALU.mult, ALU.add))
            inv_sqrt(var, var)
            go(ve, lambda: ve.tensor_tensor(dst, dst, tall(var), ALU.mult))

        def inv_sqrt(dst, src):
            w = src.shape[1]
            y, t = st[4][:, 0:w], st[4][:, w:2 * w]
            go(ve, lambda: ve.reciprocal(y, src))
            go(ac, lambda: ac.activation(y, y, ACT.Sqrt))
            go(ve, lambda: ve.tensor_tensor(t, y, y, ALU.mult))
            go(ve, lambda: ve.tensor_tensor(t, t, src, ALU.mult))
            go(ve, lambda: ve.tensor_scalar(t, t, -0.5, 1.5, ALU.mult, ALU.add))
            go(ve, lambda: ve.tensor_tensor(dst, y, t, ALU.mult))

        def relu(a):
            go(ve, lambda: ve.tensor_scalar(a, a, 0.0, None, ALU.max))

        def elu(a, tmp):
            go(ve, lambda: ve.tensor_scalar(tmp, a, 0.0, None, ALU.min))
            go(ac, lambda: ac.activation(tmp, tmp, ACT.Exp))
            go(ve, lambda: ve.tensor_scalar(a, a, 0.0, -1.0, ALU.max, ALU.add))
            go(ve, lambda: ve.tensor_tensor(a, a, tmp, ALU.add))

        def dense(src, weight, dst, K=D, M=D, bias_of=None, scale=None):
            load(wmat[0:K, 0:M], weight)
            if bias_of is not None:
                load(bias[:, 0:M], spread(bias_of, M))
            end()
            staged, turned, copied, product, moved = (S(n) for n in ("staged", "turned", "copied", "product", "moved"))
            room = G[:, :, :, :].rearrange("p r t d -> p (r t d)")
            tT = room[:, 0:NCH * P]
            chunk = room[:, NCH * P:NCH * (P + K)].rearrange("p (b k) -> p b k", b=NCH)
            count = NB // NCH
            with ExitStack() as ps:
                tp = psum(ps, "tp", [P, 1024])
                yp = psum(ps, "yp", [P, 8, P])
                for sem in (turned, product):
                    pe.sem_inc(sem, 1)
                ve.sem_inc(moved, 1)

                def stage(c):
                    ve.wait_ge(turned, c + 1)
                    ve.tensor_copy(chunk, src[:, bass.ds(c * NCH, NCH), :]).then_inc(staged, 1)

                def body(c, more):
                    pe.wait_ge(staged, c + 1)
                    settle(pe, "tensor")
                    for j in range(NCH):
                        m = pe.transpose(tp[0:K, j * P:(j + 1) * P], chunk[:, j, :], ident[:, :])
                    m.then_inc(turned, 1)
                    ac.wait_ge(turned, c + 2)
                    ac.wait_ge(product, c + 1)
                    ac.activation(tT[0:K, 0:NCH * P], tp[0:K, 0:NCH * P], ACT.Copy).then_inc(copied, 1)
                    pe.wait_ge(copied, c + 1)
                    pe.wait_ge(moved, c + 1)
                    for j in range(NCH):
                        m = pe.matmul(yp[:, j, 0:M], tT[0:K, j * P:(j + 1) * P], wmat[0:K, 0:M],
                                      start=True, stop=True)
                    m.then_inc(product, 1)
                    if more:
                        stage(c + 1)
                    ve.wait_ge(product, c + 2)
                    to, result = dst[:, bass.ds(c * NCH, NCH), :], yp[:, 0:NCH, 0:M]
                    if bias_of is not None:
                        m = ve.tensor_tensor(to, result, wide(bias[:, 0:M], NCH), ALU.add)
                    elif scale is not None:
                        m = ve.tensor_tensor(to, result, tall(scale[:, bass.ds(c * NCH, NCH)], M), ALU.mult)
                    else:
                        m = ve.tensor_copy(to, result)
                    m.then_inc(moved, 1)

                stage(0)
                with nc.Fori(0, count - 1) as c:
                    body(c, True)
                body(count - 1, False)
                ve.wait_ge(moved, count + 1)
            S.end_stage()
            begin()

        def store_table(tab, src):
            load(tab.rearrange("(b p) d -> p b d", p=P), src)

        def blocks_of(engine, q):
            return nc.values_load_multi_w_load_instructions(
                BLOCK[0:1, bass.ds(q * GT, GT)], engines=(engine,), min_val=0, max_val=NB - 1,
                skip_runtime_bounds_check_because="a tile's block is a count of blocks, less one")[1]

        def ring(W, H):
            whole = G[:, :, :, :].rearrange("p r t d -> p r (t d)")[:, :, 0:GT * (W + H)]
            return whole, whole[:, :, 0:GT * W].rearrange("p r (t w) -> p r t w", t=GT), whole[:, :, GT * W:]

        def gather_pieces(tab, rows, width, read, kept=None):
            def copy_index(q, slot, turn):
                wait(ac, S(f"gathered{slot}"), 16 * GT * turn)
                ac.activation(IDX[:, slot, :], SRC[:, bass.ds(q * GT, GT)], ACT.Copy).then_inc(S("indexed"), 1)

            def gather(q, slot, turn):
                po.wait_ge(S("indexed"), q + 1)
                wait(po, S(read), q - RING + 1)
                if kept:
                    wait(po, S(f"{kept}{slot}"), 16 * turn)
                settle(po, "pool")
                for j in range(GT):
                    po.indirect_dma_start(rows[:, slot, j, 0:width], None, tab,
                                          bass.IndirectOffsetOnAxis(ap=IDX[:, slot, j:j + 1], axis=0)
                                          ).then_inc(S(f"gathered{slot}"), 16)
            return copy_index, gather

        def gathered(eng, slot, turn):
            eng.wait_ge(S(f"gathered{slot}"), 16 * GT * (turn + 1))

        def one_hot(tile, k, j, weighted=False):
            if weighted:
                return ve.tensor_scalar(tile[:, j, :], iota_row[:, :], LOCAL[:, bass.ds(k + j, 1)],
                                        WEIGHT[:, bass.ds(k + j, 1)], ALU.is_equal, ALU.mult)
            return ve.tensor_scalar(tile[:, j, :], iota_row[:, :], LOCAL[:, bass.ds(k + j, 1)], None, ALU.is_equal)

        class Adder:

            def __init__(self, acc, sums, width, ready):
                self.acc, self.sums, self.width, self.ready = acc, sums, width, ready

            def start(self, q, slot):
                ve.wait_ge(S(self.ready), q + 1)
                self.q, self.from_ = q, self.sums[slot % 2]
                self.blocks = blocks_of(DVE, q)

            def tile(self, j):
                wait(ve, S("added"), self.q * GT + j)
                at = self.acc[:, bass.ds(self.blocks[j], 1), :].rearrange("p a d -> p (a d)")
                ve.tensor_tensor(at, at, self.from_[:, j, 0:self.width], ALU.add).then_inc(S("added"), 1)

        def interleave(*lists):
            for n in range(max(map(len, lists))):
                for calls in lists:
                    if n < len(calls):
                        calls[n]()

        def gcn_pass(acc):
            with ExitStack() as ps:
                sums = [psum(ps, f"sums{i}", [P, GT, P]) for i in range(2)]
                copy_index, gather = gather_pieces(table, G, D, "g_free")
                adder = Adder(acc, sums, D, "g_free")

                def products(q, slot, turn):
                    pe.wait_ge(S("hot"), q + 1)
                    gathered(pe, slot, turn)
                    wait(pe, S("added"), (q - 1) * GT)
                    for j in range(GT):
                        m = pe.matmul(sums[slot % 2][:, j, :], OH[:, slot % 2, j, :], G[:, slot, j, 0:D],
                                      start=True, stop=True)
                    m.then_inc(S("g_free"), 1)

                def hots(q, slot, turn):
                    wait(ve, S("g_free"), q - 1)
                    for j in range(GT):
                        m = one_hot(OH[:, slot % 2], q * GT, j, True)
                    m.then_inc(S("hot"), 1)

                def add(q, slot, turn):
                    adder.start(q, slot)
                    for j in range(GT):
                        adder.tile(j)

                pipeline(nc, [(copy_index, 0), (gather, 0), (hots, 0), (products, 0), (add, 1)])
                ve.wait_ge(S("added"), GROUPS * GT)
            S.end_stage()

        def pair_pass(acc):
            rooms = BUF[2][:, :, :].rearrange("p b d -> p (b d)")
            PAIR = rooms[:, 0:8 * GT * P].rearrange("p (r t d) -> p r t d", r=4, t=GT)
            EAT = rooms[:, 8 * GT * P:10 * GT * P].rearrange("p (r t d) -> p r t d", r=2, t=GT)
            V = rooms[:, 10 * GT * P:12 * GT * P].rearrange("p (r t d) -> p r t d", r=2, t=GT)
            unsorted = nc.values_load(FLAG[0:1, 0:1], engines=(SP,), min_val=0, max_val=1,
                                      skip_runtime_bounds_check_because="it is a minimum with 1")
            with ExitStack() as ps:
                turned = [psum(ps, f"turned{i}", [P, GT, P]) for i in range(2)]
                pre = [psum(ps, f"pre{i}", [P, GT, P]) for i in range(2)]
                sums = [psum(ps, f"sums{i}", [P, GT, P]) for i in range(2)]
                copy_index, gather = gather_pieces(table, G, D, "summed")
                adder = Adder(acc, sums, D, "v_free")

                def fetch(q, slot, turn):
                    at = nc.values_load_multi_w_load_instructions(
                        START[0:1, bass.ds(q * GT, GT)], engines=(SP,), min_val=0, max_val=E,
                        skip_runtime_bounds_check_because="a tile's first edge is a minimum with E")[1]
                    wait(sp, S("based"), q - RING + 1)
                    settle(sp, "sync")

                    def rows(pairs):
                        for j in range(GT):
                            sp.dma_start(PAIR[:, slot, j, :], pairs[bass.ds(at[j], P), :]
                                         ).then_inc(S(f"pair{slot}"), 16)

                    with sp.If(unsorted == 1):
                        rows(pair_s)
                    with sp.Else():
                        rows(A["edge_pair"])

                def turn_attr(q, slot, turn):
                    h = slot % 2
                    pe.wait_ge(S(f"pair{slot}"), 16 * GT * (turn + 1))
                    wait(pe, S("attr_copied"), q - 1)
                    for j in range(GT):
                        m = pe.transpose(turned[h][:, j, :], PAIR[:, slot, j, 0:D], ident[:, :])
                    m.then_inc(S("attr_turned"), 1)

                def copy_attr(q, slot, turn):
                    h = slot % 2
                    ac.wait_ge(S("attr_turned"), q + 1)
                    wait(ac, S("pre_done"), q - 1)
                    ac.activation(EAT[:, h], turned[h][:, :, :], ACT.Copy).then_inc(S("attr_copied"), 1)

                def times_w(q, slot, turn):
                    h = slot % 2
                    pe.wait_ge(S("attr_copied"), q + 1)
                    wait(pe, S("summed"), q - 1)
                    for j in range(GT):
                        m = pe.matmul(pre[h][:, j, :], EAT[:, h, j, :], wmat[:, :], start=True, stop=True)
                    m.then_inc(S("pre_done"), 1)

                def sum_up(q, slot, turn):
                    h = slot % 2
                    ve.wait_ge(S("pre_done"), q + 1)
                    gathered(ve, slot, turn)
                    wait(ve, S("v_free"), q - 1)
                    ve.tensor_tensor(V[:, h], pre[h][:, :, :], G[:, slot, :, 0:D], ALU.add).then_inc(S("summed"), 1)

                def gelu(q, slot, turn):
                    ac.wait_ge(S("summed"), q + 1)
                    ac.activation(V[:, slot % 2], V[:, slot % 2], ACT.Gelu).then_inc(S("gelu"), 1)

                def times_base(q, slot, turn):
                    h = slot % 2
                    ve.wait_ge(S("gelu"), q + 1)
                    ve.wait_ge(S(f"pair{slot}"), 16 * GT * (turn + 1))
                    ve.tensor_tensor(V[:, h], V[:, h], PAIR[:, slot, :, D:2 * D], ALU.mult).then_inc(S("based"), 1)

                def hots(q, slot, turn):
                    wait(ve, S("v_free"), q - 1)
                    for j in range(GT):
                        m = one_hot(OH[:, slot % 2], q * GT, j)
                    m.then_inc(S("hot"), 1)

                def products(q, slot, turn):
                    h = slot % 2
                    pe.wait_ge(S("hot"), q + 1)
                    pe.wait_ge(S("based"), q + 1)
                    wait(pe, S("added"), (q - 1) * GT)
                    for j in range(GT):
                        m = pe.matmul(sums[h][:, j, :], OH[:, h, j, :], V[:, h, j, :], start=True, stop=True)
                    m.then_inc(S("v_free"), 1)

                def add(q, slot, turn):
                    adder.start(q, slot)
                    for j in range(GT):
                        adder.tile(j)

                pipeline(nc, [(copy_index, 0), (gather, 0), (fetch, 0), (turn_attr, 1), (copy_attr, 1),
                              (times_w, 2), (times_base, 3), (sum_up, 2), (gelu, 2), (hots, 2), (products, 3),
                              (add, 4)])
                ve.wait_ge(S("added"), GROUPS * GT)
            S.end_stage()

        def gat_logits(tab, XR, H, C):
            W = H * C
            Z = BUF[2][:, 0:2 * GT, 0:W].rearrange("p (r t) d -> p r t d", r=2)
            OHT = BUF[2][:, 2 * GT:4 * GT, :].rearrange("p (r t) d -> p r t d", r=2)
            TH = GT * H
            LROW = BUF[2][0:TH, 4 * GT:4 * GT + 2, :]
            by_group = head_d[0:H * TILES * P].rearrange("(g a e) -> g a e", a=TH, e=P)
            whole, R, LOGIT = ring(W, H)
            att_g = att[:, 0:W].unsqueeze(1).broadcast_to([P, GT, W])
            with ExitStack() as ps:
                turned = [psum(ps, f"turned{i}", [P, GT, P]) for i in range(2)]
                picked = [psum(ps, f"picked{i}", [P, GT, P]) for i in range(2)]
                lrow = [psum(ps, f"lrow{i}", [P, 4 * P]) for i in range(2)]
                copy_index, gather = gather_pieces(tab, R, W, "lrow", "kept")

                def turn_hots(q, slot, turn):
                    pe.wait_ge(S("hot"), q + 1)
                    wait(pe, S("oht"), q - 1)
                    for j in range(GT):
                        m = pe.transpose(turned[slot % 2][:, j, :], OH[:, slot % 2, j, :], ident[:, :])
                    m.then_inc(S("turned"), 1)

                def copy_hots(q, slot, turn):
                    ac.wait_ge(S("turned"), q + 1)
                    wait(ac, S("picked"), q - 1)
                    ac.activation(OHT[:, slot % 2], turned[slot % 2][:, :, :], ACT.Copy).then_inc(S("oht"), 1)

                def pick(q, slot, turn):
                    pe.wait_ge(S("oht"), q + 1)
                    wait(pe, S("z"), q - 1)
                    blocks = blocks_of(PE, q)
                    for j in range(GT):
                        m = pe.matmul(picked[slot % 2][:, j, 0:W], OHT[:, slot % 2, j, :],
                                      XR[:, bass.ds(blocks[j], 1), 0:W].rearrange("p a d -> p (a d)"),
                                      start=True, stop=True)
                    m.then_inc(S("picked"), 1)

                def logit_steps(q, slot, turn):
                    z = Z[:, slot % 2]

                    def add():
                        ve.wait_ge(S("picked"), q + 1)
                        gathered(ve, slot, turn)
                        wait(ve, S("logit"), q - 1)
                        ve.tensor_tensor(z, picked[slot % 2][:, :, 0:W], R[:, slot, :, 0:W], ALU.add
                                         ).then_inc(S("z"), 1)

                    def leaky():
                        ve.wait_ge(S("z"), q + 1)
                        ve.scalar_tensor_tensor(z, z, SLOPE, z, ALU.mult, ALU.max).then_inc(S("leaky"), 1)

                    def weigh():
                        ve.wait_ge(S("leaky"), q + 1)
                        ve.tensor_tensor(z, z, att_g, ALU.mult).then_inc(S("weighed"), 1)

                    def reduce():
                        ve.wait_ge(S("weighed"), q + 1)
                        ve.tensor_reduce(LOGIT[:, slot, :].rearrange("p (t h) -> p t h", h=H), z.rearrange("p t (h c) -> p t h c", h=H), AX_X,
                                         ALU.add).then_inc(S("logit"), 1)
                    return [add, leaky, weigh, reduce]

                waiting = []

                def hots(q, slot, turn):
                    wait(ve, S("turned"), q - 1)

                    def hot(j):
                        m = one_hot(OH[:, slot % 2], q * GT, j)
                        if j == GT - 1:
                            m.then_inc(S("hot"), 1)
                    interleave(waiting.pop() if waiting else [], [lambda j=j: hot(j) for j in range(GT)])

                def logits(q, slot, turn):
                    waiting.append(logit_steps(q, slot, turn))
                    if isinstance(q, int) and q >= GROUPS - 2:
                        interleave(waiting.pop())

                def turn_logits(q, slot, turn):
                    pe.wait_ge(S("logit"), q + 1)
                    wait(pe, S("lcopied"), q - 1)
                    m = pe.matmul(lrow[slot % 2][0:TH, 0:P], LOGIT[:, slot, :], ident[:, :], start=True, stop=True)
                    m.then_inc(S("lrow"), 1)

                def copy_rows(q, slot, turn):
                    ac.wait_ge(S("lrow"), q + 1)
                    wait(ac, S(f"stored{slot % 2}"), 16 * (turn * (RING // 2) + slot // 2))
                    ac.activation(LROW[:, slot % 2, :], lrow[slot % 2][0:TH, 0:P], ACT.Copy).then_inc(S("lcopied"), 1)

                def keep(q, slot, turn):
                    sp.wait_ge(S("logit"), q + 1)
                    settle(sp, "sync")
                    sp.dma_start(kept_d[bass.ds(q, 1), :, 0:GT * (W + H)].rearrange("a p w -> p (a w)"),
                                 whole[:, slot, :]).then_inc(S(f"kept{slot}"), 16)

                def store_rows(q, slot, turn):
                    sp.wait_ge(S("lcopied"), q + 1)
                    settle(sp, "sync")
                    sp.dma_start(by_group[bass.ds(q, 1)].rearrange("g a e -> (g a) e"), LROW[:, slot % 2, :]
                                 ).then_inc(S(f"stored{slot % 2}"), 16)

                pipeline(nc, [(copy_index, 0), (gather, 0), (logits, 2), (hots, 0), (keep, 2), (turn_logits, 2),
                              (turn_hots, 0), (copy_hots, 0), (pick, 0), (copy_rows, 2), (store_rows, 2)])
                for s in range(RING):
                    sp.wait_ge(S(f"kept{s}"), 16 * (GROUPS // RING))
                for s in range(2):
                    sp.wait_ge(S(f"stored{s}"), 16 * (GROUPS // 2))
            S.end_stage()

        def edge_max(H):
            chunks = P // H
            L = TILES * H
            run = ACC[:, 0:L]
            pens = BUF[2][:, :, :].rearrange("p b d -> p (b d)").bitcast(BF16)[:, 0:L]
            ends = st[0]
            row = st[1]
            begin()
            if H == 1:
                in_dram = [head_d[0:P * L].rearrange("(c n) -> c n", c=chunks)]
                on_chip = [run]
            else:
                assert L % P == 0
                rows_of = head_d[0:P * L].rearrange("(c t h e) -> h c t e", c=chunks, h=H, e=P)
                in_dram = [rows_of[h] for h in range(H)]
                on_chip = [run[h * chunks:(h + 1) * chunks].rearrange("p (t e) -> p t e", e=P) for h in range(H)]

            def pen_loads(pen_d):
                return [(pens[h * chunks:(h + 1) * chunks, :], pen_d[0:TILES * P].rearrange("(c n) -> c n", c=chunks))
                        for h in range(H)]

            def direction(flip):
                data, pen = (run[:, ::-1], pens[:, ::-1]) if flip else (run, pens)
                last = run[:, 0:1] if flip else run[:, L - 1:L]
                go(ve, lambda: ve.tensor_tensor_scan(data, pen, data, -BIG, ALU.add, ALU.max))
                go(ve, lambda: ve.tensor_reduce(ends[:, 1:2], pen, AX_X, ALU.min))
                go(ve, lambda: ve.tensor_copy(ends[:, 0:1], last))
                value, penalty = row[0:1, 0:P], row[0:1, P:2 * P]
                state, carry = row[0:1, 2 * P:3 * P], st[2][0:1, 0:P]
                with ExitStack() as ps:
                    lines = psum(ps, "lines", [P, 3 * P])
                    for n in range(2):
                        go(pe, lambda: pe.matmul(lines[0:1, n * P:(n + 1) * P], ends[:, n:n + 1], ident[:, :],
                                                 start=True, stop=True))
                    go(ve, lambda: ve.tensor_copy(row[0:1, 0:2 * P], lines[0:1, 0:2 * P]))
                    start = chunks - 1 if flip else 0
                    first = [r.rearrange("a (h c) -> a h c", h=H)[:, :, start] for r in (penalty, carry)]
                    go(ve, lambda: ve.memset(first[0], -BIG))
                    turn = (lambda r: r[:, ::-1]) if flip else (lambda r: r)
                    go(ve, lambda: ve.tensor_tensor_scan(turn(state), turn(penalty), turn(value), -BIG,
                                                         ALU.add, ALU.max))
                    if flip:
                        go(ve, lambda: ve.tensor_copy(carry[:, 0:P - 1], state[:, 1:P]))
                    else:
                        go(ve, lambda: ve.tensor_copy(carry[:, 1:P], state[:, 0:P - 1]))
                    go(ve, lambda: ve.memset(first[1], -BIG))
                    go(pe, lambda: pe.matmul(lines[:, 2 * P:2 * P + 1], carry, ones[0:1, 0:1], start=True, stop=True))
                    go(ve, lambda: ve.tensor_copy(ends[:, 2:3], lines[:, 2 * P:2 * P + 1]))
                go(ve, lambda: ve.tensor_tensor_scan(data, pen, data, ends[:, 2:3], ALU.add, ALU.max))

            load_all(list(zip(on_chip, in_dram)) + pen_loads(open_d))
            direction(False)
            load_all(pen_loads(close_d))
            direction(True)
            load_all(list(zip(in_dram, on_chip)))
            end()

        def gat_sums(acc, H, C):
            W = H * C
            WA = W + 2 * H + 2
            TH = GT * H
            RHS = BUF[2][:, :, :].rearrange("p b d -> p (b d)")[:, 0:RING * GT * WA].rearrange(
                "p (r t w) -> p r t w", r=RING, t=GT)
            at = -(-RING * GT * WA // P)
            HOT = BUF[2][:, at:at + RING * GT, :].rearrange("p (r t) d -> p r t d", r=RING)
            at += RING * GT
            MX = BUF[2][0:TH, at:at + RING, :]
            DIF = BUF[2][:, at + RING:at + 2 * RING, 0:TH].rearrange("p r (t h) -> p r t h", h=H)
            by_group = head_d[0:H * TILES * P].rearrange("(g a e) -> g a e", a=TH, e=P)
            whole, R, LOGIT = ring(W, H)
            with ExitStack() as ps:
                mcol = [psum(ps, f"mcol{i}", [P, 4 * P]) for i in range(2)]
                sums = [psum(ps, f"asum{i}", [P, GT, 2 * P]) for i in range(2)]
                adder = Adder(acc, sums, WA, "summed")

                def fetch(q, slot, turn):
                    wait(sp, S("rows"), q - RING + 1)
                    settle(sp, "sync")
                    sp.dma_start(whole[:, slot, :], kept_d[bass.ds(q, 1), :, 0:GT * (W + H)]
                                 .rearrange("a p w -> p (a w)")).then_inc(S(f"got{slot}"), 16)
                    wait(sp, S("mcol"), q - RING + 1)
                    settle(sp, "sync")
                    sp.dma_start(MX[:, slot, :], by_group[bass.ds(q, 1)].rearrange("g a e -> (g a) e")).then_inc(S(f"max{slot}"), 16)

                def turn_max(q, slot, turn):
                    pe.wait_ge(S(f"max{slot}"), 16 * (turn + 1))
                    wait(pe, S("mfirst"), q - 1)
                    m = pe.matmul(mcol[slot % 2][:, 0:TH], MX[:, slot, :], ident[0:TH, 0:TH], start=True, stop=True)
                    m.then_inc(S("mcol"), 1)

                def by_head(a):
                    return a.rearrange("p (t h) -> p t h", h=H)

                def hots(q, slot, turn):
                    wait(ac, S("summed"), q - RING + 1)
                    for j in range(GT):
                        ac.activation(HOT[:, slot, j, :], iota_row[:, :], ACT.Abs, scale=-1.0,
                                      bias=LOCAL[:, bass.ds(q * GT + j, 1)]).then_inc(S("gap"), 1)

                def exps(q, slot, turn):
                    ac.wait_ge(S("dif"), q + 1)
                    ac.activation(RHS[:, slot, :, W:W + H], DIF[:, slot], ACT.Exp).then_inc(S("exp"), 1)
                    ac.activation(RHS[:, slot, :, W + 2 * H], NEWSEG[:, bass.ds(q * GT, GT)], ACT.Copy
                                  ).then_inc(S("extra"), 1)
                    ac.activation(RHS[:, slot, :, W + 2 * H + 1], WEIGHT[:, bass.ds(q * GT, GT)], ACT.Copy
                                  ).then_inc(S("extra"), 1)
                    ac.wait_ge(S("gap"), (q + 1) * GT)
                    ac.activation(HOT[:, slot], HOT[:, slot], ACT.Relu, scale=-1.0, bias=1.0
                                  ).then_inc(S("hot"), 1)

                def less_max(q, slot, turn):
                    ve.wait_ge(S("mcol"), q + 1)
                    ve.wait_ge(S(f"got{slot}"), 16 * (turn + 1))
                    wait(ve, S("exp"), q - RING + 1)
                    wait(ve, S("summed"), q - RING + 1)
                    ve.tensor_tensor(DIF[:, slot], by_head(LOGIT[:, slot, :]), by_head(mcol[slot % 2][:, 0:TH]),
                                     ALU.subtract).then_inc(S("dif"), 1)

                def first_max(q, slot, turn):
                    ve.tensor_tensor(RHS[:, slot, :, W + H:W + 2 * H], by_head(mcol[slot % 2][:, 0:TH]),
                                     NEWSEG[:, bass.ds(q * GT, GT)].unsqueeze(2).broadcast_to([P, GT, H]), ALU.mult
                                     ).then_inc(S("mfirst"), 1)

                def rows(q, slot, turn):
                    ve.wait_ge(S("exp"), q + 1)
                    ve.tensor_tensor(RHS[:, slot, :, 0:W].rearrange("p t (h c) -> p t h c", h=H),
                                     R[:, slot, :, 0:W].rearrange("p t (h c) -> p t h c", h=H),
                                     RHS[:, slot, :, W:W + H].unsqueeze(3).broadcast_to([P, GT, H, C]), ALU.mult
                                     ).then_inc(S("rows"), 1)

                def products(q, slot, turn):
                    pe.wait_ge(S("hot"), q + 1)
                    pe.wait_ge(S("rows"), q + 1)
                    pe.wait_ge(S("mfirst"), q + 1)
                    pe.wait_ge(S("extra"), 2 * (q + 1))
                    wait(pe, S("added"), (q - 1) * GT)
                    for j in range(GT):
                        m = pe.matmul(sums[slot % 2][:, j, 0:WA], HOT[:, slot, j, :], RHS[:, slot, j, :],
                                      start=True, stop=True)
                    m.then_inc(S("summed"), 1)

                order = []

                def ve_step(piece):
                    def keep_for_later(q, slot, turn):
                        order.append((piece, q, slot, turn))
                    return keep_for_later

                def add(q, slot, turn):
                    adder.start(q, slot)
                    work = [lambda f=f, a=a: f(*a) for f, *a in order]
                    order.clear()
                    interleave([lambda j=j: adder.tile(j) for j in range(GT)], work)

                def flush(q, slot, turn):
                    for f, *a in order:
                        f(*a)
                    order.clear()

                pipeline(nc, [(fetch, 0), (turn_max, 1), (ve_step(less_max), 1), (ve_step(first_max), 1),
                              (ve_step(rows), 2), (add, 4), (flush, 0), (hots, 1), (exps, 1), (products, 3)])
                ve.wait_ge(S("added"), GROUPS * GT)
            S.end_stage()

        def gat_layer(src, name, H, C, K, tab, XL, XR, dst):
            W = H * C
            WA = W + 2 * H + 2
            dense(src, A[f"L0_gnn_Wr{name}"], XR, K, W, A[f"L0_gnn_br{name}"])
            dense(src, A[f"L0_gnn_Wl{name}"], XL, K, W, A[f"L0_gnn_bl{name}"])
            store_table(tab, XL)
            load(att[:, 0:W], spread(A[f"L0_gnn_att{name}"].rearrange("h c -> (h c)"), W))
            acc = ACC[:, 0:NB * WA].rearrange("p (b w) -> p b w", b=NB)
            end()
            gat_logits(tab, XR, H, C)
            edge_max(H)
            clear(NB * WA)
            gat_sums(acc, H, C)
            begin()
            self_l, m_e, m_all, c_e, c_s = (st[i][:, 0:NB * H].rearrange("p (b h) -> p b h", h=H) for i in range(5))
            Zn = BUF[2][:, :, 0:W]
            go(ve, lambda: ve.tensor_tensor(Zn, XL, XR, ALU.add))
            go(ve, lambda: ve.scalar_tensor_tensor(Zn, Zn, SLOPE, Zn, ALU.mult, ALU.max))
            go(ve, lambda: ve.tensor_tensor(Zn, Zn, wide(att[:, 0:W]), ALU.mult))
            go(ve, lambda: ve.tensor_reduce(self_l, Zn.rearrange("p b (h c) -> p b h c", h=H), AX_X, ALU.add))
            has = acc[:, :, W + 2 * H].unsqueeze(2).broadcast_to([P, NB, H])
            go(ve, lambda: ve.tensor_scalar(m_all, has, -1.0, BIG, ALU.add, ALU.mult))
            go(ve, lambda: ve.tensor_tensor(m_e, acc[:, :, W + H:W + 2 * H], m_all, ALU.add))
            go(ve, lambda: ve.tensor_tensor(m_all, m_e, self_l, ALU.max))
            go(ve, lambda: ve.tensor_tensor(c_e, m_e, m_all, ALU.subtract))
            go(ve, lambda: ve.tensor_tensor(c_s, self_l, m_all, ALU.subtract))
            go(ac, lambda: ac.activation(c_e, c_e, ACT.Exp))
            go(ac, lambda: ac.activation(c_s, c_s, ACT.Exp))
            den = m_e
            go(ve, lambda: ve.tensor_tensor(den, acc[:, :, W:W + H], c_e, ALU.mult))
            go(ve, lambda: ve.tensor_tensor(den, den, c_s, ALU.add))
            go(ve, lambda: ve.reciprocal(den, den))
            go(ve, lambda: ve.tensor_tensor(c_e, c_e, den, ALU.mult))
            go(ve, lambda: ve.tensor_tensor(c_s, c_s, den, ALU.mult))

            def heads(a):
                return a.rearrange("p b (h c) -> p b h c", h=H)

            def each(c):
                return c.unsqueeze(3).broadcast_to([P, NB, H, C])

            go(ve, lambda: ve.tensor_tensor(heads(Zn), heads(acc[:, :, 0:W]), each(c_e), ALU.mult))
            go(ve, lambda: ve.tensor_tensor(heads(dst), heads(XL), each(c_s), ALU.mult))
            go(ve, lambda: ve.tensor_tensor(dst, dst, Zn, ALU.add))
            load(bias[:, 0:W], spread(A[f"L0_gnn_bias{name}"], W))
            go(ve, lambda: ve.tensor_tensor(dst, dst, wide(bias[:, 0:W]), ALU.add))
            elu(dst, Zn)
            return acc[:, :, W + 2 * H + 1]

        def clear(width):
            po.memset(ACC[:, 0:width // 2], 0.0)
            ve.memset(ACC[:, width // 2:width], 0.0)
            S.end_stage()

        def batch_norm_gelu(a, tmp, gamma, beta):
            load(gain[:, :], spread(gamma, D))
            load(bias[:, :], spread(beta, D))
            mean, total = att[:, :], wmat[:, :]

            def column_means(src):
                go(ve, lambda: ve.tensor_tensor(src[:, NB - 1, :], src[:, NB - 1, :], real[:, :], ALU.mult))
                go(ve, lambda: ve.tensor_reduce(total, src.rearrange("p b d -> p d b"), AX_X, ALU.add))
                with ExitStack() as ps:
                    tot = psum(ps, "tot", [P, P])
                    go(pe, lambda: pe.matmul(tot[:, :], ones[:, :], total, start=True, stop=True))
                    go(ve, lambda: ve.tensor_scalar(mean, tot[:, :], 1.0 / N, None, ALU.mult))

            column_means(a)
            go(ve, lambda: ve.tensor_tensor(a, a, wide(mean), ALU.subtract))
            go(ac, lambda: ac.activation(tmp, a, ACT.Square))
            column_means(tmp)
            go(ve, lambda: ve.tensor_scalar(mean, mean, EPS, None, ALU.add))
            inv_sqrt(mean, mean)
            go(ve, lambda: ve.tensor_tensor(mean, mean, gain[:, :], ALU.mult))
            go(ve, lambda: ve.tensor_tensor(a, a, wide(mean), ALU.mult))
            go(ve, lambda: ve.tensor_tensor(a, a, wide(bias[:, :]), ALU.add))
            go(ac, lambda: ac.activation(a, a, ACT.Gelu))

        Xn, B0, B1, B2 = X[:, :, :], BUF[0][:, :, :], BUF[1][:, :, :], BUF[2][:, :, :]
        accn = ACC[:, 0:NB * D].rearrange("p (b d) -> p b d", b=NB)

        def gcn(src, weight, scale, bias_of):
            dense(src, weight, accn, scale=scale)
            store_table(table, accn)
            end()
            gcn_pass(accn)
            begin()
            load(bias[:, :], spread(bias_of, D))
            go(ve, lambda: ve.tensor_tensor(accn, accn, tall(scale), ALU.mult))
            go(ve, lambda: ve.tensor_tensor(accn, accn, wide(bias[:, :]), ALU.add))

        constants()
        sort_edges()
        tile_tables()
        begin()
        load(Xn, A["x"].rearrange("(b p) d -> p b d", p=P))

        norm(Xn, B0)
        relu(B0)
        gat_layer(B0, "1", H1, C1, D, table, B0, B1, B0)
        deg, mask = st[0][:, 0:NB], st[1][:, 0:NB]
        WA = D + 2 * H1 + 2
        wsum = ACC[:, 0:NB * WA].rearrange("p (b w) -> p b w", b=NB)[:, :, WA - 1]
        go(ve, lambda: ve.tensor_scalar(deg, wsum, 1.0, None, ALU.add))
        inv_sqrt(dinv[:, :], deg)
        go(ve, lambda: ve.tensor_scalar(mask, deg, 0.0, None, ALU.is_gt))
        go(ve, lambda: ve.tensor_tensor(deg, deg, mask, ALU.mult))
        go(ve, lambda: ve.scalar_tensor_tensor(deg, mask, -1.0, deg, ALU.mult, ALU.add))
        go(ve, lambda: ve.tensor_scalar(deg, deg, 1.0, None, ALU.add))
        inv_sqrt(deg, deg)
        go(ve, lambda: ve.tensor_tensor(dinv_guarded[:, :], deg, mask, ALU.mult))
        gat_layer(B0, "2", 1, C2, D, table2, B0[:, :, 0:C2], B1[:, :, 0:C2], B0[:, :, 0:C2])
        dense(B0[:, :, 0:C2], A["L0_gnn_Wlin"], B1, C2, D, A["L0_gnn_blin"])
        elu(B1, B2)
        go(ve, lambda: ve.tensor_tensor(Xn, Xn, B1, ALU.add))

        norm(Xn, B0)
        relu(B0)
        gcn(B0, A["L1_gnn_W"], dinv_guarded[:, :], A["L1_gnn_b"])
        go(ve, lambda: ve.tensor_copy(B0, accn))
        norm(B0, B1)
        load(gain[:, :], spread(A["L1_gnn_ln_gamma"], D))
        load(bias[:, :], spread(A["L1_gnn_ln_beta"], D))
        go(ve, lambda: ve.tensor_tensor(B1, B1, wide(gain[:, :]), ALU.mult))
        go(ve, lambda: ve.tensor_tensor(B1, B1, wide(bias[:, :]), ALU.add))
        go(ve, lambda: ve.tensor_tensor(Xn, Xn, B1, ALU.add))

        norm(Xn, B0)
        relu(B0)
        dense(B0, A["L2_gnn_W1"], B1, D, D, A["L2_gnn_b1"])
        store_table(table, B1)
        go(ve, lambda: ve.memset(ACC[:, :], 0.0))
        end()
        pair_pass(accn)
        begin()
        dense(accn, A["L2_gnn_W2"], B0, D, D, A["L2_gnn_b2"])
        batch_norm_gelu(B0, B1, A["L2_gnn_g1"], A["L2_gnn_be1"])
        dense(B0, A["L2_gnn_W3"], B1, D, D, A["L2_gnn_b3"])
        batch_norm_gelu(B1, B0, A["L2_gnn_g2"], A["L2_gnn_be2"])
        go(ve, lambda: ve.tensor_tensor(Xn, Xn, B1, ALU.add))

        norm(Xn, B0)
        relu(B0)
        dense(B0, A["L3_gnn_W_init"], B2)
        for n in "123":
            gcn(B2 if n == "1" else B0, A["L3_gnn_W" + n], dinv[:, :], A["L3_gnn_b" + n])
            go(ve, lambda: ve.tensor_tensor(B0, accn, B2, ALU.add))
            if n != "3":
                relu(B0)
        go(ve, lambda: ve.tensor_tensor(Xn, Xn, B0, ALU.add))
        full = (NB - 1) * P
        load(out[0:full, :].rearrange("(b p) d -> p b d", p=P), X[:, 0:NB - 1, :])
        load(out[full:N, :], X[0:LAST, NB - 1, :])
        end()


NODES = ["x"]
EDGES = {"src": (0, TAIL, 0), "dst": (FRONT, TAIL, NPAD), "edge_weight": (0, TAIL, 0), "edge_pair": (0, P, 0)}
TURNED = ["L2_gnn_W1", "L2_gnn_W2", "L2_gnn_W3"]


def kernel(**inputs):
    import concourse.bacc as bacc
    from concourse.bass_utils import run_bass_kernel_spmd

    nc = bacc.Bacc("TRN2", target_bir_lowering=False, num_devices=1)
    arrays, args = {}, {}
    inputs["edge_pair"] = np.concatenate([inputs.pop("edge_attr_128"), inputs.pop("edge_attr_128_n2")], axis=1)
    for name, value in inputs.items():
        a = np.asarray(value)
        if name in TURNED:
            a = a.T
        if name in NODES:
            a = np.pad(a, ((0, NPAD - N), (0, 0)))
        if name in EDGES:
            front, tail, fill = EDGES[name]
            a = np.pad(a, ((front, tail),) + ((0, 0),) * (a.ndim - 1), constant_values=fill)
        a = np.ascontiguousarray(a)
        arrays["in_" + name] = a
        args[name] = nc.dram_tensor("in_" + name, a.shape, mybir.dt.from_np(a.dtype), kind="ExternalInput").ap()
    out = nc.dram_tensor("out", (N, D), F32, kind="ExternalOutput").ap()
    gnn(nc, args, out)
    return run_bass_kernel_spmd(nc, [arrays], core_ids=[0]).results[0]["out"]
```

```python
from contextlib import ExitStack

import numpy as np

import concourse.bass as bass
from concourse import mybir

ALU = mybir.AluOpType
ACT = mybir.ActivationFunctionType
F32 = mybir.dt.float32
I32 = mybir.dt.int32
BF16 = mybir.dt.bfloat16
AX_X = mybir.AxisListType.X
DVE = mybir.EngineType.DVE
PE = mybir.EngineType.PE
SP = mybir.EngineType.SP

P = 128
N, D, E = 6250, 128, 106250
NB = -(-N // P)
NPAD = NB * P
LAST = N - (NB - 1) * P
FRONT = P
TAIL = 2 * P
GT = 4
RING = 4
SORT_T = -(-E // P)
TILES = -(-((E + NB * (P - 1)) // P) // (GT * RING)) * GT * RING
GROUPS = TILES // GT
TCOL = -(-TILES // P)
TTAB = TCOL * P
BIG = 1e30
EPS = 1e-5
H1, C1, C2 = 8, 16, 64
SLOPE = 0.2
NCH = 7
WMAX = D + 2 * H1 + 2
EP, EC = 125, E // 125


class Sems:

    SOFT = ("gathered", "windows", "scattered")

    def __init__(self, nc, most=32):
        self.nc, self.names = nc, {}
        self.pool = [nc.alloc_semaphore(f"pool{i}") for i in range(most)]
        self.ids = range(self.pool[0].num, self.pool[0].num + most)
        assert [s.num for s in self.pool] == list(self.ids)
        self.free = list(self.pool)

    def __call__(self, name):
        if name not in self.names:
            soft = name.startswith(self.SOFT)
            self.names[name] = self.nc.alloc_semaphore(f"{name}_{self.nc.next_id()}") if soft else self.free.pop(0)
        return self.names[name]

    def end_stage(self):
        self.nc.all_engine_barrier(sems_to_clear=self.ids)
        self.names, self.free = {}, list(self.pool)


class Chain:

    def __init__(self, sem, base=0, settle=None):
        self.sem, self.n, self.settle = sem, base, settle

    def run(self, eng, ins_of, by=1):
        wait(eng, self.sem, self.n)
        if self.settle:
            self.settle(eng)
        ins_of().then_inc(self.sem, by)
        self.n = self.n + by


def wait(eng, sem, value):
    if not (isinstance(value, int) and value <= 0):
        eng.wait_ge(sem, value)


def pipeline(nc, pieces):
    most = max(late for _, late in pieces)
    first = -(-(most + RING) // RING) * RING

    def step(turn, u):
        for piece, late in pieces:
            slot = (u - late) % RING
            own = turn + (u - late - slot) // RING
            q = own * RING + slot
            if isinstance(q, int) and not 0 <= q < GROUPS:
                continue
            piece(q, slot, own)

    for t in range(first):
        step(t // RING, t % RING)
    with nc.Fori(first // RING, GROUPS // RING) as turn:
        for u in range(RING):
            step(turn, u)
    for t in range(GROUPS, GROUPS + most):
        step(t // RING, t % RING)


def gnn(nc, A, out):
    S = Sems(nc)
    ve, ac, pe, po, sp = nc.vector, nc.scalar, nc.tensor, nc.gpsimd, nc.sync
    with ExitStack() as ctx:
        def sb(name, shape, dt=F32):
            return ctx.enter_context(nc.sbuf_tensor(name, shape, dt))

        def dram(name, shape, dt=F32):
            return nc.dram_tensor(name, shape, dt).ap()

        ident = sb("ident", [P, P])
        iota_row = sb("iota_row", [P, P])
        iota_col = sb("iota_col", [P, 1])
        ones = sb("ones", [P, P])
        real = sb("real", [P, P])
        before = sb("before", [P, P])
        X = sb("X", [P, NB, D])
        BUF = [sb(f"BUF{i}", [P, NB, D]) for i in range(3)]
        ACC = sb("ACC", [P, NB * WMAX])
        LOCAL = sb("LOCAL", [P, TTAB])
        NEWSEG = sb("NEWSEG", [P, TTAB])
        WEIGHT = sb("WEIGHT", [P, TTAB])
        SRC = sb("SRC", [P, TTAB], I32)
        BLOCK = sb("BLOCK", [1, TTAB], I32)
        START = sb("START", [1, TTAB], I32)
        FLAG = sb("FLAG", [1, 4], I32)
        G = sb("G", [P, RING, GT, D + H1])
        IDX = sb("IDX", [P, RING, GT], I32)
        OH = sb("OH", [P, 2, GT, P])
        st = [sb(f"st{i}", [P, NB * H1]) for i in range(5)]
        dinv_guarded = sb("dinv_guarded", [P, NB])
        dinv = sb("dinv", [P, NB])
        bias = sb("bias", [P, D])
        gain = sb("gain", [P, D])
        att = sb("att", [P, D])
        wmat = sb("wmat", [P, D])
        wbias = sb("wbias", [P, D])

        src_s = dram("src_sorted", [E + TAIL], I32)
        dst_s = dram("dst_sorted", [FRONT + E + TAIL], I32)
        w_s = dram("w_sorted", [E + TAIL])
        pair_s = dram("pair_sorted", [E + P, 2 * D])
        table = dram("table", [NPAD, D])
        table2 = dram("table2", [NPAD, C2])
        open_d = dram("open_pen", [TTAB * P], BF16)
        close_d = dram("close_pen", [TTAB * P], BF16)
        kept_d = dram("kept", [GROUPS, P, GT * (D + H1)])
        head_d = dram("heads", [H1 * TILES * P])

        named = [0]

        def psum(stack, name, shape):
            named[0] += 1
            return stack.enter_context(nc.psum_tensor(f"{name}_{named[0]}", shape, F32))

        chain = [None]

        def begin():
            chain[0] = Chain(S("chain"))

        def go(eng, f, by=1):
            chain[0].run(eng, f, by=by)

        def load(dst, src):
            go(sp, lambda: sp.dma_start(dst, src), by=16)

        def load_all(pairs):
            sp.wait_ge(chain[0].sem, chain[0].n)
            for dst, src in pairs:
                sp.dma_start(dst, src).then_inc(chain[0].sem, 16)
            chain[0].n += 16 * len(pairs)

        def end():
            sp.wait_ge(chain[0].sem, chain[0].n)
            S.end_stage()

        def spread(row, width):
            return row.rearrange("(a n) -> a n", a=1).broadcast_to([P, width])

        def settle(eng, name):
            eng.sem_inc(S(f"settled_{name}"), 1)

        def wide(a, n=NB):
            return a.unsqueeze(1).broadcast_to([P, n, a.shape[1]])

        def tall(a, width=D):
            return a.unsqueeze(2).broadcast_to([P, a.shape[1], width])

        Xn, B0, B1, B2 = X[:, :, :], BUF[0][:, :, :], BUF[1][:, :, :], BUF[2][:, :, :]

        def constants():
            begin()
            go(po, lambda: po.iota(SRC[:, 0:P], pattern=[[1, P]], base=0, channel_multiplier=0))
            go(ve, lambda: ve.tensor_copy(iota_row[:, :], SRC[:, 0:P]))
            go(po, lambda: po.iota(SRC[:, 0:1], pattern=[[1, 1]], base=0, channel_multiplier=1))
            go(ve, lambda: ve.tensor_copy(iota_col[:, :], SRC[:, 0:1]))
            go(ve, lambda: ve.memset(ones[:, :], 1.0))
            go(ve, lambda: ve.tensor_scalar(ident[:, :], iota_row[:, :], iota_col[:, 0:1], None, ALU.is_equal))
            go(ve, lambda: ve.tensor_scalar(before[:, :], iota_row[:, :], iota_col[:, 0:1], None, ALU.is_gt))
            go(ve, lambda: ve.tensor_scalar(real[:, :], ones[:, :], iota_col[:, 0:1], float(LAST),
                                            ALU.mult, ALU.is_lt))
            end()

        def sort_edges():
            begin()
            cnt = st[0][:, 0:NB + 1]
            starts = st[1][:, 0:NB + 2]
            thr = st[2][:, 0:NB]
            here = BUF[0][:, :, :].rearrange("p b d -> p (b d)")
            after = BUF[1][:, :, :].rearrange("p b d -> p (b d)")
            junk = BUF[2][:, :, :].rearrange("p b d -> p (b d)")
            here_i = here[0:EP, 2 * EC:3 * EC].bitcast(I32)
            after_i = after[0:EP, 2 * EC:3 * EC].bitcast(I32)
            block_i = here[0:EP, 3 * EC:4 * EC].bitcast(I32)
            block = here[0:EP, 4 * EC:5 * EC].bitcast(BF16)[:, 0:EC]
            before_t = here[0:EP, 5 * EC:6 * EC].bitcast(BF16)[:, 0:EC]
            load_all([(here_i, A["dst"][FRONT:FRONT + E].rearrange("(p c) -> p c", p=EP)),
                      (after_i, A["dst"][FRONT + 1:FRONT + 1 + E].rearrange("(p c) -> p c", p=EP))])
            for copy, given in ((src_s, A["src"]), (dst_s, A["dst"]), (w_s, A["edge_weight"])):
                sp.dma_start(copy, given).then_inc(S("edges_copied"), 16)
            sp.dma_start(Xn, A["x"].rearrange("(b p) d -> p b d", p=P)).then_inc(S("edges_copied"), 16)
            go(ve, lambda: ve.tensor_copy(here[0:EP, 0:EC], here_i))
            go(ve, lambda: ve.tensor_copy(after[0:EP, 0:EC], after_i))
            go(ve, lambda: ve.tensor_scalar(block_i, here_i, 7, None, ALU.logical_shift_right))
            go(ve, lambda: ve.tensor_copy(block, block_i))
            go(ve, lambda: ve.memset(cnt, 0.0))
            go(ve, lambda: ve.tensor_copy(thr, iota_row[:, 0:NB]))
            go(ve, lambda: ve.tensor_tensor(junk[0:EP, 0:EC], here[0:EP, 0:EC], after[0:EP, 0:EC], ALU.is_gt))
            go(ve, lambda: ve.tensor_reduce(cnt[0:EP, NB:NB + 1], junk[0:EP, 0:EC], AX_X, ALU.add))
            lap = S("count")
            ve.wait_ge(chain[0].sem, chain[0].n)
            ve.tensor_copy(before_t[:, 0:1], block[:, 0:1]).then_inc(lap, 1)
            with ve.Fori(0, NB) as t:
                ve.wait_ge(lap, t + 1)
                ve.tensor_scalar(before_t, block, thr[0:EP, bass.ds(t, 1)], 0.0,
                                 ALU.is_lt, ALU.add, accum_out=cnt[0:EP, bass.ds(t, 1)]).then_inc(lap, 1)
            pe.wait_ge(lap, NB + 1)
            with ExitStack() as ps:
                tot = psum(ps, "tot", [P, 64])
                go(pe, lambda: pe.matmul(tot[:, 0:NB + 1], ones[0:EP, :], cnt[0:EP, :], start=True, stop=True))
                go(ve, lambda: ve.tensor_copy(starts[:, 0:NB], tot[:, 0:NB]))
                go(ve, lambda: ve.tensor_scalar(junk[:, 0:1], tot[:, NB:NB + 1], 1.0, None, ALU.min))
            go(ve, lambda: ve.memset(starts[:, NB:NB + 1], float(E)))
            go(ve, lambda: ve.tensor_copy(FLAG[0:1, 0:1], junk[0:1, 0:1]))
            sp.wait_ge(S("edges_copied"), 64)
            end()
            unsorted = nc.values_load(FLAG[0:1, 0:1], min_val=0, max_val=1,
                                      skip_runtime_bounds_check_because="it is a minimum with 1")
            with nc.If(unsorted == 1):
                counting_sort()
            nc.all_engine_barrier()

        def counting_sort():
            NA = NB + 1
            where = st[3][:, 0:NA]
            small = st[4]
            oh_b, oh_a = BUF[0][:, 0, :], BUF[0][:, 1, 0:NA]
            oh_bT, oh_aT, same = BUF[0][:, 2, :], BUF[0][:, 3, :], BUF[0][:, 4, :]
            pair_t = BUF[0][:, 5:7, :].rearrange("p a d -> p (a d)")
            d_i, b_i, a_i, s_i, pos_i, pos_d = (BUF[0][:, 7, j:j + 1].bitcast(I32) for j in range(6))
            w_t, b_f, a_f, pos = (BUF[0][:, 7, j:j + 1] for j in range(8, 12))
            lap = S("lap")
            scattered = [S(f"scattered{j}") for j in range(4)]

            def digits(k, c):
                c.run(sp, lambda: sp.dma_start(d_i, A["dst"][bass.ds(k * P + FRONT, P)].rearrange("(p a) -> p a", a=1)),
                      by=16)
                c.run(ve, lambda: ve.tensor_scalar(b_i, d_i, P - 1, None, ALU.bitwise_and))
                c.run(ve, lambda: ve.tensor_scalar(a_i, d_i, 7, None, ALU.logical_shift_right))
                c.run(ve, lambda: ve.tensor_copy(b_f, b_i))
                c.run(ve, lambda: ve.tensor_copy(a_f, a_i))
                c.run(ve, lambda: ve.tensor_scalar(oh_b, iota_row[:, :], b_f, None, ALU.is_equal))
                c.run(ve, lambda: ve.tensor_scalar(oh_a, iota_row[:, 0:NA], a_f, None, ALU.is_equal))

            with ExitStack() as ps:
                pa, pb, pc = (psum(ps, f"ps{j}", [P, 512]) for j in range(3))

                def looped(body, steps, start):
                    with nc.Fori(0, SORT_T) as k:
                        c = Chain(lap, k * steps + start, lambda eng: settle(eng, "sync") if eng is sp else None)
                        body(k, c)
                    return start + SORT_T * steps

                c = Chain(lap)
                c.run(ve, lambda: ve.memset(where, 0.0))
                c.run(sp, lambda: sp.dma_start(pair_s[E:E + P, :], A["edge_pair"][E:E + P, :]), by=16)

                def count(k, c):
                    digits(k, c)
                    c.run(pe, lambda: pe.matmul(pa[:, 0:NA], oh_b, oh_a, start=True, stop=True))
                    c.run(ve, lambda: ve.tensor_tensor(where, where, pa[:, 0:NA], ALU.add))

                at = looped(count, 24, c.n)
                c = Chain(lap, at)
                c.run(pe, lambda: pe.matmul(pa[:, 0:NA], ones[:, :], where, start=True, stop=True))
                c.run(ve, lambda: ve.tensor_copy(small[:, 0:NA], pa[:, 0:NA]))
                c.run(ve, lambda: ve.tensor_tensor_scan(small[:, NA:2 * NA], small[:, 0:NA], small[:, 0:NA], 0.0,
                                                        ALU.add, ALU.bypass))
                c.run(pe, lambda: pe.matmul(pb[:, 0:NA], before[:, :], where, start=True, stop=True))
                c.run(ve, lambda: ve.tensor_tensor(small[:, NA:2 * NA], small[:, NA:2 * NA], small[:, 0:NA],
                                                   ALU.subtract))
                c.run(ve, lambda: ve.tensor_tensor(where, small[:, NA:2 * NA], pb[:, 0:NA], ALU.add))

                def place(k, c):
                    digits(k, c)
                    c.run(sp, lambda: sp.dma_start(s_i, A["src"][bass.ds(k * P, P)].rearrange("(p a) -> p a", a=1)),
                          by=16)
                    c.run(sp, lambda: sp.dma_start(w_t, A["edge_weight"][bass.ds(k * P, P)]
                                                   .rearrange("(p a) -> p a", a=1)), by=16)
                    c.run(sp, lambda: sp.dma_start(pair_t, A["edge_pair"][bass.ds(k * P, P), :]), by=16)
                    c.run(pe, lambda: pe.transpose(pa[:, 0:P], oh_b, ident[:, :]))
                    c.run(ve, lambda: ve.tensor_copy(oh_bT, pa[:, 0:P]))
                    c.run(pe, lambda: pe.matmul(pa[0:NA, 0:P], oh_a, ident[:, :], start=True, stop=True))
                    c.run(ve, lambda: ve.tensor_copy(oh_aT[0:NA, :], pa[0:NA, 0:P]))
                    c.run(pe, lambda: pe.matmul(pa[:, 0:P], oh_bT, oh_bT, start=True, stop=True))
                    c.run(pe, lambda: pe.matmul(pb[:, 0:P], oh_aT[0:NA, :], oh_aT[0:NA, :], start=True, stop=True))
                    c.run(ve, lambda: ve.tensor_tensor(same, before[:, :], pa[:, 0:P], ALU.mult))
                    c.run(ve, lambda: ve.tensor_tensor(same, same, pb[:, 0:P], ALU.mult))
                    c.run(pe, lambda: pe.matmul(pc[:, 0:1], same, ones[:, 0:1], start=True, stop=True))
                    c.run(pe, lambda: pe.matmul(pa[:, 0:NA], oh_bT, where, start=True, stop=True))
                    c.run(ve, lambda: ve.tensor_tensor(same[:, 0:NA], oh_a, pa[:, 0:NA], ALU.mult))
                    c.run(ve, lambda: ve.tensor_reduce(pos, same[:, 0:NA], AX_X, ALU.add))
                    c.run(ve, lambda: ve.tensor_tensor(pos, pos, pc[:, 0:1], ALU.add))
                    c.run(ve, lambda: ve.tensor_copy(pos_i, pos))
                    c.run(ve, lambda: ve.tensor_scalar(pos_d, pos, float(FRONT), None, ALU.add))
                    for j, (rows, at, dst) in enumerate(((s_i, pos_i, src_s), (d_i, pos_d, dst_s),
                                                         (w_t, pos_i, w_s))):
                        po.wait_ge(lap, c.n)
                        settle(po, "pool")
                        po.indirect_dma_start(dst.rearrange("(n a) -> n a", a=1),
                                              bass.IndirectOffsetOnAxis(ap=at, axis=0), rows, None
                                              ).then_inc(scattered[j], 16)
                    po.indirect_dma_start(pair_s, bass.IndirectOffsetOnAxis(ap=pos_i, axis=0), pair_t, None
                                          ).then_inc(scattered[3], 16)
                    for s in scattered:
                        po.wait_ge(s, 16 * k + 16)
                    po.wait_ge(lap, c.n)
                    c.n = c.n + 1
                    po.sem_inc(lap, 1)
                    c.run(pe, lambda: pe.matmul(pb[:, 0:NA], oh_b, oh_a, start=True, stop=True))
                    c.run(ve, lambda: ve.tensor_tensor(where, where, pb[:, 0:NA], ALU.add))

                at = looped(place, 22 + 48 + 15 + 1 + 2, c.n)
                sp.wait_ge(lap, at)

        def tile_tables():
            begin()
            starts = st[1][:, 0:NB + 1]
            starts_t = st[1][:, 0:NB]
            number = st[2][:, 0:NB + 1]
            number_i = st[3][:, 0:NB].bitcast(I32)
            first = st[4][:, 0:NB]
            shift = st[4][:, NB:2 * NB]
            step = st[4][:, 2 * NB:3 * NB]
            kk = st[0][:, 0:TCOL]
            blk = st[0][:, 8:8 + TCOL]
            edge = st[0][:, 16:16 + TCOL]
            edge_i = st[0][:, 24:24 + TCOL].bitcast(I32)
            prev_i = st[0][:, 32:32 + TCOL].bitcast(I32)
            scaled = st[0][:, 40:40 + TCOL]
            go(ve, lambda: ve.tensor_tensor(number[:, 0:NB], starts[:, 1:NB + 1], starts_t, ALU.subtract))
            go(ve, lambda: ve.tensor_scalar(number[:, 0:NB], number[:, 0:NB], float(P - 1), None, ALU.add))
            go(ve, lambda: ve.tensor_copy(number_i, number[:, 0:NB]))
            go(ve, lambda: ve.tensor_scalar(number_i, number_i, 7, None, ALU.logical_shift_right))
            go(ve, lambda: ve.tensor_copy(number[:, 0:NB], number_i))
            go(ve, lambda: ve.tensor_tensor_scan(first, number[:, 0:NB], number[:, 0:NB], 0.0, ALU.add, ALU.bypass))
            go(ve, lambda: ve.tensor_tensor(first, first, number[:, 0:NB], ALU.subtract))
            go(ve, lambda: ve.scalar_tensor_tensor(shift, first, float(-P), starts_t, ALU.mult, ALU.add))
            go(ve, lambda: ve.tensor_copy(step, shift))
            go(ve, lambda: ve.tensor_tensor(step[:, 1:NB], shift[:, 1:NB], shift[:, 0:NB - 1], ALU.subtract))
            for g in range(TCOL):
                go(ve, lambda: ve.tensor_scalar(kk[:, g:g + 1], iota_col[:, :], float(g * P), None, ALU.add))
            cube = BUF[0][:, 0:TCOL * NB * 2 // P + 1, :].rearrange("p b d -> p (b d)")
            le = cube[:, 0:TCOL * NB].rearrange("p (g t) -> p g t", g=TCOL)
            part = cube[:, TCOL * NB:2 * TCOL * NB].rearrange("p (g t) -> p g t", g=TCOL)
            go(ve, lambda: ve.tensor_tensor(le, first.unsqueeze(1).broadcast_to([P, TCOL, NB]),
                                            kk.unsqueeze(2).broadcast_to([P, TCOL, NB]), ALU.is_le))
            go(ve, lambda: ve.tensor_reduce(blk, le, AX_X, ALU.add))
            go(ve, lambda: ve.tensor_scalar(blk, blk, -1.0, None, ALU.add))
            go(ve, lambda: ve.tensor_tensor(part, le, step.unsqueeze(1).broadcast_to([P, TCOL, NB]), ALU.mult))
            go(ve, lambda: ve.tensor_reduce(edge, part, AX_X, ALU.add))
            go(ve, lambda: ve.scalar_tensor_tensor(edge, kk, float(P), edge, ALU.mult, ALU.add))
            go(ve, lambda: ve.tensor_scalar(edge, edge, float(E), None, ALU.min))
            go(ve, lambda: ve.tensor_copy(edge_i, edge))
            go(ve, lambda: ve.tensor_scalar(prev_i, edge, float(FRONT - 1), None, ALU.add))
            go(ve, lambda: ve.tensor_scalar(scaled, blk, float(P), None, ALU.mult))
            with ExitStack() as ps:
                rows = psum(ps, "rows", [1, 2, 1024])
                for n, (col, tab) in enumerate(((blk, BLOCK), (edge, START))):
                    for g in range(TCOL):
                        go(pe, lambda: pe.matmul(rows[0:1, n, g * P:(g + 1) * P], col[:, g:g + 1], ident[:, :],
                                                 start=True, stop=True))
                    go(ve, lambda: ve.tensor_copy(tab[0:1, :], rows[0:1, n, 0:TTAB]))
            W3 = P + 2
            raw = BUF[0][:, :, :].rearrange("p b d -> p (b d)")
            dst_i = raw[:, 0:TCOL * W3].bitcast(I32).rearrange("p (g e) -> p g e", g=TCOL)
            src_i = raw[:, 1024:1024 + TTAB].bitcast(I32).rearrange("p (g e) -> p g e", g=TCOL)
            wt = raw[:, 2048:2048 + TTAB].rearrange("p (g e) -> p g e", g=TCOL)
            two = BUF[1][:, :, :].rearrange("p b d -> p (b d)")
            dst_f = two[:, 0:TCOL * W3].rearrange("p (g e) -> p g e", g=TCOL)
            src_f = two[:, 1024:1024 + TTAB].rearrange("p (g e) -> p g e", g=TCOL)
            local, new = (two[:, 1024 * j:1024 * j + TTAB].rearrange("p (g e) -> p g e", g=TCOL) for j in (2, 3))
            pen_open, pen_close = (two[:, 1024 * j:1024 * j + TTAB // 2].bitcast(BF16).rearrange(
                "p (g e) -> p g e", g=TCOL) for j in (4, 5))
            for g in range(TCOL):
                for tile, tab, at, w in ((dst_i, dst_s, prev_i, W3), (src_i, src_s, edge_i, P), (wt, w_s, edge_i, P)):
                    total = tab.shape[0]
                    view = tab[0:total // w * w].rearrange("(n e) -> n e", e=w)
                    po.wait_ge(chain[0].sem, chain[0].n)
                    po.indirect_dma_start(tile[:, g, :], None, view,
                                          bass.IndirectOffsetOnAxis(ap=at[:, g:g + 1], axis=1)
                                          ).then_inc(S("windows"), 16)
            ve.wait_ge(S("windows"), 3 * TCOL * 16)
            go(ve, lambda: ve.tensor_copy(dst_f, dst_i))
            go(ve, lambda: ve.tensor_copy(src_f, src_i))
            mid = dst_f[:, :, 1:P + 1]
            go(ve, lambda: ve.tensor_tensor(local, mid, scaled.unsqueeze(2).broadcast_to([P, TCOL, P]), ALU.subtract))
            go(ve, lambda: ve.tensor_tensor(new, mid, dst_f[:, :, 0:P], ALU.not_equal))
            go(ve, lambda: ve.tensor_scalar(pen_open, new, -BIG, None, ALU.mult))
            src_spare = raw[:, 3072:3072 + TTAB].rearrange("p (g e) -> p g e", g=TCOL)
            go(ve, lambda: ve.tensor_tensor(src_spare, mid, dst_f[:, :, 2:P + 2], ALU.not_equal))
            go(ve, lambda: ve.tensor_scalar(pen_close, src_spare, -BIG, None, ALU.mult))
            load(open_d.rearrange("(g p e) -> p g e", g=TCOL, p=P), pen_open)
            load(close_d.rearrange("(g p e) -> p g e", g=TCOL, p=P), pen_close)
            with ExitStack() as ps:
                turned = psum(ps, "turned", [P, 1024])
                for rows, tab in ((local, LOCAL), (new, NEWSEG), (wt, WEIGHT), (src_f, SRC)):
                    for g in range(TCOL):
                        go(pe, lambda: pe.transpose(turned[:, g * P:(g + 1) * P], rows[:, g, :], ident[:, :]))
                    go(ve, lambda: ve.tensor_copy(tab[:, :], turned[:, 0:TTAB]))
            end()

        def centre(src, dst, tmp):
            mean, var = st[0][:, 0:NB], st[1][:, 0:NB]
            go(ve, lambda: ve.tensor_reduce(mean, src, AX_X, ALU.add))
            go(ve, lambda: ve.tensor_scalar(mean, mean, 1.0 / D, None, ALU.mult))
            go(ve, lambda: ve.tensor_tensor(dst, src, tall(mean), ALU.subtract))
            go(ac, lambda: ac.activation(tmp, dst, ACT.Square))
            go(ve, lambda: ve.tensor_reduce(var, tmp, AX_X, ALU.add))
            go(ve, lambda: ve.tensor_scalar(var, var, 1.0 / D, EPS, ALU.mult, ALU.add))
            inv_sqrt(var, var)
            return var

        def inv_sqrt(dst, src):
            w = src.shape[1]
            y, t = st[4][:, 0:w], st[4][:, w:2 * w]
            go(ve, lambda: ve.reciprocal(y, src))
            go(ac, lambda: ac.activation(y, y, ACT.Sqrt))
            go(ve, lambda: ve.tensor_tensor(t, y, y, ALU.mult))
            go(ve, lambda: ve.tensor_tensor(t, t, src, ALU.mult))
            go(ve, lambda: ve.tensor_scalar(t, t, -0.5, 1.5, ALU.mult, ALU.add))
            go(ve, lambda: ve.tensor_tensor(dst, y, t, ALU.mult))

        def elu_and_one(a, tmp):
            go(ve, lambda: ve.tensor_scalar(tmp, a, 0.0, None, ALU.min))
            go(ac, lambda: ac.activation(tmp, tmp, ACT.Exp))
            go(ve, lambda: ve.scalar_tensor_tensor(a, a, 0.0, tmp, ALU.max, ALU.add))

        def relu_times(scale):
            return lambda chunk, part, at: [lambda: ve.scalar_tensor_tensor(
                chunk, part, 0.0, tall(scale[:, at]), ALU.max, ALU.mult)]

        def less_one(chunk, part, at):
            return [lambda: ve.tensor_scalar(chunk, part, -1.0, None, ALU.add)]

        def dense(src, weight, dst, K=D, M=D, bias_of=None, scale=None, prepare=None, store=None,
                  turned_by=(ACT.Copy, None, None)):
            sp.dma_start(wmat[0:K, 0:M], weight).then_inc(S("weights"), 16)
            if bias_of is not None:
                sp.dma_start(wbias[:, 0:M], spread(bias_of, M)).then_inc(S("weights"), 16)
            staged, turned, copied, product, moved = (S(n) for n in ("staged", "turned", "copied", "product", "moved"))
            room = G[:, :, :, :].rearrange("p r t d -> p (r t d)")
            chunk = room[:, 0:NCH * K].rearrange("p (b k) -> p b k", b=NCH)
            tT = (room[:, NCH * K:NCH * (K + P)], OH[:, :, :, :].rearrange("p r t d -> p (r t d)")[:, 0:NCH * P])
            count = NB // NCH
            with ExitStack() as ps:
                tp = [psum(ps, f"tp{i}", [P, 1024]) for i in range(2)]
                yp = [psum(ps, f"yp{i}", [P, 8, P]) for i in range(2)]
                for eng in (ve, ac):
                    wait(eng, chain[0].sem, chain[0].n)
                pe.wait_ge(S("weights"), 16 * (1 if bias_of is None else 2))
                if bias_of is not None:
                    ve.wait_ge(S("weights"), 32)

                def stage(c):
                    wait(ve, turned, c)
                    at = bass.ds(c * NCH, NCH)
                    steps = (prepare(chunk, src[:, at, :], at) if prepare
                             else [lambda: ve.tensor_copy(chunk, src[:, at, :])])
                    more = len(steps) - 1
                    for i, f in enumerate(steps):
                        if i:
                            ve.wait_ge(S("prepared"), c * more + i)
                        f().then_inc(staged if i == more else S("prepared"), 1)

                def turn(c, half):
                    pe.wait_ge(staged, c + 1)
                    wait(pe, copied, c - 1)
                    settle(pe, "tensor")
                    for j in range(NCH):
                        m = pe.transpose(tp[half][0:K, j * P:(j + 1) * P], chunk[:, j, :], ident[:, :])
                    m.then_inc(turned, 1)
                    ac.wait_ge(turned, c + 1)
                    wait(ac, product, c - 1)
                    func, by, plus = turned_by
                    given = {} if by is None else {"scale": by, "bias": plus}
                    ac.activation(tT[half][0:K, :], tp[half][0:K, 0:NCH * P], func, **given).then_inc(copied, 1)

                def multiply(c, half):
                    pe.wait_ge(copied, c + 1)
                    wait(pe, moved, c - 1)
                    settle(pe, "tensor")
                    for j in range(NCH):
                        m = pe.matmul(yp[half][:, j, 0:M], tT[half][0:K, j * P:(j + 1) * P], wmat[0:K, 0:M],
                                      start=True, stop=True)
                    m.then_inc(product, 1)

                def move(c, half):
                    ve.wait_ge(product, c + 1)
                    at = bass.ds(c * NCH, NCH)
                    to, result = dst[:, at, :], yp[half][:, 0:NCH, 0:M]
                    if bias_of is not None:
                        m = ve.tensor_tensor(to, result, wide(wbias[:, 0:M], NCH), ALU.add)
                    elif scale is not None:
                        m = ve.tensor_tensor(to, result, tall(scale[:, at], M), ALU.mult)
                    else:
                        m = ve.tensor_copy(to, result)
                    m.then_inc(moved, 1)
                    if store is not None:
                        sp.wait_ge(moved, c + 1)
                        settle(sp, "sync")
                        sp.dma_start(store.rearrange("(b p) d -> p b d", p=P)[:, at, :], to).then_inc(S("stored"), 16)

                assert count % 2 == 1
                stage(0)
                turn(0, 0)
                stage(1)
                turn(1, 1)
                multiply(0, 0)
                stage(2)
                move(0, 0)

                def step(c, half):
                    turn(c, half)
                    multiply(c - 1, 1 - half)
                    stage(c + 1)
                    move(c - 1, 1 - half)

                with nc.Fori(1, (count - 1) // 2) as pair:
                    step(2 * pair, 0)
                    step(2 * pair + 1, 1)
                turn(count - 1, 0)
                multiply(count - 2, 1)
                multiply(count - 1, 0)
                move(count - 2, 1)
                move(count - 1, 0)
                ve.wait_ge(moved, count)
                if store is not None:
                    sp.wait_ge(S("stored"), 16 * count)
            S.end_stage()
            begin()

        def meanwhile(row, width, steps):
            if row is not None:
                sp.dma_start(bias[:, 0:width], spread(row, width)).then_inc(S("row"), 16)
                ve.wait_ge(S("row"), 16)
            for i, f in enumerate(steps):
                wait(ve, S("between"), i)
                f().then_inc(S("between"), 1)

        def blocks_of(engine, q):
            return nc.values_load_multi_w_load_instructions(
                BLOCK[0:1, bass.ds(q * GT, GT)], engines=(engine,), min_val=0, max_val=NB - 1,
                skip_runtime_bounds_check_because="a tile's block is a count of blocks, less one")[1]

        def ring(W, H):
            whole = G[:, :, :, :].rearrange("p r t d -> p r (t d)")[:, :, 0:GT * (W + H)]
            return whole, whole[:, :, 0:GT * W].rearrange("p r (t w) -> p r t w", t=GT), whole[:, :, GT * W:]

        def gather_pieces(tab, rows, width, read, kept=None):
            def copy_index(q, slot, turn):
                wait(ac, S(f"gathered{slot}"), 16 * GT * turn)
                ac.activation(IDX[:, slot, :], SRC[:, bass.ds(q * GT, GT)], ACT.Copy).then_inc(S("indexed"), 1)

            def gather(q, slot, turn):
                po.wait_ge(S("indexed"), q + 1)
                wait(po, S(read), q - RING + 1)
                if kept:
                    wait(po, S(f"{kept}{slot}"), 16 * turn)
                settle(po, "pool")
                for j in range(GT):
                    po.indirect_dma_start(rows[:, slot, j, 0:width], None, tab,
                                          bass.IndirectOffsetOnAxis(ap=IDX[:, slot, j:j + 1], axis=0)
                                          ).then_inc(S(f"gathered{slot}"), 16)
            return copy_index, gather

        def gathered(eng, slot, turn):
            eng.wait_ge(S(f"gathered{slot}"), 16 * GT * (turn + 1))

        def one_hot(tile, k, j, weighted=False):
            if weighted:
                return ve.tensor_scalar(tile[:, j, :], iota_row[:, :], LOCAL[:, bass.ds(k + j, 1)],
                                        WEIGHT[:, bass.ds(k + j, 1)], ALU.is_equal, ALU.mult)
            return ve.tensor_scalar(tile[:, j, :], iota_row[:, :], LOCAL[:, bass.ds(k + j, 1)], None, ALU.is_equal)

        class Adder:

            def __init__(self, acc, sums, width, ready):
                self.acc, self.sums, self.width, self.ready = acc, sums, width, ready

            def start(self, q, slot):
                ve.wait_ge(S(self.ready), q + 1)
                self.q, self.from_ = q, self.sums[slot % 2]
                self.blocks = blocks_of(DVE, q)

            def tile(self, j):
                wait(ve, S("added"), self.q * GT + j)
                at = self.acc[:, bass.ds(self.blocks[j], 1), :].rearrange("p a d -> p (a d)")
                ve.tensor_tensor(at, at, self.from_[:, j, 0:self.width], ALU.add).then_inc(S("added"), 1)

        def interleave(*lists):
            for n in range(max(map(len, lists))):
                for calls in lists:
                    if n < len(calls):
                        calls[n]()

        def gcn_pass(acc, beside):
            meanwhile(*beside)
            with ExitStack() as ps:
                sums = [psum(ps, f"sums{i}", [P, GT, P]) for i in range(2)]
                copy_index, gather = gather_pieces(table, G, D, "g_free")
                adder = Adder(acc, sums, D, "g_free")

                def products(q, slot, turn):
                    pe.wait_ge(S("hot"), q + 1)
                    gathered(pe, slot, turn)
                    wait(pe, S("added"), (q - 1) * GT)
                    for j in range(GT):
                        m = pe.matmul(sums[slot % 2][:, j, :], OH[:, slot % 2, j, :], G[:, slot, j, 0:D],
                                      start=True, stop=True)
                    m.then_inc(S("g_free"), 1)

                def hots(q, slot, turn):
                    wait(ve, S("g_free"), q - 1)
                    for j in range(GT):
                        m = one_hot(OH[:, slot % 2], q * GT, j, True)
                    m.then_inc(S("hot"), 1)

                def add(q, slot, turn):
                    adder.start(q, slot)
                    for j in range(GT):
                        adder.tile(j)

                pipeline(nc, [(copy_index, 0), (gather, 0), (hots, 0), (products, 0), (add, 1)])
                ve.wait_ge(S("added"), GROUPS * GT)
            S.end_stage()

        def pair_pass(acc):
            rooms = BUF[2][:, :, :].rearrange("p b d -> p (b d)")
            PAIR = rooms[:, 0:8 * GT * P].rearrange("p (r t d) -> p r t d", r=4, t=GT)
            EAT = rooms[:, 8 * GT * P:10 * GT * P].rearrange("p (r t d) -> p r t d", r=2, t=GT)
            V = rooms[:, 10 * GT * P:12 * GT * P].rearrange("p (r t d) -> p r t d", r=2, t=GT)
            unsorted = nc.values_load(FLAG[0:1, 0:1], engines=(SP,), min_val=0, max_val=1,
                                      skip_runtime_bounds_check_because="it is a minimum with 1")
            with ExitStack() as ps:
                turned = [psum(ps, f"turned{i}", [P, GT, P]) for i in range(2)]
                pre = [psum(ps, f"pre{i}", [P, GT, P]) for i in range(2)]
                sums = [psum(ps, f"sums{i}", [P, GT, P]) for i in range(2)]
                copy_index, gather = gather_pieces(table, G, D, "summed")
                adder = Adder(acc, sums, D, "v_free")

                def fetch(q, slot, turn):
                    at = nc.values_load_multi_w_load_instructions(
                        START[0:1, bass.ds(q * GT, GT)], engines=(SP,), min_val=0, max_val=E,
                        skip_runtime_bounds_check_because="a tile's first edge is a minimum with E")[1]
                    wait(sp, S("based"), q - RING + 1)
                    settle(sp, "sync")

                    def rows(pairs):
                        for j in range(GT):
                            sp.dma_start(PAIR[:, slot, j, :], pairs[bass.ds(at[j], P), :]
                                         ).then_inc(S(f"pair{slot}"), 16)

                    with sp.If(unsorted == 1):
                        rows(pair_s)
                    with sp.Else():
                        rows(A["edge_pair"])

                def turn_attr(q, slot, turn):
                    h = slot % 2
                    pe.wait_ge(S(f"pair{slot}"), 16 * GT * (turn + 1))
                    wait(pe, S("attr_copied"), q - 1)
                    for j in range(GT):
                        m = pe.transpose(turned[h][:, j, :], PAIR[:, slot, j, 0:D], ident[:, :])
                    m.then_inc(S("attr_turned"), 1)

                def copy_attr(q, slot, turn):
                    h = slot % 2
                    ac.wait_ge(S("attr_turned"), q + 1)
                    wait(ac, S("pre_done"), q - 1)
                    ac.activation(EAT[:, h], turned[h][:, :, :], ACT.Copy).then_inc(S("attr_copied"), 1)

                def times_w(q, slot, turn):
                    h = slot % 2
                    pe.wait_ge(S("attr_copied"), q + 1)
                    wait(pe, S("summed"), q - 1)
                    for j in range(GT):
                        m = pe.matmul(pre[h][:, j, :], EAT[:, h, j, :], wmat[:, :], start=True, stop=True)
                    m.then_inc(S("pre_done"), 1)

                def sum_up(q, slot, turn):
                    h = slot % 2
                    ve.wait_ge(S("pre_done"), q + 1)
                    gathered(ve, slot, turn)
                    wait(ve, S("v_free"), q - 1)
                    ve.tensor_tensor(V[:, h], pre[h][:, :, :], G[:, slot, :, 0:D], ALU.add).then_inc(S("summed"), 1)

                def gelu(q, slot, turn):
                    ac.wait_ge(S("summed"), q + 1)
                    ac.activation(V[:, slot % 2], V[:, slot % 2], ACT.Gelu).then_inc(S("gelu"), 1)

                def times_base(q, slot, turn):
                    h = slot % 2
                    ve.wait_ge(S("gelu"), q + 1)
                    ve.wait_ge(S(f"pair{slot}"), 16 * GT * (turn + 1))
                    ve.tensor_tensor(V[:, h], V[:, h], PAIR[:, slot, :, D:2 * D], ALU.mult).then_inc(S("based"), 1)

                def hots(q, slot, turn):
                    wait(ve, S("v_free"), q - 1)
                    for j in range(GT):
                        m = one_hot(OH[:, slot % 2], q * GT, j)
                    m.then_inc(S("hot"), 1)

                def products(q, slot, turn):
                    h = slot % 2
                    pe.wait_ge(S("hot"), q + 1)
                    pe.wait_ge(S("based"), q + 1)
                    wait(pe, S("added"), (q - 1) * GT)
                    for j in range(GT):
                        m = pe.matmul(sums[h][:, j, :], OH[:, h, j, :], V[:, h, j, :], start=True, stop=True)
                    m.then_inc(S("v_free"), 1)

                def add(q, slot, turn):
                    adder.start(q, slot)
                    for j in range(GT):
                        adder.tile(j)

                pipeline(nc, [(copy_index, 0), (gather, 0), (fetch, 0), (turn_attr, 1), (copy_attr, 1),
                              (times_w, 2), (times_base, 3), (sum_up, 2), (gelu, 2), (hots, 2), (products, 3),
                              (add, 4)])
                ve.wait_ge(S("added"), GROUPS * GT)
            S.end_stage()

        def gat_logits(tab, XL, XR, self_l, H, C):
            W = H * C
            Z = BUF[2][:, 0:2 * GT, 0:W].rearrange("p (r t) d -> p r t d", r=2)
            OHT = BUF[2][:, 2 * GT:4 * GT, :].rearrange("p (r t) d -> p r t d", r=2)
            TH = GT * H
            LROW = BUF[2][0:TH, 4 * GT:4 * GT + 2, :]
            by_group = head_d[0:H * TILES * P].rearrange("(g a e) -> g a e", a=TH, e=P)
            whole, R, LOGIT = ring(W, H)
            att_g = att[:, 0:W].unsqueeze(1).broadcast_to([P, GT, W])
            Zn = ACC[:, 0:NB * W].rearrange("p (b w) -> p b w", b=NB)
            meanwhile(None, 0, [
                lambda: ve.tensor_tensor(Zn, XL, XR, ALU.add),
                lambda: ve.scalar_tensor_tensor(Zn, Zn, SLOPE, Zn, ALU.mult, ALU.max),
                lambda: ve.tensor_tensor(Zn, Zn, wide(att[:, 0:W]), ALU.mult),
                lambda: ve.tensor_reduce(self_l, Zn.rearrange("p b (h c) -> p b h c", h=H), AX_X, ALU.add)])
            with ExitStack() as ps:
                turned = [psum(ps, f"turned{i}", [P, GT, P]) for i in range(2)]
                picked = [psum(ps, f"picked{i}", [P, GT, P]) for i in range(2)]
                lrow = [psum(ps, f"lrow{i}", [P, 4 * P]) for i in range(2)]
                copy_index, gather = gather_pieces(tab, R, W, "lrow", "kept")

                def turn_hots(q, slot, turn):
                    pe.wait_ge(S("hot"), q + 1)
                    wait(pe, S("oht"), q - 1)
                    for j in range(GT):
                        m = pe.transpose(turned[slot % 2][:, j, :], OH[:, slot % 2, j, :], ident[:, :])
                    m.then_inc(S("turned"), 1)

                def copy_hots(q, slot, turn):
                    ac.wait_ge(S("turned"), q + 1)
                    wait(ac, S("picked"), q - 1)
                    ac.activation(OHT[:, slot % 2], turned[slot % 2][:, :, :], ACT.Copy).then_inc(S("oht"), 1)

                def pick(q, slot, turn):
                    pe.wait_ge(S("oht"), q + 1)
                    wait(pe, S("z"), q - 1)
                    blocks = blocks_of(PE, q)
                    for j in range(GT):
                        m = pe.matmul(picked[slot % 2][:, j, 0:W], OHT[:, slot % 2, j, :],
                                      XR[:, bass.ds(blocks[j], 1), 0:W].rearrange("p a d -> p (a d)"),
                                      start=True, stop=True)
                    m.then_inc(S("picked"), 1)

                def logit_steps(q, slot, turn):
                    z = Z[:, slot % 2]

                    def add():
                        ve.wait_ge(S("picked"), q + 1)
                        gathered(ve, slot, turn)
                        wait(ve, S("logit"), q - 1)
                        ve.tensor_tensor(z, picked[slot % 2][:, :, 0:W], R[:, slot, :, 0:W], ALU.add
                                         ).then_inc(S("z"), 1)

                    def leaky():
                        ve.wait_ge(S("z"), q + 1)
                        ve.scalar_tensor_tensor(z, z, SLOPE, z, ALU.mult, ALU.max).then_inc(S("leaky"), 1)

                    def weigh():
                        ve.wait_ge(S("leaky"), q + 1)
                        ve.tensor_tensor(z, z, att_g, ALU.mult).then_inc(S("weighed"), 1)

                    def reduce():
                        ve.wait_ge(S("weighed"), q + 1)
                        ve.tensor_reduce(LOGIT[:, slot, :].rearrange("p (t h) -> p t h", h=H),
                                         z.rearrange("p t (h c) -> p t h c", h=H), AX_X, ALU.add
                                         ).then_inc(S("logit"), 1)
                    return [add, leaky, weigh, reduce]

                waiting = []

                def hots(q, slot, turn):
                    wait(ve, S("turned"), q - 1)

                    def hot(j):
                        m = one_hot(OH[:, slot % 2], q * GT, j)
                        if j == GT - 1:
                            m.then_inc(S("hot"), 1)
                    interleave(waiting.pop() if waiting else [], [lambda j=j: hot(j) for j in range(GT)])

                def logits(q, slot, turn):
                    waiting.append(logit_steps(q, slot, turn))
                    if isinstance(q, int) and q >= GROUPS - 3:
                        interleave(waiting.pop())

                def turn_logits(q, slot, turn):
                    pe.wait_ge(S("logit"), q + 1)
                    wait(pe, S("lcopied"), q - 1)
                    m = pe.matmul(lrow[slot % 2][0:TH, 0:P], LOGIT[:, slot, :], ident[:, :], start=True, stop=True)
                    m.then_inc(S("lrow"), 1)

                def copy_rows(q, slot, turn):
                    ac.wait_ge(S("lrow"), q + 1)
                    wait(ac, S(f"stored{slot % 2}"), 16 * (turn * (RING // 2) + slot // 2))
                    ac.activation(LROW[:, slot % 2, :], lrow[slot % 2][0:TH, 0:P], ACT.Copy).then_inc(S("lcopied"), 1)

                def keep(q, slot, turn):
                    sp.wait_ge(S("logit"), q + 1)
                    settle(sp, "sync")
                    sp.dma_start(kept_d[bass.ds(q, 1), :, 0:GT * (W + H)].rearrange("a p w -> p (a w)"),
                                 whole[:, slot, :]).then_inc(S(f"kept{slot}"), 16)

                def store_rows(q, slot, turn):
                    sp.wait_ge(S("lcopied"), q + 1)
                    settle(sp, "sync")
                    sp.dma_start(by_group[bass.ds(q, 1)].rearrange("g a e -> (g a) e"), LROW[:, slot % 2, :]
                                 ).then_inc(S(f"stored{slot % 2}"), 16)

                pipeline(nc, [(copy_index, 0), (gather, 1), (logits, 3), (hots, 0), (keep, 3), (turn_logits, 3),
                              (turn_hots, 0), (pick, 1), (copy_hots, 0), (copy_rows, 3), (store_rows, 3)])
                for s in range(RING):
                    sp.wait_ge(S(f"kept{s}"), 16 * (GROUPS // RING))
                for s in range(2):
                    sp.wait_ge(S(f"stored{s}"), 16 * (GROUPS // 2))
            S.end_stage()

        def edge_max(H):
            chunks = P // H
            L = TILES * H
            run = ACC[:, 0:L]
            pens = BUF[2][:, :, :].rearrange("p b d -> p (b d)").bitcast(BF16)[:, 0:L]
            assert L % 2 == 0
            unread = G[:, :, :, :].rearrange("p r t d -> p (r t d)").bitcast(BF16)[:, 0:L // 2]
            pens_done = [0]
            ends = st[0]
            row = st[1]
            begin()
            if H == 1:
                in_dram = [head_d[0:P * L].rearrange("(c n) -> c n", c=chunks)]
                on_chip = [run]
            else:
                assert L % P == 0
                rows_of = head_d[0:P * L].rearrange("(c t h e) -> h c t e", c=chunks, h=H, e=P)
                in_dram = [rows_of[h] for h in range(H)]
                on_chip = [run[h * chunks:(h + 1) * chunks].rearrange("p (t e) -> p t e", e=P) for h in range(H)]

            def pen_loads(pen_d):
                return [(pens[h * chunks:(h + 1) * chunks, :], pen_d[0:TILES * P].rearrange("(c n) -> c n", c=chunks))
                        for h in range(H)]

            def direction(flip):
                data, pen = (run[:, ::-1], pens[:, ::-1]) if flip else (run, pens)
                last = run[:, 0:1] if flip else run[:, L - 1:L]
                ac.wait_ge(chain[0].sem, chain[0].n)
                for i in range(2):
                    ac.activation(unread, pens[:, i * L // 2:(i + 1) * L // 2], ACT.Copy,
                                  accum_out=ends[:, 4 + i:5 + i]).then_inc(S("pens"), 1)
                    pens_done[0] += 1
                    ac.wait_ge(S("pens"), pens_done[0])
                go(ve, lambda: ve.tensor_tensor_scan(data, pen, data, -BIG, ALU.add, ALU.max))
                ve.wait_ge(S("pens"), pens_done[0])
                go(ve, lambda: ve.tensor_tensor(ends[:, 1:2], ends[:, 4:5], ends[:, 5:6], ALU.add))
                go(ve, lambda: ve.tensor_copy(ends[:, 0:1], last))
                value, penalty = row[0:1, 0:P], row[0:1, P:2 * P]
                state, carry = row[0:1, 2 * P:3 * P], st[2][0:1, 0:P]
                with ExitStack() as ps:
                    lines = psum(ps, "lines", [P, 3 * P])
                    for n in range(2):
                        go(pe, lambda: pe.matmul(lines[0:1, n * P:(n + 1) * P], ends[:, n:n + 1], ident[:, :],
                                                 start=True, stop=True))
                    go(ve, lambda: ve.tensor_copy(row[0:1, 0:2 * P], lines[0:1, 0:2 * P]))
                    start = chunks - 1 if flip else 0
                    first = [r.rearrange("a (h c) -> a h c", h=H)[:, :, start] for r in (penalty, carry)]
                    go(ve, lambda: ve.memset(first[0], -BIG))
                    turn = (lambda r: r[:, ::-1]) if flip else (lambda r: r)
                    go(ve, lambda: ve.tensor_tensor_scan(turn(state), turn(penalty), turn(value), -BIG,
                                                         ALU.add, ALU.max))
                    if flip:
                        go(ve, lambda: ve.tensor_copy(carry[:, 0:P - 1], state[:, 1:P]))
                    else:
                        go(ve, lambda: ve.tensor_copy(carry[:, 1:P], state[:, 0:P - 1]))
                    go(ve, lambda: ve.memset(first[1], -BIG))
                    go(pe, lambda: pe.matmul(lines[:, 2 * P:2 * P + 1], carry, ones[0:1, 0:1], start=True, stop=True))
                    go(ve, lambda: ve.tensor_copy(ends[:, 2:3], lines[:, 2 * P:2 * P + 1]))
                go(ve, lambda: ve.tensor_tensor_scan(data, pen, data, ends[:, 2:3], ALU.add, ALU.max))

            load_all(list(zip(on_chip, in_dram)) + pen_loads(open_d))
            direction(False)
            load_all(pen_loads(close_d))
            direction(True)
            load_all(list(zip(in_dram, on_chip)))
            end()

        def gat_sums(acc, H, C):
            W = H * C
            WA = W + 2 * H + 2
            TH = GT * H
            RHS = BUF[2][:, :, :].rearrange("p b d -> p (b d)")[:, 0:RING * GT * WA].rearrange(
                "p (r t w) -> p r t w", r=RING, t=GT)
            at = -(-RING * GT * WA // P)
            HOT = BUF[2][:, at:at + RING * GT, :].rearrange("p (r t) d -> p r t d", r=RING)
            at += RING * GT
            MX = BUF[2][0:TH, at:at + RING, :]
            DIF = BUF[2][:, at + RING:at + 2 * RING, 0:TH].rearrange("p r (t h) -> p r t h", h=H)
            by_group = head_d[0:H * TILES * P].rearrange("(g a e) -> g a e", a=TH, e=P)
            whole, R, LOGIT = ring(W, H)
            with ExitStack() as ps:
                mcol = [psum(ps, f"mcol{i}", [P, 4 * P]) for i in range(2)]
                sums = [psum(ps, f"asum{i}", [P, GT, 2 * P]) for i in range(2)]
                adder = Adder(acc, sums, WA, "summed")

                def fetch_max(q, slot, turn):
                    wait(sp, S("mcol"), q - RING + 1)
                    settle(sp, "sync")
                    sp.dma_start(MX[:, slot, :], by_group[bass.ds(q, 1)].rearrange("g a e -> (g a) e")
                                 ).then_inc(S(f"max{slot}"), 16)

                def fetch_rows(q, slot, turn):
                    wait(sp, S("rows"), 2 * (q - RING + 1))
                    settle(sp, "sync")
                    sp.dma_start(whole[:, slot, :], kept_d[bass.ds(q, 1), :, 0:GT * (W + H)]
                                 .rearrange("a p w -> p (a w)")).then_inc(S(f"got{slot}"), 16)

                def turn_max(q, slot, turn):
                    pe.wait_ge(S(f"max{slot}"), 16 * (turn + 1))
                    wait(pe, S("mfirst"), q - 1)
                    m = pe.matmul(mcol[slot % 2][:, 0:TH], MX[:, slot, :], ident[0:TH, 0:TH], start=True, stop=True)
                    m.then_inc(S("mcol"), 1)

                def by_head(a):
                    return a.rearrange("p (t h) -> p t h", h=H)

                def hots(q, slot, turn):
                    wait(ac, S("summed"), q - RING + 1)
                    for j in range(GT):
                        ac.activation(HOT[:, slot, j, :], iota_row[:, :], ACT.Abs, scale=-1.0,
                                      bias=LOCAL[:, bass.ds(q * GT + j, 1)]).then_inc(S("gap"), 1)

                def exps(q, slot, turn):
                    ac.wait_ge(S("dif"), q + 1)
                    ac.activation(RHS[:, slot, :, W:W + H], DIF[:, slot], ACT.Exp).then_inc(S("exp"), 1)
                    ac.wait_ge(S("gap"), (q + 1) * GT)
                    ac.activation(HOT[:, slot], HOT[:, slot], ACT.Relu, scale=-1.0, bias=1.0
                                  ).then_inc(S("hot"), 1)

                def extras(q, slot, turn):
                    wait(po, S("summed"), q - RING + 1)
                    po.tensor_copy(RHS[:, slot, :, W + 2 * H], NEWSEG[:, bass.ds(q * GT, GT)]
                                   ).then_inc(S("extra"), 1)
                    po.tensor_copy(RHS[:, slot, :, W + 2 * H + 1], WEIGHT[:, bass.ds(q * GT, GT)]
                                   ).then_inc(S("extra"), 1)

                def less_max(q, slot, turn):
                    ve.wait_ge(S("mcol"), q + 1)
                    ve.wait_ge(S(f"got{slot}"), 16 * (turn + 1))
                    ve.tensor_tensor(DIF[:, slot], by_head(LOGIT[:, slot, :]), by_head(mcol[slot % 2][:, 0:TH]),
                                     ALU.subtract).then_inc(S("dif"), 1)

                def first_max(q, slot, turn):
                    ve.tensor_tensor(RHS[:, slot, :, W + H:W + 2 * H], by_head(mcol[slot % 2][:, 0:TH]),
                                     NEWSEG[:, bass.ds(q * GT, GT)].unsqueeze(2).broadcast_to([P, GT, H]), ALU.mult
                                     ).then_inc(S("mfirst"), 1)

                def rows(q, slot, part):
                    ve.wait_ge(S("exp"), q + 1)
                    half = slice(part * GT // 2, (part + 1) * GT // 2)
                    ve.tensor_tensor(RHS[:, slot, half, 0:W].rearrange("p t (h c) -> p t h c", h=H),
                                     R[:, slot, half, 0:W].rearrange("p t (h c) -> p t h c", h=H),
                                     RHS[:, slot, half, W:W + H].unsqueeze(3).broadcast_to([P, GT // 2, H, C]),
                                     ALU.mult).then_inc(S("rows"), 1)

                def first_rows(q, slot, turn):
                    rows(q, slot, 0)

                def last_rows(q, slot, turn):
                    rows(q, slot, 1)

                def products(q, slot, turn):
                    pe.wait_ge(S("hot"), q + 1)
                    pe.wait_ge(S("rows"), 2 * (q + 1))
                    pe.wait_ge(S("mfirst"), q + 1)
                    pe.wait_ge(S("extra"), 2 * (q + 1))
                    wait(pe, S("added"), (q - 1) * GT)
                    for j in range(GT):
                        m = pe.matmul(sums[slot % 2][:, j, 0:WA], HOT[:, slot, j, :], RHS[:, slot, j, :],
                                      start=True, stop=True)
                    m.then_inc(S("summed"), 1)

                order = []

                def ve_step(piece):
                    def keep_for_later(q, slot, turn):
                        order.append((piece, q, slot, turn))
                    return keep_for_later

                def add(q, slot, turn):
                    adder.start(q, slot)
                    work = [lambda f=f, a=a: f(*a) for f, *a in order]
                    order.clear()
                    interleave([lambda j=j: adder.tile(j) for j in range(GT)], work)

                def flush(q, slot, turn):
                    for f, *a in order:
                        f(*a)
                    order.clear()

                pipeline(nc, [(fetch_max, 0), (fetch_rows, 1), (extras, 2), (turn_max, 2), (ve_step(less_max), 2),
                              (ve_step(first_rows), 3), (ve_step(first_max), 2), (ve_step(last_rows), 3), (add, 5),
                              (flush, 0), (hots, 2), (exps, 2), (products, 4)])
                ve.wait_ge(S("added"), GROUPS * GT)
            S.end_stage()

        def gat_layer(src, prepare, name, H, C, K, tab, XL, XR, dst):
            W = H * C
            WA = W + 2 * H + 2
            acc = ACC[:, 0:NB * WA].rearrange("p (b w) -> p b w", b=NB)
            self_l, m_e, m_all, c_e, c_s = (st[i][:, 0:NB * H].rearrange("p (b h) -> p b h", h=H)
                                            for i in (3, 0, 1, 2, 4))
            dense(src, A[f"L0_gnn_Wr{name}"], XR, K, W, A[f"L0_gnn_br{name}"], prepare=prepare)
            load(att[:, 0:W], spread(A[f"L0_gnn_att{name}"].rearrange("h c -> (h c)"), W))
            dense(src, A[f"L0_gnn_Wl{name}"], XL, K, W, A[f"L0_gnn_bl{name}"], prepare=prepare, store=tab)
            end()
            gat_logits(tab, XL, XR, self_l, H, C)
            edge_max(H)
            clear(NB * WA)
            gat_sums(acc, H, C)
            begin()
            Zn = BUF[2][:, :, 0:W]
            load(bias[:, 0:W], spread(A[f"L0_gnn_bias{name}"], W))
            has = acc[:, :, W + 2 * H].unsqueeze(2).broadcast_to([P, NB, H])
            go(ve, lambda: ve.tensor_scalar(m_all, has, -1.0, BIG, ALU.add, ALU.mult))
            go(ve, lambda: ve.tensor_tensor(m_e, acc[:, :, W + H:W + 2 * H], m_all, ALU.add))
            go(ve, lambda: ve.tensor_tensor(m_all, m_e, self_l, ALU.max))
            go(ve, lambda: ve.tensor_tensor(c_e, m_e, m_all, ALU.subtract))
            go(ve, lambda: ve.tensor_tensor(c_s, self_l, m_all, ALU.subtract))
            go(ac, lambda: ac.activation(c_e, c_e, ACT.Exp))
            go(ac, lambda: ac.activation(c_s, c_s, ACT.Exp))
            den = m_e
            go(ve, lambda: ve.tensor_tensor(den, acc[:, :, W:W + H], c_e, ALU.mult))
            go(ve, lambda: ve.tensor_tensor(den, den, c_s, ALU.add))
            go(ve, lambda: ve.reciprocal(den, den))
            go(ve, lambda: ve.tensor_tensor(c_e, c_e, den, ALU.mult))
            go(ve, lambda: ve.tensor_tensor(c_s, c_s, den, ALU.mult))

            def heads(a):
                return a.rearrange("p b (h c) -> p b h c", h=H)

            def each(c):
                return c.unsqueeze(3).broadcast_to([P, NB, H, C])

            go(ve, lambda: ve.tensor_tensor(heads(Zn), heads(acc[:, :, 0:W]), each(c_e), ALU.mult))
            go(ve, lambda: ve.tensor_tensor(heads(dst), heads(XL), each(c_s), ALU.mult))
            go(ve, lambda: ve.tensor_tensor(dst, dst, Zn, ALU.add))
            go(ve, lambda: ve.tensor_tensor(dst, dst, wide(bias[:, 0:W]), ALU.add))
            elu_and_one(dst, Zn)
            return acc[:, :, W + 2 * H + 1]

        def clear(width):
            po.memset(ACC[:, 0:width // 2], 0.0)
            ve.memset(ACC[:, width // 2:width], 0.0)
            S.end_stage()

        def batch_norm(a, tmp, gamma, beta):
            columns = (gain[:, 0:1], bias[:, 0:1])
            load_all([(columns[0], gamma.rearrange("(p a) -> p a", a=1)),
                      (columns[1], beta.rearrange("(p a) -> p a", a=1))])
            mean, total = att[:, :], OH[:, 0, 0, :]
            var = st[0][:, 0:1]

            def column_sums(src):
                go(ve, lambda: ve.tensor_tensor(src[:, NB - 1, :], src[:, NB - 1, :], real[:, :], ALU.mult))
                go(ve, lambda: ve.tensor_reduce(total, src.rearrange("p b d -> p d b"), AX_X, ALU.add))

            with ExitStack() as ps:
                tot = psum(ps, "tot", [P, 4 * P])
                column_sums(a)
                go(pe, lambda: pe.matmul(tot[:, 0:P], ones[:, :], total, start=True, stop=True))
                go(ve, lambda: ve.tensor_scalar(mean, tot[:, 0:P], 1.0 / N, None, ALU.mult))
                go(ve, lambda: ve.tensor_tensor(a, a, wide(mean), ALU.subtract))
                go(ac, lambda: ac.activation(tmp, a, ACT.Square))
                column_sums(tmp)
                go(pe, lambda: pe.matmul(tot[:, P:P + 1], total, ones[:, 0:1], start=True, stop=True))
                go(ve, lambda: ve.tensor_scalar(var, tot[:, P:P + 1], 1.0 / N, EPS, ALU.mult, ALU.add))
                inv_sqrt(var, var)
                go(ve, lambda: ve.tensor_tensor(columns[0], columns[0], var, ALU.mult))
            return columns

        def rows_of(columns):
            rows = []
            with ExitStack() as ps:
                tot = psum(ps, "rows", [P, 4 * P])
                for i, (column, row) in enumerate(zip(columns, (OH[:, 0, 2, :], OH[:, 0, 3, :]))):
                    spare = OH[:, 0, i, :]
                    go(ve, lambda: ve.tensor_scalar(spare, ident[:, :], column, None, ALU.mult))
                    go(pe, lambda: pe.matmul(tot[:, i * P:(i + 1) * P], ones[:, :], spare, start=True, stop=True))
                    go(ve, lambda: ve.tensor_copy(row, tot[:, i * P:(i + 1) * P]))
                    rows.append(row)
            return rows

        accn = ACC[:, 0:NB * D].rearrange("p (b d) -> p b d", b=NB)

        def gcn(src, weight, scale, prepare, beside):
            dense(src, weight, accn, scale=scale, prepare=prepare, store=table)
            end()
            gcn_pass(accn, beside)
            begin()

        constants()
        sort_edges()
        tile_tables()
        begin()
        rstd = centre(Xn, B0, B1)
        gat_layer(B0, relu_times(rstd), "1", H1, C1, D, table, B0, B1, B0)
        deg, mask = st[0][:, 0:NB], st[1][:, 0:NB]
        WA = D + 2 * H1 + 2
        wsum = ACC[:, 0:NB * WA].rearrange("p (b w) -> p b w", b=NB)[:, :, WA - 1]
        go(ve, lambda: ve.tensor_scalar(deg, wsum, 1.0, None, ALU.add))
        inv_sqrt(dinv[:, :], deg)
        go(ve, lambda: ve.tensor_scalar(mask, deg, 0.0, None, ALU.is_gt))
        go(ve, lambda: ve.tensor_tensor(deg, deg, mask, ALU.mult))
        go(ve, lambda: ve.scalar_tensor_tensor(deg, mask, -1.0, deg, ALU.mult, ALU.add))
        go(ve, lambda: ve.tensor_scalar(deg, deg, 1.0, None, ALU.add))
        inv_sqrt(deg, deg)
        go(ve, lambda: ve.tensor_tensor(dinv_guarded[:, :], deg, mask, ALU.mult))
        gat_layer(B0, less_one, "2", 1, C2, D, table2, B0[:, :, 0:C2], B1[:, :, 0:C2], B0[:, :, 0:C2])
        dense(B0[:, :, 0:C2], A["L0_gnn_Wlin"], B1, C2, D, A["L0_gnn_blin"], prepare=less_one)
        elu_and_one(B1, B2)
        go(ve, lambda: ve.scalar_tensor_tensor(Xn, B1, -1.0, Xn, ALU.add, ALU.add))

        rstd = centre(Xn, B0, B1)
        gcn(B0, A["L1_gnn_W"], dinv_guarded[:, :], relu_times(rstd),
            (A["L1_gnn_ln_beta"], D, [lambda: ve.tensor_tensor(Xn, Xn, wide(bias[:, :]), ALU.add)]))
        load_all([(gain[:, :], spread(A["L1_gnn_ln_gamma"], D)), (bias[:, :], spread(A["L1_gnn_b"], D))])
        go(ve, lambda: ve.tensor_tensor(accn, accn, tall(dinv_guarded[:, :]), ALU.mult))
        go(ve, lambda: ve.tensor_tensor(accn, accn, wide(bias[:, :]), ALU.add))
        rstd = centre(accn, B0, B1)
        go(ve, lambda: ve.tensor_tensor(B0, B0, tall(rstd), ALU.mult))
        go(ve, lambda: ve.tensor_tensor(B0, B0, wide(gain[:, :]), ALU.mult))
        go(ve, lambda: ve.tensor_tensor(Xn, Xn, B0, ALU.add))

        po.wait_ge(chain[0].sem, chain[0].n)
        po.memset(accn, 0.0)
        rstd = centre(Xn, B0, B1)
        dense(B0, A["L2_gnn_W1"], B1, D, D, A["L2_gnn_b1"], prepare=relu_times(rstd), store=table)
        end()
        pair_pass(accn)
        begin()
        dense(accn, A["L2_gnn_W2"], B0, D, D, A["L2_gnn_b2"])
        gain_c, beta_c = batch_norm(B0, B1, A["L2_gnn_g1"], A["L2_gnn_be1"])
        dense(B0, A["L2_gnn_W3"], B1, D, D, A["L2_gnn_b3"], turned_by=(ACT.Gelu, gain_c, beta_c))
        gain_r, beta_r = rows_of(batch_norm(B1, B0, A["L2_gnn_g2"], A["L2_gnn_be2"]))
        go(ve, lambda: ve.tensor_tensor(B1, B1, wide(gain_r), ALU.mult))
        go(ve, lambda: ve.tensor_tensor(B1, B1, wide(beta_r), ALU.add))
        go(ac, lambda: ac.activation(B1, B1, ACT.Gelu))
        go(ve, lambda: ve.tensor_tensor(Xn, Xn, B1, ALU.add))

        rstd = centre(Xn, B0, B1)
        dense(B0, A["L3_gnn_W_init"], B2, prepare=relu_times(rstd))

        def finish(out, part, at):
            return [lambda: ve.tensor_tensor(out, part, tall(dinv[:, at]), ALU.mult),
                    lambda: ve.tensor_tensor(out, out, B1[:, at, :], ALU.add)]

        def finish_relu(out, part, at):
            return finish(out, part, at) + [lambda: ve.tensor_scalar(out, out, 0.0, None, ALU.max)]

        for n in "123":
            beside = [lambda: ve.tensor_tensor(B1, B2, wide(bias[:, :]), ALU.add)]
            if n == "3":
                beside.append(lambda: ve.tensor_tensor(B1, B1, Xn, ALU.add))
            gcn(B2 if n == "1" else accn, A["L3_gnn_W" + n], dinv[:, :], None if n == "1" else finish_relu,
                (A["L3_gnn_b" + n], D, beside))
        for f in finish(Xn, accn, slice(0, NB)):
            go(ve, f)
        full = (NB - 1) * P
        load(out[0:full, :].rearrange("(b p) d -> p b d", p=P), X[:, 0:NB - 1, :])
        load(out[full:N, :], X[0:LAST, NB - 1, :])
        end()


NODES = ["x"]
EDGES = {"src": (0, TAIL, 0), "dst": (FRONT, TAIL, NPAD), "edge_weight": (0, TAIL, 0), "edge_pair": (0, P, 0)}
TURNED = ["L2_gnn_W1", "L2_gnn_W2", "L2_gnn_W3"]


def kernel(**inputs):
    import concourse.bacc as bacc
    from concourse.bass_utils import run_bass_kernel_spmd

    nc = bacc.Bacc("TRN2", target_bir_lowering=False, num_devices=1)
    arrays, args = {}, {}
    inputs["edge_pair"] = np.concatenate([inputs.pop("edge_attr_128"), inputs.pop("edge_attr_128_n2")], axis=1)
    for name, value in inputs.items():
        a = np.asarray(value)
        if name in TURNED:
            a = a.T
        if name in NODES:
            a = np.pad(a, ((0, NPAD - N), (0, 0)))
        if name in EDGES:
            front, tail, fill = EDGES[name]
            a = np.pad(a, ((front, tail),) + ((0, 0),) * (a.ndim - 1), constant_values=fill)
        a = np.ascontiguousarray(a)
        arrays["in_" + name] = a
        args[name] = nc.dram_tensor("in_" + name, a.shape, mybir.dt.from_np(a.dtype), kind="ExternalInput").ap()
    out = nc.dram_tensor("out", (N, D), F32, kind="ExternalOutput").ap()
    gnn(nc, args, out)
    return run_bass_kernel_spmd(nc, [arrays], core_ids=[0]).results[0]["out"]
```
